# Optimizing a Trainium2 kernel written in Bass

```python
import numpy as np
import jax
import jax.numpy as jnp

def _softmax(x, axis=-1):
    return jax.nn.softmax(x, axis=axis)

def _gelu(x):
    return jax.nn.gelu(x, approximate=True)

def _silu(x):
    return jax.nn.silu(x)

def _sigmoid(x):
    return jax.nn.sigmoid(x)

def _layernorm(x, axis=-1, eps=1e-05):
    m = jnp.mean(x, axis=axis, keepdims=True)
    v = jnp.var(x, axis=axis, keepdims=True)
    return (x - m) / jnp.sqrt(v + eps)

def _scatter_add(tgt, idx, src, axis=0):
    return tgt.at[idx].add(src)

def _segment_sum(src, seg, n):
    return jax.ops.segment_sum(src, seg, n)
kernel_name = 'mk_sandwich_d2_jaxref_r8_3dce39'

def setup_inputs(seed: int=0):
    np.random.seed(seed)
    _w = jnp.asarray

    def _L0_attn_setup():
        import jax, jax.numpy as jnp
        import numpy as np
        HEADS = 32
        key = jax.random.key(seed)
        ks = jax.random.split(key, 5)
        H = 512
        B, S = (2, 256)
        w_scale = 1.0 / np.sqrt(H)
        return {'x': jax.random.normal(ks[0], (B, S, H), dtype=jnp.float32), 'attn_qkvw': jax.random.normal(ks[1], (H, 3 * H), dtype=jnp.float32) * w_scale, 'attn_qkvb': jax.random.normal(ks[2], (3 * H,), dtype=jnp.float32) * 0.02, 'attn_ow': jax.random.normal(ks[3], (H, H), dtype=jnp.float32) * w_scale, 'attn_ob': jax.random.normal(ks[4], (H,), dtype=jnp.float32) * 0.02}
    _L0_attn_in = _L0_attn_setup()

    def _L0_ffn_setup():
        import jax, jax.numpy as jnp
        import numpy as np

        def ternary_quantize(w):
            thresh = 0.7 * jnp.mean(jnp.abs(w), axis=-1, keepdims=True)
            q = jnp.where(w > thresh, 1.0, jnp.where(w < -thresh, -1.0, 0.0)).astype(w.dtype)
            return w + jax.lax.stop_gradient(q - w)
        key = jax.random.key(seed)
        k1, k2, k3 = jax.random.split(key, 3)
        B, S, D_in, D_out = (4, 256, 512, 512)
        x = jax.random.normal(k1, (B, S, D_in), dtype=jnp.float32)
        bound = float(np.sqrt(6.0 / D_in))
        weight = jax.random.uniform(k2, (D_out, D_in), dtype=jnp.float32, minval=-bound, maxval=bound)
        bias = jnp.zeros((D_out,), dtype=jnp.float32)
        return {'x': x, 'weight': weight, 'bias': bias}
    _L0_ffn_in = _L0_ffn_setup()

    def _L1_attn_setup():
        import jax, jax.numpy as jnp
        import numpy as np
        B, T, H, S, F, G = (2, 256, 512, 128, 1248, 6)
        GRAD_ORDER_MIN = 4
        THD = 2.5
        key = jax.random.key(seed)
        ks = jax.random.split(key, 9)
        sc = 0.02
        hidden_states = jax.random.normal(ks[0], (B, T, H), jnp.float32)
        up_w = jax.random.normal(ks[1], (S, H), jnp.float32) * sc
        gate_w = jax.random.normal(ks[2], (S, H), jnp.float32) / np.sqrt(H)
        local_point = jax.random.normal(ks[3], (S,), jnp.float32)
        local_approx_output = jax.random.normal(ks[4], (H, S), jnp.float32) * sc
        fuse_weight = jax.random.normal(ks[5], (H, S, G), jnp.float32) * sc
        discount_factor = jnp.asarray(np.cumsum(np.log(np.arange(1, G + 1, dtype=np.float64))), jnp.float32)
        ffn_gate_w = jax.random.normal(ks[6], (F, H), jnp.float32) * sc
        ffn_up_w = jax.random.normal(ks[7], (F, H), jnp.float32) * sc
        ffn_down_w = jax.random.normal(ks[8], (H, F), jnp.float32) * sc
        return {'hidden_states': hidden_states, 'up_w': up_w, 'gate_w': gate_w, 'local_point': local_point, 'local_approx_output': local_approx_output, 'fuse_weight': fuse_weight, 'discount_factor': discount_factor, 'ffn_gate_w': ffn_gate_w, 'ffn_up_w': ffn_up_w, 'ffn_down_w': ffn_down_w}
    _L1_attn_in = _L1_attn_setup()

    def _L1_ffn_setup():
        import jax, jax.numpy as jnp
        import numpy as np
        LORA_SCALE = 16.0 / jnp.sqrt(16.0)
        TOP_K = 2
        key = jax.random.key(seed)
        k1, k2, k3, k4 = jax.random.split(key, 4)
        B_, S, D, O, E, R = (4, 256, 512, 512, 4, 16)
        x = jax.random.normal(k1, (B_, S, D), dtype=jnp.float32)
        router_w = jax.random.normal(k2, (E, D), dtype=jnp.float32) * 0.02
        A = jax.random.normal(k3, (E, R, D), dtype=jnp.float32) * 0.02
        B = jax.random.normal(k4, (O,), dtype=jnp.float32)
        B = jax.random.normal(k4, (E, O, R), dtype=jnp.float32) * 0.02
        return {'x': x, 'router_w': router_w, 'A': A, 'B': B}
    _L1_ffn_in = _L1_ffn_setup()
    _d = {'L0_attn_x': _L0_attn_in['x'], 'L0_attn_attn_qkvw': _L0_attn_in['attn_qkvw'], 'L0_attn_attn_qkvb': _L0_attn_in['attn_qkvb'], 'L0_attn_attn_ow': _L0_attn_in['attn_ow'], 'L0_attn_attn_ob': _L0_attn_in['attn_ob'], 'L0_ffn_weight': _L0_ffn_in['weight'], 'L0_ffn_bias': _L0_ffn_in['bias'], 'L1_attn_up_w': _L1_attn_in['up_w'], 'L1_attn_gate_w': _L1_attn_in['gate_w'], 'L1_attn_local_point': _L1_attn_in['local_point'], 'L1_attn_local_approx_output': _L1_attn_in['local_approx_output'], 'L1_attn_fuse_weight': _L1_attn_in['fuse_weight'], 'L1_attn_discount_factor': _L1_attn_in['discount_factor'], 'L1_attn_ffn_gate_w': _L1_attn_in['ffn_gate_w'], 'L1_attn_ffn_up_w': _L1_attn_in['ffn_up_w'], 'L1_attn_ffn_down_w': _L1_attn_in['ffn_down_w'], 'L1_ffn_router_w': _L1_ffn_in['router_w'], 'L1_ffn_A': _L1_ffn_in['A'], 'L1_ffn_B': _L1_ffn_in['B']}
    _x0 = _d['L0_attn_x']
    _d['L0_attn_x'] = jax.random.normal(jax.random.fold_in(jax.random.key(seed), 1), (2, 1024, 512), dtype=_x0.dtype)
    del _x0
    return _d

def reference(L0_attn_x, L0_attn_attn_qkvw, L0_attn_attn_qkvb, L0_attn_attn_ow, L0_attn_attn_ob, L0_ffn_weight, L0_ffn_bias, L1_attn_up_w, L1_attn_gate_w, L1_attn_local_point, L1_attn_local_approx_output, L1_attn_fuse_weight, L1_attn_discount_factor, L1_attn_ffn_gate_w, L1_attn_ffn_up_w, L1_attn_ffn_down_w, L1_ffn_router_w, L1_ffn_A, L1_ffn_B):

    def _L0_attn_ref(x, attn_qkvw, attn_qkvb, attn_ow, attn_ob):
        import jax, jax.numpy as jnp
        import numpy as np
        HEADS = 32
        B, S, H = x.shape
        hd = H // HEADS
        scale = 1.0 / np.sqrt(hd)
        qkv = x @ attn_qkvw + attn_qkvb
        qkv = qkv.reshape(B, S, 3, HEADS, hd)
        q = jnp.transpose(qkv[:, :, 0], (0, 2, 1, 3))
        k = jnp.transpose(qkv[:, :, 1], (0, 2, 1, 3))
        v = jnp.transpose(qkv[:, :, 2], (0, 2, 1, 3))
        scores = jnp.einsum('bhqd,bhkd->bhqk', q, k) * scale
        probs = jax.nn.softmax(scores, axis=-1)
        ctx = jnp.einsum('bhqk,bhkd->bhqd', probs, v)
        ctx = jnp.transpose(ctx, (0, 2, 1, 3)).reshape(B, S, H)
        return ctx @ attn_ow + attn_ob

    def _L0_ffn_ref(x, weight, bias):
        import jax, jax.numpy as jnp
        import numpy as np

        def ternary_quantize(w):
            thresh = 0.7 * jnp.mean(jnp.abs(w), axis=-1, keepdims=True)
            q = jnp.where(w > thresh, 1.0, jnp.where(w < -thresh, -1.0, 0.0)).astype(w.dtype)
            return w + jax.lax.stop_gradient(q - w)
        q_weight = ternary_quantize(weight)
        return jnp.einsum('bsd,od->bso', x, q_weight) + bias

    def _L1_attn_ref(hidden_states, up_w, gate_w, local_point, local_approx_output, fuse_weight, discount_factor, ffn_gate_w, ffn_up_w, ffn_down_w):
        import jax, jax.numpy as jnp
        import numpy as np
        B, T, H, S, F, G = (2, 256, 512, 128, 1248, 6)
        GRAD_ORDER_MIN = 4
        THD = 2.5
        approx_up = hidden_states @ up_w.T
        gate_pre = hidden_states @ gate_w.T
        delta = gate_pre - local_point
        neg_factor = jnp.where(delta > 0, 1.0, -1.0).astype(hidden_states.dtype)
        delta_abs = jnp.abs(delta)
        log_delta = jnp.log(delta_abs)
        keep = (delta_abs <= THD).astype(hidden_states.dtype)
        approx_out = approx_up @ local_approx_output.T
        for idx in range(G):
            m = idx + 1
            dterm = jnp.exp(log_delta * m - discount_factor[idx])
            if m % 2 == 1:
                dterm = dterm * neg_factor
            tmp = dterm * approx_up
            if m > GRAD_ORDER_MIN:
                tmp = tmp * keep
            approx_out = approx_out + tmp @ fuse_weight[:, :, idx].T
        ffn_out = jax.nn.silu(hidden_states @ ffn_gate_w.T) * (hidden_states @ ffn_up_w.T) @ ffn_down_w.T
        return approx_out + ffn_out

    def _L1_ffn_ref(x, router_w, A, B):
        import jax, jax.numpy as jnp
        import numpy as np
        LORA_SCALE = 16.0 / jnp.sqrt(16.0)
        TOP_K = 2
        D = x.shape[-1]
        flat = x.reshape(-1, D)
        logits = flat @ router_w.T
        topk_vals, topk_idx = jax.lax.top_k(logits, TOP_K)
        sparse = jnp.full_like(logits, -jnp.inf)
        rows = jnp.arange(logits.shape[0])[:, None]
        sparse = sparse.at[rows, topk_idx].set(topk_vals)
        gates = jax.nn.softmax(sparse, axis=-1)
        mid = jnp.einsum('tf,erf->ter', flat, A)
        all_deltas = jnp.einsum('ter,eor->teo', mid, B) * LORA_SCALE
        delta = jnp.einsum('te,teo->to', gates, all_deltas)
        return delta.reshape(*x.shape[:-1], -1)
    x = L0_attn_x
    x = x + _layernorm(_L0_attn_ref(_layernorm(x, axis=-1), L0_attn_attn_qkvw, L0_attn_attn_qkvb, L0_attn_attn_ow, L0_attn_attn_ob), axis=-1)
    x = x + _layernorm(_L0_ffn_ref(_layernorm(x, axis=-1), L0_ffn_weight, L0_ffn_bias), axis=-1)
    x = x + _layernorm(_L1_attn_ref(_layernorm(x, axis=-1), L1_attn_up_w, L1_attn_gate_w, L1_attn_local_point, L1_attn_local_approx_output, L1_attn_fuse_weight, L1_attn_discount_factor, L1_attn_ffn_gate_w, L1_attn_ffn_up_w, L1_attn_ffn_down_w), axis=-1)
    x = x + _layernorm(_L1_ffn_ref(_layernorm(x, axis=-1), L1_ffn_router_w, L1_ffn_A, L1_ffn_B), axis=-1)
    return x

_drawn_inputs = setup_inputs


def setup_inputs(seed=0):
    import zlib

    import numpy as np

    out = dict(_drawn_inputs(seed))
    spreads = {'L0_ffn_bias': (0.0, 0.447)}
    factors = {}
    for name, (base, spread) in spreads.items():
        noise = np.random.default_rng([zlib.crc32(name.encode()), seed]).standard_normal(out[name].shape)
        drawn = base * np.exp(spread * noise) if base else spread * noise
        out[name] = jnp.asarray(drawn.astype(out[name].dtype))
    for name, factor in factors.items():
        out[name] = (out[name] * factor).astype(out[name].dtype)
    return out
```

```python
from contextlib import ExitStack

import concourse.bass as bass
from concourse import mybir

F32 = mybir.dt.float32
F16 = mybir.dt.float16
BF16 = mybir.dt.bfloat16
I32 = mybir.dt.int32
ACT = mybir.ActivationFunctionType
ALU = mybir.AluOpType
AX_X = mybir.AxisListType.X
RMAX = bass.bass_isa.ReduceOp.max

P = 128
BATCH, SEQ, H = 2, 1024, 512
TOKENS = BATCH * SEQ
KC = H // P
HEADS = 32
HD = H // HEADS
SOFTMAX_SCALE = float(HD) ** -0.5
EPS = 1e-5
CHUNK = 512
TPC = CHUNK // P
CHUNKS = TOKENS // CHUNK

Z_BITS = 10
Z_SCALE = float(2 ** Z_BITS)
W_BITS = 14
EXP_MASK = 0x7F800000
SCALE_FROM_EXP = float((254 + W_BITS) << 23)
INV_FROM_EXP = -float((W_BITS + Z_BITS) << 23)
TINY = 1e-30

GH = 4
GROUPS_B = HEADS // GH
GROUPS = BATCH * GROUPS_B
KT = SEQ // P
HALF = SEQ // 2
Q_ROWS = (0, 1, 2, 0, 1, 0)
K_ROWS = (0, 0, 0, 1, 1, 2)
STACK = 6 * HD
MAX_ROW = STACK
ROWS = STACK + 2
SLOTS = 3
MAX_MM = GH * KT * 2
MAX_BY = 26
EXPS = 2 * KT * 2
PAIRS = EXPS // 2
PROBS = 8
PAIR_LAG = 5
SHARED_ROWS = ()
STORE_RING = 4
RING = 3
FOLDS = 9


def pair_at(u):
    for p in range(-2, PAIRS):
        first_of_half = p % KT == 0
        if 2 * p + PAIR_LAG + first_of_half == u:
            return (p < 0, p % PAIRS)
    return None


def ring_plan(prologue=False, first=False, last=False):
    plan, n = [], 0

    def use(u, what, which):
        nonlocal n
        plan.append((u, what, which, n % RING, n // RING))
        n += 1

    if prologue:
        for w in range(MAX_MM):
            use(0, "scores", w)
        use(1, "max", 0)
        return plan
    for u in range(EXPS):
        if not last:
            for w in range(MAX_MM * min(u, MAX_BY) // MAX_BY, MAX_MM * min(u + 1, MAX_BY) // MAX_BY):
                use(u, "scores", w)
            if u == MAX_BY + 2:
                use(u, "max", 0)
        if u == PAIR_LAG + 2 and not first:
            use(u, "ctx", 1)
        if u == PAIR_LAG + 2 + 2 * KT:
            use(u, "ctx", 0)
    return plan


def uses(plan, bank):
    return sum(b == bank for _, _, _, b, _ in plan)


def find(plan, what, which):
    return next((b, k) for _, a, w, b, k in plan if (a, w) == (what, which))


def attention_block(nc, x, w_qkv, b_qk, b_v, ident_dram, ctx_dram):
    qk_dram = nc.dram_tensor("qk_parts", [2, 3, TOKENS // SEQ * H, SEQ], BF16, kind="Internal").ap()
    qk_groups = qk_dram.rearrange("w s (g r) t -> w s g r t", r=GH * HD)

    with ExitStack() as ctx:
        def sb(name, shape, dt):
            return ctx.enter_context(nc.sbuf_tensor(name, shape, dt))

        def psum(name, shape, dt=F32):
            return ctx.enter_context(nc.psum_tensor(name, shape, dt))

        def sem(name):
            return ctx.enter_context(nc.semaphore(name))

        arena = sb("arena", [P, PROBS * 2 * HALF], F32)
        xin = arena[:, 0:2 * TPC * H].rearrange("p (c j f) -> p c j f", c=2, j=TPC)
        z_both = arena[:, 2 * TPC * H:4 * TPC * H].bitcast(F16).rearrange("p (w c k t) -> p w c k t", w=2, c=2, k=KC)
        z_hi, z_lo = z_both[:, 0], z_both[:, 1]
        probs = arena[:].rearrange("p (r t) -> p r t", r=PROBS)
        w_hi = sb("w_hi", [P, KC, 3 * H], F16)
        w_lo = sb("w_lo", [P, KC, 3 * H], F16)
        bqk = sb("bqk", [P, 2 * KC], F32)
        bv = sb("bv", [P, H], F32)
        ident = sb("ident", [P, P], F32)
        amax = sb("amax", [P, 4], F32)
        wscale = sb("wscale", [P, 2], F32)
        stats = sb("stats", [P, 2, TPC, 6], F32)
        mv = sb("mv", [P, 2, TPC, 2], F32)
        rstd = sb("rstd", [P, 2, TPC], F32)
        neg_half = sb("neg_half", [P, TPC], F32)
        y = sb("y", [P, STORE_RING, CHUNK], F32)
        parts = sb("parts", [P, STORE_RING, 3, CHUNK], BF16)
        v_all = sb("v_all", [P, TOKENS // P, H], F32)
        stack = sb("stack", [P, SLOTS, 2, GH * SEQ], BF16)
        w_stage = stack[:].rearrange("p s w t -> p (s w t)")[:, 0:2 * KC * 3 * H].bitcast(F32)
        v_stage = sb("v_stage", [P, SLOTS, KT, GH, 32], F32)
        shared = sb("shared", [P, 2, SEQ], F32)
        max_part = sb("max_part", [P, MAX_MM], F32)
        maxes = sb("maxes", [P, GH * KT], F32)
        max_rows = sb("max_rows", [GH * KT, 2, P], BF16)
        ctx_t = sb("ctx_t", [P, HALF], F32)
        rsum = sb("rsum", [P, 2, 4 * GH], F32)
        ctx_n = sb("ctx_n", [P, 2, 4, GH * HD], F32)

        ps_s = [psum(f"ps_s{i}", [P, 2 * HALF]) for i in range(2)]
        ps_c = psum("ps_c", [P, HALF])
        ps_r = [psum(f"ps_r{i}", [P, 512]) for i in range(RING)]
        ps_tr = ps_r[0:2]
        ps_vp = [ps_c, ps_r[2]]
        ps_qk = [ps_s[i][:, 512 * e:512 * (e + 1)] for i in range(2) for e in range(2)]

        consts_in = sem("consts_in")
        w_in = sem("w_in")
        x_in = [sem(f"x_in{c}") for c in range(2)]
        neg_half_set = sem("neg_half_set")
        amax_set = sem("amax_set")
        amax_all = sem("amax_all")
        exp_set = sem("exp_set")
        wscale_set = sem("wscale_set")
        w_hi_set = sem("w_hi_set")
        w_lo_set = sem("w_lo_set")
        stats_set = sem("stats_set")
        mv_set = sem("mv_set")
        var_eps = sem("var_eps")
        rstd_set = sem("rstd_set")
        z_set = sem("z_set")
        tr_done = sem("tr_done")
        z_hi_set = sem("z_hi_set")
        tr_free = sem("tr_free")
        v_done = sem("v_done")
        v_free = sem("v_free")
        qk_done = sem("qk_done")
        qk_free = sem("qk_free")
        part_step = sem("part_step")
        parts_set = sem("parts_set")
        stored = [sem(f"stored{s}") for s in range(STORE_RING)]
        stage_const = sem("stage_const")
        loaded = [sem(f"loaded{i}") for i in range(SLOTS)]
        v_staged = sem("v_staged")
        ring_done = [sem(f"ring_done{b}") for b in range(RING)]
        ring_free = [sem(f"ring_free{b}") for b in range(RING)]
        folded = sem("folded")
        shared_free = sem("shared_free")
        mx_set = sem("mx_set")
        mx_step = sem("mx_step")
        mx_in = sem("mx_in")
        st_done = sem("st_done")
        exp_done = sem("exp_done")
        pv_done = sem("pv_done")
        pv_free = sem("pv_free")
        rsum_set = sem("rsum_set")
        ctx_out = [sem(f"ctx_out{h}") for h in range(2)]
        block = ctx.enter_context(nc.Block())

        prologue, plan0 = ring_plan(prologue=True), ring_plan(first=True)
        plan_n, plan_z = ring_plan(), ring_plan(last=True)

        def plan_of(g):
            return plan_n if not isinstance(g, int) else plan0 if g == 0 else plan_z if g == GROUPS - 1 else plan_n

        def used(g, bank):
            if isinstance(g, int) and g == 0:
                return uses(prologue, bank)
            return uses(prologue, bank) + uses(plan0, bank) + uses(plan_n, bank) * (g - 1)

        def after(g, what, which):
            bank, k = find(plan_of(g), what, which)
            return bank, used(g, bank) + k + 1

        def steps(engine, step):
            step(0, 0, first=True)
            with engine.Fori(0, (GROUPS - 4) // SLOTS) as i:
                step(3 * i + 1, 1)
                step(3 * i + 2, 2)
                step(3 * i + 3, 0)
            step(GROUPS - 3, 1)
            step(GROUPS - 2, 2)
            step(GROUPS - 1, 0, last=True)

        @block.sync
        def _(sp):
            for n in range(2):
                sp.dma_start(xin[:, n], x[n * CHUNK:(n + 1) * CHUNK, :].rearrange("(j p) f -> p j f", p=P)).then_inc(x_in[n], 16)
            sp.dma_start(ident[:], ident_dram).then_inc(consts_in, 16)
            sp.dma_start(bqk[:], b_qk).then_inc(consts_in, 16)
            sp.dma_start(bv[:], b_v.to_broadcast([P, H])).then_inc(consts_in, 16)

            def store_parts(n, c):
                for f in range(8):
                    sp.wait_ge(parts_set, 8 * n + f + 1)
                    row = (n - c) * (H // 2) + (f % 4) * P
                    dst = qk_dram[f // 4, :, bass.ds(row, P), c * CHUNK:(c + 1) * CHUNK]
                    sp.dma_start(dst.rearrange("s r t -> r s t"), parts[:, f % STORE_RING]).then_inc(stored[f % STORE_RING], 16)

            def load_x(n):
                sp.wait_ge(tr_done, TPC * (n - 1))
                sp.dma_start(xin[:, n % 2], x[n * CHUNK:(n + 1) * CHUNK, :].rearrange("(j p) f -> p j f", p=P)
                             ).then_inc(x_in[n % 2], 16)

            load_x(2)
            store_parts(0, 0)
            load_x(3)
            for n in range(1, CHUNKS):
                store_parts(n, n % 2)
            for s in range(STORE_RING):
                sp.wait_ge(stored[s], 16 + 16 * 8 * CHUNKS // STORE_RING)

            def load(g, slot):
                for which, rows in ((0, Q_ROWS), (1, K_ROWS)):
                    for r, part in enumerate(rows):
                        sp.dma_start(stack[r * HD:(r + 1) * HD, slot, which, :].rearrange("d (j t) -> d j t", j=GH),
                                     qk_groups[which, part, g, :, :].rearrange("(j d) t -> d j t", j=GH)
                                     ).then_inc(loaded[slot], 16)

            def max_rows_in(bank, count, slot):
                sp.wait_ge(ring_free[bank], count + 1)
                for s in range(2):
                    sp.dma_start(stack[MAX_ROW + s:MAX_ROW + s + 1, slot, 0, :], max_rows[:, s, :]).then_inc(mx_in, 16)

            def ctx_store(g, half, bank, count):
                sp.wait_ge(ring_free[bank], count + 1)
                row = (g // GROUPS_B) * SEQ + half * HALF
                dst = ctx_dram[bass.ds(row, HALF), bass.ds((g % GROUPS_B) * GH * HD, GH * HD)]
                sp.dma_start(dst.rearrange("(t p) f -> p t f", p=P), ctx_n[:, half]).then_inc(ctx_out[half], 16)

            def step(g, slot, first=False, last=False):
                if not isinstance(g, int) or g + 2 < GROUPS:
                    if not first:
                        sp.wait_ge(st_done, EXPS * g)
                    load(g + 2, (slot + 2) % SLOTS)
                if not first:
                    ctx_store(g - 1, 1, *after(g, "ctx", 1))
                ctx_store(g, 0, *after(g, "ctx", 0))
                if not last:
                    max_rows_in(*after(g, "max", 0), (slot + 1) % SLOTS)

            sp.wait_ge(w_lo_set, KC)
            sp.wait_ge(stage_const, 2)
            load(0, 0)
            load(1, 1)
            bank, k = find(prologue, "max", 0)
            max_rows_in(bank, k + 1, 0)
            steps(sp, step)
            bank = 0
            ctx_store(GROUPS - 1, 1, bank, used(GROUPS - 1, bank) + uses(plan_z, bank) + 1)
            for half in range(2):
                sp.wait_ge(ctx_out[half], 16 + 16 * GROUPS)

        @block.gpsimd
        def _(pool):
            nc.gpsimd.memset(neg_half[:], -0.5).then_inc(neg_half_set, 1)
            nc.gpsimd.memset(v_stage[:], 0.0).then_inc(stage_const, 1)
            def rstds(n, c):
                pool.wait_ge(mv_set, TPC * (n + 1))
                nc.gpsimd.tensor_scalar(rstd[:, c, :], mv[:, c, :, 1], EPS, None, ALU.add).then_inc(var_eps, 1)
                pool.wait_ge(var_eps, n + 1)
                pool.wait_ge(neg_half_set, 1)
                nc.gpsimd.tensor_tensor(rstd[:, c, :], rstd[:, c, :], neg_half[:], ALU.pow).then_inc(rstd_set, 1)

            rstds(0, 0)
            rstds(1, 1)
            pool.wait_ge(amax_set, 1)
            nc.gpsimd.partition_all_reduce(amax[:, 1:2], amax[:, 0:1], P, RMAX).then_inc(amax_all, 1)
            rstds(2, 0)
            rstds(3, 1)

            v_view = v_all[:].rearrange("p (b t) (g j d) -> p b t g j d", b=BATCH, g=GROUPS_B, j=GH)

            def stage_v(g, par):
                nc.gpsimd.tensor_copy(v_stage[:, par, :, :, 0:HD],
                                      v_view[:, g // GROUPS_B, :, g % GROUPS_B, :, :]).then_inc(v_staged, 1)

            def fold(bank, count, gg, t, r):
                pool.wait_ge(ring_free[bank], count + 1)
                width, buf = SEQ // 2, shared[:, t % 2]
                for m in range(FOLDS):
                    done = (gg * len(SHARED_ROWS) + t) * FOLDS + m
                    if m:
                        pool.wait_ge(folded, done)
                    to = buf[:, 0:width] if m < FOLDS - 1 else max_part[:, 2 * r:2 * r + 2]
                    ins = nc.gpsimd.tensor_tensor(to, buf[:, 0:width], buf[:, width:2 * width], ALU.max)
                    ins.then_inc(folded, 1)
                    width //= 2
                pool.wait_ge(folded, done + 1)
                pool.sem_inc(shared_free, 1)

            def folds(plan, before, gg):
                for t, r in enumerate(SHARED_ROWS):
                    bank, k = find(plan, "scores", 2 * r + 1)
                    fold(bank, before(bank) + k + 1, gg, t, r)

            def step(g, slot, first=False, last=False):
                if last:
                    return
                if not first:
                    pool.wait_ge(pv_done, 4 + PAIRS * (g - 1))
                stage_v(g + 1, (slot + 1) % SLOTS)
                folds(plan_of(g), lambda bank: used(g, bank), g + 1)

            pool.wait_ge(v_free, 2 + TOKENS // P)
            pool.wait_ge(stage_const, 2)
            stage_v(0, 0)
            folds(prologue, lambda bank: 0, 0)
            steps(pool, step)

        @block.scalar
        def _(act):
            nc.scalar.dma_start(w_stage.rearrange("p (k n) -> p k n", k=KC), w_qkv.rearrange("(k p) n -> p k n", p=P)).then_inc(w_in, 16)
            act.wait_ge(w_in, 16)
            act.wait_ge(wscale_set, 2)
            for k in range(KC):
                nc.scalar.activation(w_hi[:, k, :], w_stage[:, k * 3 * H:(k + 1) * 3 * H], ACT.Copy,
                                     scale=wscale[:, 0:1]).then_inc(w_hi_set, 1)
            act.wait_ge(consts_in, 48)

            def project(n, c):
                for j in range(TPC):
                    act.wait_ge(tr_done, TPC * n + j + 1)
                    nc.scalar.activation(z_hi[:, c, :, j * P:(j + 1) * P],
                                         ps_tr[j % 2][:].rearrange("p (k t) -> p k t", k=KC), ACT.Copy,
                                         scale=Z_SCALE).then_inc(z_hi_set, 1)
                for f in range(8):
                    act.wait_ge(qk_done, 8 * n + f + 1)
                    act.wait_ge(stored[f % STORE_RING], 16 * (2 * n + f // STORE_RING + 1))
                    nc.scalar.activation(y[:, f % STORE_RING], ps_qk[f % 4], ACT.Identity,
                                         bias=bqk[:, f:f + 1], scale=wscale[:, 1:2])
                    nc.scalar.activation(parts[:, f % STORE_RING, 0], ps_qk[f % 4], ACT.Identity,
                                         bias=bqk[:, f:f + 1], scale=wscale[:, 1:2]).then_inc(qk_free, 1)

            with act.Fori(0, BATCH) as i:
                for c in range(2):
                    project(2 * i + c, c)

            def share(w, bank, count, gg):
                t = SHARED_ROWS.index(w // 2)
                act.wait_ge(ring_done[bank], count)
                if w % 2 == 0:
                    act.wait_ge(shared_free, gg * len(SHARED_ROWS) + t + 1)
                at = (w % 2) * (SEQ // 2)
                nc.scalar.copy(shared[:, t % 2, at:at + SEQ // 2], ps_r[bank][:]).then_inc(ring_free[bank], 1)

            def shares(plan, before, gg, u):
                for at, what, w, bank, k in plan:
                    if at == u and what == "scores" and w // 2 in SHARED_ROWS:
                        share(w, bank, before(bank) + k + 1, gg)

            def take_ctx(g, half):
                act.wait_ge(pv_done, 4 + PAIRS * g + KT * (half + 1))
                if half or not isinstance(g, int) or g:
                    act.wait_ge(rsum_set, 2 * g + half)
                nc.scalar.copy(ctx_t[:], ps_c[:]).then_inc(pv_free, 1)

            def step(g, slot, first=False, last=False):
                for u in range(EXPS):
                    act.wait_ge(st_done, EXPS * g + (u + 1))
                    if u % 2 == 0:
                        act.wait_ge(pv_done, PAIRS * g + (u // 2 + 1))
                    nc.scalar.activation(probs[:, u % PROBS], ps_s[u % 2][:], ACT.Exp,
                                         scale=SOFTMAX_SCALE).then_inc(exp_done, 1)
                    if u == PAIR_LAG - 1 and not first:
                        take_ctx(g - 1, 1)
                    if u == PAIR_LAG - 1 + 2 * KT:
                        take_ctx(g, 0)
                    shares(plan_of(g), lambda bank: used(g, bank), g + 1, u)

            shares(prologue, lambda bank: 0, 0, 0)
            steps(act, step)
            take_ctx(GROUPS - 1, 1)

        @block.vector
        def _(dve):
            for credits, count in ((tr_free, 2), (v_free, 2), (qk_free, 4), (exp_done, 2), (pv_done, 4),
                                   (pv_free, 1), (shared_free, 2), *((s, 1) for s in ring_free), *((s, 16) for s in stored), *((s, 16) for s in ctx_out)):
                dve.sem_inc(credits, count)

            def norm_in(n, c):
                dve.wait_ge(x_in[c], 16 * (n // 2 + 1))
                for j in range(TPC):
                    nc.vector.bn_stats(stats[:, c, j, :], xin[:, c, j, :]).then_inc(stats_set, 1)
                dve.wait_ge(stats_set, TPC * (n + 1))
                for j in range(TPC):
                    nc.vector.bn_aggr(mv[:, c, j, :], stats[:, c, j, :]).then_inc(mv_set, 1)
                dve.wait_ge(rstd_set, n + 1)
                for j in range(TPC):
                    nc.vector.tensor_scalar(xin[:, c, j, :], xin[:, c, j, :], mv[:, c, j, 0:1], rstd[:, c, j:j + 1],
                                            ALU.subtract, ALU.mult).then_inc(z_set, 1)

            def split_weights():
                dve.wait_ge(w_in, 16)
                nc.vector.tensor_reduce(amax[:, 0:1], w_stage, AX_X, ALU.max,
                                        apply_absolute_value=True).then_inc(amax_set, 1)
                dve.wait_ge(amax_all, 1)
                nc.vector.tensor_scalar(amax[:, 1:2], amax[:, 1:2], TINY, None, ALU.max).then_inc(exp_set, 1)
                dve.wait_ge(exp_set, 1)
                nc.vector.tensor_single_scalar(amax[:, 2:3].bitcast(I32), amax[:, 1:2].bitcast(I32), EXP_MASK,
                                               ALU.bitwise_and).then_inc(exp_set, 1)
                dve.wait_ge(exp_set, 2)
                nc.vector.tensor_scalar(wscale[:, 0:1].bitcast(I32), amax[:, 2:3].bitcast(I32), -1.0,
                                        SCALE_FROM_EXP, ALU.mult, ALU.add).then_inc(wscale_set, 1)
                nc.vector.tensor_scalar(wscale[:, 1:2].bitcast(I32), amax[:, 2:3].bitcast(I32), INV_FROM_EXP,
                                        None, ALU.add).then_inc(wscale_set, 1)
                dve.wait_ge(wscale_set, 2)
                for k in range(KC):
                    dve.wait_ge(w_hi_set, k + 1)
                    nc.vector.scalar_tensor_tensor(out=w_lo[:, k, :], in0=w_stage[:, k * 3 * H:(k + 1) * 3 * H],
                                                   scalar=wscale[:, 0:1], in1=w_hi[:, k, :], op0=ALU.mult,
                                                   op1=ALU.subtract).then_inc(w_lo_set, 1)

            def project(n, c):
                for j in range(TPC):
                    dve.wait_ge(z_hi_set, TPC * n + j + 1)
                    nc.vector.scalar_tensor_tensor(
                        out=z_lo[:, c, :, j * P:(j + 1) * P], in0=ps_tr[j % 2][:].rearrange("p (k t) -> p k t", k=KC),
                        scalar=Z_SCALE, in1=z_hi[:, c, :, j * P:(j + 1) * P], op0=ALU.mult,
                        op1=ALU.subtract).then_inc(tr_free, 1)
                for j in range(TPC):
                    dve.wait_ge(v_done, TPC * n + j + 1)
                    nc.vector.scalar_tensor_tensor(out=v_all[:, TPC * n + j, :], in0=ps_vp[j % 2][:],
                                                   scalar=wscale[:, 1:2], in1=bv[:], op0=ALU.mult,
                                                   op1=ALU.add).then_inc(v_free, 1)
                for f in range(8):
                    s = f % STORE_RING
                    dve.wait_ge(qk_free, 4 + 8 * n + f + 1)
                    nc.vector.tensor_tensor(y[:, s], y[:, s], parts[:, s, 0], ALU.subtract).then_inc(part_step, 1)
                    dve.wait_ge(part_step, 2 * (8 * n + f) + 1)
                    nc.vector.tensor_copy(parts[:, s, 1], y[:, s]).then_inc(part_step, 1)
                    dve.wait_ge(part_step, 2 * (8 * n + f) + 2)
                    nc.vector.tensor_tensor(parts[:, s, 2], y[:, s], parts[:, s, 1], ALU.subtract).then_inc(parts_set, 1)

            norm_in(0, 0)
            norm_in(1, 1)
            split_weights()
            dve.wait_ge(consts_in, 48)
            project(0, 0)
            norm_in(2, 0)
            project(1, 1)
            norm_in(3, 1)
            project(2, 0)
            project(3, 1)
            for s in range(SLOTS):
                nc.vector.memset(stack[MAX_ROW:ROWS, s, 1, :], 1.0)
            dve.wait_ge(stage_const, 1)
            nc.vector.memset(v_stage[:, :, :, :, HD:HD + 1], 1.0).then_inc(stage_const, 1)

            def reduce_max(w, bank, count):
                dve.wait_ge(ring_done[bank], count)
                nc.vector.tensor_reduce(max_part[:, w:w + 1], ps_r[bank][:], AX_X, ALU.max).then_inc(ring_free[bank], 1)

            def join_max(gg, bank, count):
                dve.wait_ge(shared_free, 2 + len(SHARED_ROWS) * (gg + 1))
                dve.wait_ge(ring_free[bank], count + 1)
                nc.vector.tensor_reduce(maxes[:], max_part[:].rearrange("p (t h) -> p t h", h=2), AX_X,
                                        ALU.max).then_inc(mx_set, 1)

            def split_max(gg, bank, count):
                dve.wait_ge(ring_done[bank], count)
                if not (isinstance(gg, int) and gg == 0):
                    dve.wait_ge(mx_in, 32 * gg)
                turned = ps_r[bank][0:GH * KT, 0:P]
                nc.vector.tensor_scalar(max_rows[:, 0, :], turned, -1.0, None, ALU.mult).then_inc(mx_step, 1)
                dve.wait_ge(mx_step, gg + 1)
                nc.vector.scalar_tensor_tensor(out=max_rows[:, 1, :], in0=turned, scalar=-1.0, in1=max_rows[:, 0, :],
                                               op0=ALU.mult, op1=ALU.subtract).then_inc(ring_free[bank], 1)

            def normalise(g, half, bank, count):
                view = ps_r[bank][:].rearrange("p (t j c) -> p (t j) c", t=4, j=GH)
                dve.wait_ge(ring_done[bank], count)
                nc.vector.reciprocal(rsum[:, half], view[:, :, HD]).then_inc(rsum_set, 1)
                dve.wait_ge(rsum_set, 2 * g + half + 1)
                dve.wait_ge(ctx_out[half], 16 * (g + 1))
                nc.vector.tensor_tensor(ctx_n[:, half].rearrange("p t (j d) -> p (t j) d", j=GH), view[:, :, 0:HD],
                                        rsum[:, half].unsqueeze(2).to_broadcast([P, 4 * GH, HD]),
                                        ALU.mult).then_inc(ring_free[bank], 1)

            last_w = max(w for w in range(MAX_MM) if w // 2 not in SHARED_ROWS)

            def step(g, slot, first=False, last=False):
                due = [(u + (what != "scores"), what, which, bank, k) for u, what, which, bank, k in plan_of(g)]
                for u in range(EXPS + 1):
                    for _, what, which, bank, k in sorted((d for d in due if d[0] == u), key=lambda d: d[1] == "scores"):
                        count = used(g, bank) + (k + 1)
                        if what == "scores" and which // 2 not in SHARED_ROWS:
                            reduce_max(which, bank, count)
                        if what == "max":
                            split_max(g + 1, bank, count)
                        if what == "ctx":
                            normalise(g - which, which, bank, count)
                    if u == MAX_BY - 1 and not last:
                        bank, k = find(plan_of(g), "scores", last_w)
                        join_max(g + 1, bank, used(g, bank) + (k + 1))

            for _, what, w, bank, k in prologue:
                if what == "scores" and w // 2 not in SHARED_ROWS:
                    reduce_max(w, bank, k + 1)
            bank, k = find(prologue, "scores", last_w)
            join_max(0, bank, k + 1)
            bank, k = find(prologue, "max", 0)
            split_max(0, bank, k + 1)
            steps(dve, step)
            normalise(GROUPS - 1, 1, 0, used(GROUPS - 1, 0) + uses(plan_z, 0) + 1)

        @block.tensor
        def _(pe):
            pe.wait_ge(consts_in, 48)

            def transposes(n, c):
                for j in range(TPC):
                    pe.wait_ge(z_set, TPC * n + j + 1)
                    pe.wait_ge(tr_free, TPC * n + j + 1)
                    for k in range(KC):
                        tr = nc.tensor.transpose(ps_tr[j % 2][:, k * P:(k + 1) * P], xin[:, c, j, k * P:(k + 1) * P], ident[:])
                    tr.then_inc(tr_done, 1)

            def project(n, c):
                transposes(n, c)
                pe.wait_ge(tr_free, 2 + TPC * (n + 1))
                pe.wait_ge(w_lo_set, KC)
                for j in range(TPC):
                    pe.wait_ge(v_free, TPC * n + j + 1)
                    t = slice(j * P, (j + 1) * P)
                    passes = [(z_hi, w_hi), (z_hi, w_lo), (z_lo, w_hi)]
                    for m, (a, w) in enumerate(passes):
                        for k in range(KC):
                            mm = nc.tensor.matmul(ps_vp[j % 2][:], a[:, c, k, t], w[:, k, 2 * H:3 * H],
                                                  start=(m == 0 and k == 0), stop=(m == 2 and k == KC - 1))
                    mm.then_inc(v_done, 1)
                for f in range(8):
                    pe.wait_ge(qk_free, 8 * n + f + 1)
                    passes = [(w_hi, z_hi), (w_hi, z_lo), (w_lo, z_hi)]
                    for m, (w, a) in enumerate(passes):
                        for k in range(KC):
                            mm = nc.tensor.matmul(ps_qk[f % 4], w[:, k, f * P:(f + 1) * P], a[:, c, k, :],
                                                  start=(m == 0 and k == 0), stop=(m == 2 and k == KC - 1))
                    mm.then_inc(qk_done, 1)

            with pe.Fori(0, BATCH) as i:
                for c in range(2):
                    project(2 * i + c, c)

            def max_tile(slot, w, bank, count):
                j, qt, kh = w // (2 * KT), w // 2 % KT, w % 2
                pe.wait_ge(ring_free[bank], count)
                nc.tensor.matmul(ps_r[bank][:], stack[0:STACK, slot, 0, j * SEQ + qt * P:j * SEQ + (qt + 1) * P],
                                 stack[0:STACK, slot, 1, j * SEQ + kh * HALF:j * SEQ + (kh + 1) * HALF],
                                 start=True, stop=True).then_inc(ring_done[bank], 1)

            def turn_max(gg, bank, count):
                pe.wait_ge(mx_set, gg + 1)
                pe.wait_ge(ring_free[bank], count)
                nc.tensor.transpose(ps_r[bank][0:GH * KT, 0:P], maxes[:], ident[:]).then_inc(ring_done[bank], 1)

            def turn_ctx(g, half, bank, count):
                pe.wait_ge(pv_free, 1 + 2 * g + half + 1)
                pe.wait_ge(ring_free[bank], count)
                for t in range(4):
                    tr = nc.tensor.transpose(ps_r[bank][:, t * P:(t + 1) * P], ctx_t[:, t * P:(t + 1) * P], ident[:])
                tr.then_inc(ring_done[bank], 1)

            def scores(g, slot, u):
                half, kt, hp = u // (2 * KT), u // 2 % KT, u % 2
                pe.wait_ge(exp_done, EXPS * g + (u + 1))
                for e in range(2):
                    j = 2 * hp + e
                    mm = nc.tensor.matmul(ps_s[u % 2][:, e * HALF:(e + 1) * HALF],
                                          stack[0:ROWS, slot, 1, j * SEQ + kt * P:j * SEQ + (kt + 1) * P],
                                          stack[0:ROWS, slot, 0, j * SEQ + half * HALF:j * SEQ + (half + 1) * HALF],
                                          start=True, stop=True)
                mm.then_inc(st_done, 1)

            def times_v(g, slot, pair):
                half, kt = pair // KT, pair % KT
                pe.wait_ge(exp_done, EXPS * g + (2 * pair + 4))
                if pair == 0:
                    pe.wait_ge(v_staged, g + 1)
                if kt == 0:
                    pe.wait_ge(pv_free, 2 * g + half + 1)
                for j in range(GH):
                    mm = nc.tensor.matmul(ps_c[32 * j:32 * j + 32, :], v_stage[:, slot, kt, j, :],
                                          probs[:, (2 * pair + j // 2) % PROBS, (j % 2) * HALF:(j % 2 + 1) * HALF],
                                          start=(kt == 0), stop=(kt == KT - 1), skip_group_check=True)
                mm.then_inc(pv_done, 1)

            def step(g, slot, first=False, last=False):
                pe.wait_ge(mx_in, 32 * (g + 1))
                if not last:
                    nxt = (slot + 1) % SLOTS
                    pe.wait_ge(loaded[nxt], 192 * loads_by(g + 1, nxt))
                for u in range(EXPS):
                    scores(g, slot, u)
                    for at, what, which, bank, k in plan_of(g):
                        count = used(g, bank) + (k + 1)
                        if at == u and what == "scores":
                            max_tile(nxt, which, bank, count)
                        if at == u and what == "max":
                            turn_max(g + 1, bank, count)
                    if (found := pair_at(u)) is not None:
                        before, pair = found
                        if not before:
                            times_v(g, slot, pair)
                        elif not first:
                            times_v(g - 1, (slot - 1) % SLOTS, pair)
                    for at, what, half, bank, k in plan_of(g):
                        if at == u and what == "ctx":
                            turn_ctx(g - half, half, bank, used(g, bank) + (k + 1))

            def loads_by(g, slot):
                return (g - slot) // SLOTS + 1

            pe.wait_ge(tr_free, 2 + TOKENS // P)
            pe.wait_ge(v_free, 2 + TOKENS // P)
            pe.wait_ge(qk_free, 4 + 8 * CHUNKS)
            pe.wait_ge(loaded[0], 192)
            pe.wait_ge(stage_const, 2)
            for _, what, w, bank, k in prologue:
                if what == "scores":
                    max_tile(0, w, bank, k + 1)
                else:
                    turn_max(0, bank, k + 1)
            steps(pe, step)
            for pair in (PAIRS - 2, PAIRS - 1):
                times_v(GROUPS - 1, 0, pair)
            turn_ctx(GROUPS - 1, 1, 0, used(GROUPS - 1, 0) + uses(plan_z, 0) + 1)


def layers_block(nc, x, ctx_dram, w_o, b_o, w_0, b_0, w_gu, point, w_terms, discount, w_g, w_u, w_d, w_ra, w_b,
                 ident_dram, out):
    F = w_g.shape[1]
    FB = -(-F // P)
    F_LAST = F - (FB - 1) * P
    S = w_gu.shape[1] // 2
    G = w_terms.shape[1] - 1
    TERMS = G + 1
    GRAD_ORDER_MIN, THD = 4, 2.5
    RA = w_ra.shape[1]
    E = 4
    R = (RA - E) // E
    LORA_SCALE = 4.0
    CTX_BITS = 4
    O_, F0, L1, L3 = range(4)
    ROUTE_EXP, ROUTE_STEPS = 9, 20
    T_COLS, H_COLS = TERMS * CHUNK, FB * CHUNK
    assert S == P

    with ExitStack() as ctx:
        def sb(name, shape, dt):
            return ctx.enter_context(nc.sbuf_tensor(name, shape, dt))

        def psum(name, shape, dt=F32):
            return ctx.enter_context(nc.psum_tensor(name, shape, dt))

        def sem(name):
            return ctx.enter_context(nc.semaphore(name))

        xs = sb("xs", [P, TOKENS // P, H], F32)
        zf = sb("zf", [P, TPC, H], F32)
        z_hi = sb("zz_hi", [P, 2, KC, CHUNK], F16)
        z_lo = sb("zz_lo", [P, 2, KC, CHUNK], F16)
        y = sb("yy", [P, TPC, H], F32)
        work = sb("work", [P, T_COLS + H_COLS], F32)
        terms = work[:, 0:T_COLS].rearrange("p (m t) -> p m t", m=TERMS)
        hidden = work[:, T_COLS:T_COLS + H_COLS].rearrange("p (f t) -> p f t", f=FB)
        wd = sb("wd", [P, FB, H], F32)
        wt = sb("wt", [P, TERMS, H], F32)
        wb = sb("wb", [P, H], F32)
        wdims = {"o": H, "0": H, "gu": 2 * S, "ra": RA, "g": F, "u": F}
        names = list(wdims)
        hi = {k: sb(f"hi_{k}", [P, KC, n], F16) for k, n in wdims.items()}
        lo = {k: sb(f"lo_{k}", [P, KC, n], F16) for k, n in wdims.items()}
        w_amax = sb("w_amax", [P, len(names), 3], F32)
        w_scale = sb("w_scale", [P, len(names), 2], F32)
        bo = sb("bo", [P, H], F32)
        b0 = sb("b0", [P, H], F32)
        lp = sb("lp", [P, 1], F32)
        disc = sb("disc", [P, G], F32)
        ident = sb("ident2", [P, P], F32)
        ones = sb("ones", [P, P], F32)
        half = sb("half", [P, TPC], F32)
        eps = sb("eps", [P, TPC], F32)
        turn = sb("turn", [P, 1], F32)
        st_x = sb("st_x", [P, TPC, 6], F32)
        mv_x = sb("mv_x", [P, TPC, 2], F32)
        rs_x = sb("rs_x", [P, TPC], F32)
        st_y = sb("st_y", [P, TPC, 6], F32)
        mv_y = sb("mv_y", [P, TPC, 2], F32)
        rs_y = sb("rs_y", [P, TPC], F32)
        c_amax = sb("c_amax", [P, TPC], F32)
        c_exp = sb("c_exp", [P, TPC], F32)
        c_scale = sb("c_scale", [P, TPC], F32)
        c_inv = sb("c_inv", [P, 2, TPC], F32)
        delta, kept = hidden[:, FB - 1, :], hidden[:, FB - 2, :]
        sg = sb("sg", [P, 2, CHUNK], F32)
        lm = work[:, 0:TPC * RA].rearrange("p (j r) -> p j r", j=TPC)
        gt = sb("gt", [P, 6, TPC], F32)
        rank = sb("rank", [P, TPC, E], F32)
        top = sb("top", [P, TPC], F32)
        gates = sb("gates", [P, TPC, E], F32)
        gm = sb("gm", [P, TPC, P], F32)
        gmt = work[:, T_COLS:T_COLS + TPC * P].rearrange("p (j t) -> p j t", j=TPC)

        ps_t = [psum(f"ps_t{i}", [P, 512]) for i in range(2)]
        ps_y = [psum(f"ps_y{i}", [P, 512]) for i in range(2)]
        ps_p = [psum(f"ps_p{i}", [P, 512]) for i in range(4)]

        w_in = {k: sem(f"w_in_{k}") for k in names}
        c_in = sem("c_in")
        wt_in, wd_in = sem("wt_in"), sem("wd_in")
        xs_in = sem("xs_in")
        cx_in = sem("cx_in")
        mem = sem("mem")
        absd = sem("absd")
        colsum = sem("colsum")
        tern = sem("tern")
        wa = sem("wa")
        wr = sem("wr")
        we = sem("we")
        ws = sem("ws")
        whi = sem("whi")
        wlo = sem("wlo")
        disc_e = sem("disc_e")
        wt_set = sem("wt_set")
        sx, ax, vx, rx = sem("sx"), sem("ax"), sem("vx"), sem("rx")
        z_set = sem("zf_set")
        t_done = sem("t_done")
        zh_set = sem("zh_set")
        t_free = sem("t_free")
        y_done = sem("y_done")
        y_free = sem("y_free")
        sy, ay, vy, ry = sem("sy"), sem("ay"), sem("vy"), sem("ry")
        yn = sem("yn")
        x_set = sem("x_set")
        cs = sem("cs")
        gu_done = sem("gu_done")
        dl = sem("dl")
        p_done = sem("p_done")
        sg_set = sem("sg_set")
        h_set = sem("h_set")
        r_done = sem("r_done")
        rt = sem("rt")
        ex = sem("ex")
        gm_set = sem("gm_set")
        gt_done = sem("gt_done")
        gt_set = sem("gt_set")
        stored = sem("out_stored")
        block = ctx.enter_context(nc.Block())

        stage_at, at = {}, 0
        for k in ("0", "o", "gu", "ra"):
            stage_at[k] = at
            at += KC * wdims[k]
        stage_at["g"] = stage_at["u"] = 0

        def staged(k):
            return work[:, stage_at[k]:stage_at[k] + KC * wdims[k]]

        def kpn(w):
            return w.rearrange("(k p) n -> p k n", p=P)

        order = ["0", "o", "gu", "ra", "g", "u"]
        wd_flat = wd[:].rearrange("p f n -> p (f n)")
        t_a, t_b = wd_flat[:, 0:KC * H], wd_flat[:, KC * H:2 * KC * H]
        inv = {k: w_scale[:, names.index(k), 1:2] for k in names}

        def layer_loops(engine, stage):
            for n in range(CHUNKS):
                stage(n, O_, n, n % 2)
            for layer in (F0, L1):
                with engine.Fori(0, CHUNKS // 2) as i:
                    for c in range(2):
                        stage(CHUNKS * layer + c + 2 * i, layer, 2 * i + c, c)
            for n in range(CHUNKS):
                stage(CHUNKS * L3 + n, L3, n, n % 2)

        @block.sync
        def _(sp):
            sp.dma_start(staged("0").rearrange("p (k n) -> p k n", k=KC), kpn(w_0)).then_inc(w_in["0"], 16)
            for dst, src in ((ident[:], ident_dram), (bo[:], b_o.to_broadcast([P, H])), (b0[:], b_0.to_broadcast([P, H])),
                             (lp[:], point), (disc[:], discount.to_broadcast([P, G]))):
                sp.dma_start(dst, src).then_inc(c_in, 16)
            sp.dma_start(zf[:], ctx_dram[0:CHUNK, :].rearrange("(j p) f -> p j f", p=P)).then_inc(cx_in, 16)
            sp.dma_start(xs[:], x.rearrange("(j p) f -> p j f", p=P)).then_inc(xs_in, 16)
            for n in range(1, CHUNKS):
                sp.wait_ge(t_done, TPC * n)
                sp.dma_start(zf[:], ctx_dram[n * CHUNK:(n + 1) * CHUNK, :].rearrange("(j p) f -> p j f", p=P)
                             ).then_inc(cx_in, 16)
            sp.wait_ge(mem, 5)
            for n in range(CHUNKS):
                sp.wait_ge(x_set, TPC * (CHUNKS * L3 + n + 1))
                sp.dma_start(out[n * CHUNK:(n + 1) * CHUNK, :].rearrange("(j p) f -> p j f", p=P),
                             xs[:, n * TPC:(n + 1) * TPC, :]).then_inc(stored, 16)
            sp.wait_ge(stored, 16 * CHUNKS)

        @block.gpsimd
        def _(pool):
            nc.gpsimd.memset(half[:], -0.5).then_inc(mem, 1)
            nc.gpsimd.memset(eps[:], EPS).then_inc(mem, 1)
            nc.gpsimd.memset(ones[:], 1.0).then_inc(mem, 1)
            nc.gpsimd.memset(gm[:], 0.0).then_inc(mem, 1)
            nc.gpsimd.memset(wb[:], 0.0).then_inc(mem, 1)
            for k, w in (("o", w_o), ("gu", w_gu), ("ra", w_ra)):
                nc.gpsimd.dma_start(staged(k).rearrange("p (k n) -> p k n", k=KC), kpn(w)).then_inc(w_in[k], 16)
            nc.gpsimd.dma_start(wt[:], w_terms).then_inc(wt_in, 16)
            pool.wait_ge(mem, 5)
            nc.gpsimd.dma_start(wb[0:E * R, :], w_b).then_inc(wt_in, 16)
            for m, k in enumerate(order):
                if k == "g":
                    pool.wait_ge(wlo, 4)
                    nc.gpsimd.dma_start(wd[:, 0:FB - 1, :], w_d[0:(FB - 1) * P, :].rearrange("(f p) n -> p f n", p=P)
                                        ).then_inc(wd_in, 16)
                    nc.gpsimd.dma_start(wd[0:F_LAST, FB - 1, :], w_d[(FB - 1) * P:F, :]).then_inc(wd_in, 16)
                if k in ("g", "u"):
                    pool.wait_ge(wlo, order.index(k))
                    nc.gpsimd.dma_start(staged(k).rearrange("p (k n) -> p k n", k=KC), kpn(w_g if k == "g" else w_u)
                                        ).then_inc(w_in[k], 16)
                a = w_amax[:, names.index(k)]
                pool.wait_ge(wa, m + 1)
                nc.gpsimd.partition_all_reduce(a[:, 1:2], a[:, 0:1], P, RMAX).then_inc(wr, 1)

            def inv_std(seen, mv, rs, steps, done, means):
                pool.wait_ge(means, TPC * (seen + 1))
                nc.gpsimd.tensor_tensor(rs[:], mv[:, :, 1], eps[:], ALU.add).then_inc(steps, 1)
                pool.wait_ge(steps, seen + 1)
                nc.gpsimd.tensor_tensor(rs[:], rs[:], half[:], ALU.pow).then_inc(done, 1)

            def stage(s, layer, n, c):
                if not (layer == L3 and n == CHUNKS - 1) and not (layer == O_ and n < CHUNKS - 1):
                    inv_std(s + 1 - CHUNKS, mv_x, rs_x, vx, rx, ax)
                inv_std(s, mv_y, rs_y, vy, ry, ay)
                for j in range(TPC):
                    pool.wait_ge(yn, TPC * s + (j + 1))
                    tile = xs[:, TPC * n + j, :] if isinstance(n, int) else xs[:, bass.ds(TPC * n + j, 1), :].rearrange("p a f -> p (a f)")
                    nc.gpsimd.tensor_tensor(tile, tile, y[:, j, :], ALU.add).then_inc(x_set, 1)

            pool.wait_ge(xs_in, 16)
            layer_loops(pool, stage)

        @block.scalar
        def _(act):
            act.wait_ge(w_in["0"], 16)
            nc.scalar.activation(t_a, staged("0"), ACT.Abs).then_inc(absd, 1)
            act.wait_ge(c_in, 80)
            nc.scalar.activation(disc[:], disc[:], ACT.Exp, scale=-1.0).then_inc(disc_e, 1)
            for m, k in enumerate(order):
                act.wait_ge(ws, 2 * (m + 1))
                nc.scalar.activation(hi[k][:].rearrange("p k n -> p (k n)"), staged(k), ACT.Copy,
                                     scale=w_scale[:, names.index(k), 0:1]).then_inc(whi, 1)
            act.wait_ge(disc_e, 1)
            act.wait_ge(wt_in, 32)
            for m in range(G):
                nc.scalar.activation(wt[:, m + 1, :], wt[:, m + 1, :], ACT.Copy, scale=disc[:, m:m + 1]).then_inc(wt_set, 1)

            def high_parts(s, c):
                for j in range(TPC):
                    act.wait_ge(t_done, TPC * s + (j + 1))
                    nc.scalar.activation(z_hi[:, c, :, j * P:(j + 1) * P],
                                         ps_t[j % 2][:].rearrange("p (k t) -> p k t", k=KC), ACT.Copy,
                                         scale=Z_SCALE).then_inc(zh_set, 1)

            def stage(s, layer, n, c):
                if not (layer == L3 and n == CHUNKS - 1):
                    high_parts(s + 1, 1 - c)
                if layer == L1:
                    for f in range(FB):
                        rows = P if f < FB - 1 else F_LAST
                        k = (s - CHUNKS * L1) * FB + f
                        act.wait_ge(p_done, 2 * k + 1)
                        act.wait_ge(h_set, k + 1)
                        nc.scalar.activation(sg[0:rows, f % 2, :], ps_p[2 * (f % 2)][0:rows, :], ACT.Silu,
                                             scale=inv["g"][0:rows, :]).then_inc(sg_set, 1)
                if layer == L3:
                    act.wait_ge(rt, ROUTE_STEPS * n + ROUTE_EXP)
                    nc.scalar.activation(gates[:], gates[:], ACT.Exp).then_inc(ex, 1)
                    for j in range(TPC):
                        act.wait_ge(gt_done, TPC * n + j + 1)
                        nc.scalar.copy(gmt[:, j, :], ps_p[1 + j % 2][:, 0:P]).then_inc(gt_set, 1)
                if layer in (L1, L3):
                    for j in range(TPC):
                        act.wait_ge(y_done, TPC * s + (j + 1))
                        act.wait_ge(x_set, TPC * s)
                        nc.scalar.copy(y[:, j, :], ps_y[j % 2][:]).then_inc(y_free, 1)

            high_parts(0, 0)
            layer_loops(act, stage)

        @block.vector
        def _(dve):
            for credits, count in ((t_free, 2), (y_free, 2), (h_set, 2)):
                dve.sem_inc(credits, count)

            def split(m, k):
                a, sc = w_amax[:, names.index(k)], w_scale[:, names.index(k)]
                if k != "0":
                    dve.wait_ge(w_in[k], 16)
                nc.vector.tensor_reduce(a[:, 0:1], staged(k), AX_X, ALU.max, apply_absolute_value=True).then_inc(wa, 1)
                dve.wait_ge(wr, m + 1)
                nc.vector.tensor_scalar(a[:, 1:2], a[:, 1:2], TINY, None, ALU.max).then_inc(we, 1)
                dve.wait_ge(we, 2 * m + 1)
                nc.vector.tensor_single_scalar(a[:, 2:3].bitcast(I32), a[:, 1:2].bitcast(I32), EXP_MASK,
                                               ALU.bitwise_and).then_inc(we, 1)
                dve.wait_ge(we, 2 * m + 2)
                nc.vector.tensor_scalar(sc[:, 0:1].bitcast(I32), a[:, 2:3].bitcast(I32), -1.0, SCALE_FROM_EXP,
                                        ALU.mult, ALU.add).then_inc(ws, 1)
                nc.vector.tensor_scalar(sc[:, 1:2].bitcast(I32), a[:, 2:3].bitcast(I32), INV_FROM_EXP, None,
                                        ALU.add).then_inc(ws, 1)
                dve.wait_ge(ws, 2 * m + 2)
                dve.wait_ge(whi, m + 1)
                nc.vector.scalar_tensor_tensor(out=lo[k][:].rearrange("p k n -> p (k n)"), in0=staged(k),
                                               scalar=sc[:, 0:1], in1=hi[k][:].rearrange("p k n -> p (k n)"),
                                               op0=ALU.mult, op1=ALU.subtract).then_inc(wlo, 1)

            def ternary():
                w = staged("0")
                k3 = lambda ap: ap.rearrange("p (k n) -> p k n", k=KC)
                dve.wait_ge(colsum, 1)
                nc.vector.tensor_scalar(sg[:, 0, :], ps_y[0][:], 1.0 / H, 0.7, ALU.mult, ALU.mult).then_inc(tern, 1)
                dve.wait_ge(tern, 1)
                thr = sg[:, 0:1, :].to_broadcast([P, KC, H])
                nc.vector.tensor_tensor(k3(t_a), k3(w), thr, ALU.is_gt).then_inc(tern, 1)
                nc.vector.scalar_tensor_tensor(out=k3(t_b), in0=k3(w), scalar=-1.0, in1=thr, op0=ALU.mult,
                                               op1=ALU.is_gt).then_inc(tern, 1)
                dve.wait_ge(tern, 3)
                nc.vector.tensor_tensor(t_a, t_a, t_b, ALU.subtract).then_inc(tern, 1)
                dve.wait_ge(tern, 4)
                nc.vector.tensor_tensor(t_a, t_a, w, ALU.subtract).then_inc(tern, 1)
                dve.wait_ge(tern, 5)
                nc.vector.tensor_tensor(w, w, t_a, ALU.add).then_inc(tern, 1)
                dve.wait_ge(tern, 6)

            def scale_context(n, c):
                dve.wait_ge(cx_in, 16 * (n + 1))
                nc.vector.tensor_reduce(c_amax[:], zf[:], AX_X, ALU.max, apply_absolute_value=True).then_inc(cs, 1)
                dve.wait_ge(cs, 6 * n + 1)
                nc.vector.tensor_scalar(c_amax[:], c_amax[:], TINY, None, ALU.max).then_inc(cs, 1)
                dve.wait_ge(cs, 6 * n + 2)
                nc.vector.tensor_single_scalar(c_exp[:].bitcast(I32), c_amax[:].bitcast(I32), EXP_MASK,
                                               ALU.bitwise_and).then_inc(cs, 1)
                dve.wait_ge(cs, 6 * n + 3)
                nc.vector.tensor_scalar(c_scale[:].bitcast(I32), c_exp[:].bitcast(I32), -1.0,
                                        float((254 + CTX_BITS) << 23), ALU.mult, ALU.add).then_inc(cs, 1)
                nc.vector.tensor_scalar(c_inv[:, c, :].bitcast(I32), c_exp[:].bitcast(I32), -float(CTX_BITS << 23), None,
                                        ALU.add).then_inc(cs, 1)
                dve.wait_ge(cs, 6 * n + 5)
                nc.vector.tensor_scalar(c_inv[:, c, :], c_inv[:, c, :], inv["o"], None, ALU.mult).then_inc(cs, 1)
                for j in range(TPC):
                    nc.vector.tensor_scalar(zf[:, j, :], zf[:, j, :], c_scale[:, j:j + 1], None,
                                            ALU.mult).then_inc(z_set, 1)

            def norm_in(s, n):
                seen = s - CHUNKS
                dve.wait_ge(x_set, TPC * (seen + 1))
                def tile(j):
                    if isinstance(n, int):
                        return xs[:, TPC * n + j, :]
                    return xs[:, bass.ds(TPC * n + j, 1), :].rearrange("p a f -> p (a f)")
                for j in range(TPC):
                    nc.vector.bn_stats(st_x[:, j, :], tile(j)).then_inc(sx, 1)
                dve.wait_ge(sx, TPC * (seen + 1))
                nc.vector.memset(turn[:], 0.0)
                for j in range(TPC):
                    nc.vector.bn_aggr(mv_x[:, j, :], st_x[:, j, :]).then_inc(ax, 1)
                dve.wait_ge(rx, seen + 1)
                dve.wait_ge(t_done, TPC * s)
                for j in range(TPC):
                    nc.vector.tensor_scalar(zf[:, j, :], tile(j), mv_x[:, j, 0:1], rs_x[:, j:j + 1], ALU.subtract,
                                            ALU.mult).then_inc(z_set, 1)

            def low_parts(s, c):
                for j in range(TPC):
                    dve.wait_ge(zh_set, TPC * s + (j + 1))
                    nc.vector.scalar_tensor_tensor(
                        out=z_lo[:, c, :, j * P:(j + 1) * P], in0=ps_t[j % 2][:].rearrange("p (k t) -> p k t", k=KC),
                        scalar=Z_SCALE, in1=z_hi[:, c, :, j * P:(j + 1) * P], op0=ALU.mult,
                        op1=ALU.subtract).then_inc(t_free, 1)

            def make_terms(q):
                DL = TERMS + 4
                dve.wait_ge(gu_done, q + 1)
                nc.vector.tensor_scalar(delta, ps_y[0][:], inv["gu"], lp[:, 0:1], ALU.mult,
                                        ALU.subtract).then_inc(dl, 1)
                nc.vector.tensor_scalar(terms[:, 0, :], ps_y[1][:], inv["gu"], None, ALU.mult).then_inc(dl, 1)
                dve.wait_ge(dl, DL * q + 2)
                nc.vector.tensor_single_scalar(kept, delta, THD, ALU.is_le).then_inc(dl, 1)
                dve.wait_ge(dl, DL * q + 3)
                nc.vector.scalar_tensor_tensor(out=kept, in0=delta, scalar=-THD, in1=kept, op0=ALU.is_ge,
                                               op1=ALU.mult).then_inc(dl, 1)
                dve.wait_ge(dl, DL * q + 4)
                nc.vector.tensor_tensor(kept, kept, delta, ALU.mult).then_inc(dl, 1)
                for m in range(1, TERMS):
                    dve.wait_ge(dl, DL * q + (4 + m))
                    by = kept if m == GRAD_ORDER_MIN + 1 else delta
                    nc.vector.tensor_tensor(terms[:, m, :], terms[:, m - 1, :], by, ALU.mult).then_inc(dl, 1)

            def make_hidden(q):
                for f in range(FB):
                    rows = P if f < FB - 1 else F_LAST
                    k = q * FB + f
                    dve.wait_ge(sg_set, k + 1)
                    dve.wait_ge(p_done, 2 * k + 2)
                    nc.vector.scalar_tensor_tensor(out=hidden[0:rows, f, :], in0=ps_p[2 * (f % 2) + 1][0:rows, :],
                                                   scalar=inv["u"][0:rows, :], in1=sg[0:rows, f % 2, :], op0=ALU.mult,
                                                   op1=ALU.mult).then_inc(h_set, 1)

            def route(n):
                base = ROUTE_STEPS * n
                count = [0]

                def done(ins, wait=True):
                    count[0] += 1
                    ins.then_inc(rt, 1)
                    if wait:
                        dve.wait_ge(rt, base + count[0])

                dve.wait_ge(r_done, n + 1)
                done(nc.vector.tensor_scalar(lm, ps_p[0][:, 0:TPC * RA].rearrange("p (j r) -> p j r", j=TPC),
                                             inv["ra"], None, ALU.mult))
                lg = lm[:, :, 0:E]
                pairs = [(a, b) for a in range(E) for b in range(a + 1, E)]
                done(nc.vector.tensor_reduce(top[:], lg, AX_X, ALU.max), wait=False)
                for i, (a, b) in enumerate(pairs):
                    done(nc.vector.tensor_tensor(gt[:, i, :], lg[:, :, b], lg[:, :, a], ALU.is_gt), wait=(i == 5))
                done(nc.vector.tensor_tensor(gates[:], lg, top[:].unsqueeze(2).to_broadcast([P, TPC, E]), ALU.subtract))
                assert count[0] == ROUTE_EXP
                g = lambda a, b: gt[:, pairs.index((a, b)), :]
                chains = [(0, [(g(0, 1), 1), (g(0, 2), 1), (g(0, 3), 1)]), (1, [(g(0, 1), -1), (g(1, 2), 1), (g(1, 3), 1)]),
                          (2, [(g(0, 2), -1), (g(1, 2), -1), (g(2, 3), 1)]), (3, [(g(0, 3), -1), (g(1, 3), -1), (g(2, 3), -1)])]
                for step in (1, 2):
                    for e, terms_ in chains:
                        r = rank[:, :, e]
                        if step == 1:
                            (a, sa), (b, sb_) = terms_[0], terms_[1]
                            done(nc.vector.scalar_tensor_tensor(out=r, in0=a, scalar=float(sa), in1=b, op0=ALU.mult,
                                                                op1=ALU.add if sb_ > 0 else ALU.subtract), wait=(e == 3))
                        else:
                            c_, sc_ = terms_[2]
                            done(nc.vector.scalar_tensor_tensor(out=r, in0=r, scalar=float(sum(s < 0 for _, s in terms_)), in1=c_,
                                                                op0=ALU.add, op1=ALU.add if sc_ > 0 else ALU.subtract),
                                 wait=(e == 3))
                dve.wait_ge(ex, n + 1)
                done(nc.vector.scalar_tensor_tensor(out=gates[:], in0=rank[:], scalar=2.0, in1=gates[:], op0=ALU.is_lt,
                                                    op1=ALU.mult))
                done(nc.vector.tensor_reduce(top[:], gates[:], AX_X, ALU.add))
                done(nc.vector.reciprocal(top[:], top[:]))
                assert count[0] == ROUTE_STEPS, count
                nc.vector.scalar_tensor_tensor(out=gates[:], in0=gates[:], scalar=LORA_SCALE,
                                               in1=top[:].unsqueeze(2).to_broadcast([P, TPC, E]), op0=ALU.mult,
                                               op1=ALU.mult).then_inc(gm_set, 1)
                dve.wait_ge(gm_set, (1 + TPC) * n + 1)
                dve.wait_ge(mem, 5)
                for j in range(TPC):
                    nc.vector.tensor_tensor(gm[:, j, 0:E * R].rearrange("p (e r) -> p e r", e=E),
                                            lm[:, j, E:RA].rearrange("p (e r) -> p e r", e=E),
                                            gates[:, j, :].unsqueeze(2).to_broadcast([P, E, R]),
                                            ALU.mult).then_inc(gm_set, 1)

            def finish(s, layer, c):
                for j in range(TPC):
                    if layer in (O_, F0):
                        dve.wait_ge(y_done, TPC * s + (j + 1))
                        if layer != O_ or not isinstance(s, int) or s:
                            dve.wait_ge(x_set, TPC * s)
                        nc.vector.scalar_tensor_tensor(out=y[:, j, :], in0=ps_y[j % 2][:],
                                                       scalar=c_inv[:, c, j:j + 1] if layer == O_ else inv["0"],
                                                       in1=(bo if layer == O_ else b0)[:], op0=ALU.mult,
                                                       op1=ALU.add).then_inc(y_free, 1)
                    dve.wait_ge(y_free, 2 + TPC * s + (j + 1))
                    nc.vector.bn_stats(st_y[:, j, :], y[:, j, :]).then_inc(sy, 1)
                dve.wait_ge(sy, TPC * (s + 1))
                nc.vector.memset(turn[:], 0.0)
                for j in range(TPC):
                    nc.vector.bn_aggr(mv_y[:, j, :], st_y[:, j, :]).then_inc(ay, 1)
                dve.wait_ge(ry, s + 1)
                for j in range(TPC):
                    nc.vector.tensor_scalar(y[:, j, :], y[:, j, :], mv_y[:, j, 0:1], rs_y[:, j:j + 1], ALU.subtract,
                                            ALU.mult).then_inc(yn, 1)

            def stage(s, layer, n, c):
                if layer == O_ and n < CHUNKS - 1:
                    scale_context(n + 1, 1 - c)
                    low_parts(s + 1, 1 - c)
                elif not (layer == L3 and n == CHUNKS - 1):
                    norm_in(s + 1, (n + 1) % CHUNKS)
                    low_parts(s + 1, 1 - c)
                if layer == L1:
                    make_terms(s - CHUNKS * L1)
                    make_hidden(s - CHUNKS * L1)
                if layer == L3:
                    route(n)
                finish(s, layer, c)

            ternary()
            for m, k in enumerate(order):
                split(m, k)
            dve.wait_ge(c_in, 80)
            scale_context(0, 0)
            low_parts(0, 0)
            layer_loops(dve, stage)

        @block.tensor
        def _(pe):
            pe.wait_ge(absd, 1)
            pe.wait_ge(mem, 5)
            for k in range(KC):
                mm = nc.tensor.matmul(ps_y[0][:], ones[:], t_a[:, k * H:(k + 1) * H], start=(k == 0), stop=(k == KC - 1))
            mm.then_inc(colsum, 1)
            pe.wait_ge(c_in, 80)

            def transposes(s):
                for j in range(TPC):
                    pe.wait_ge(z_set, TPC * s + (j + 1))
                    pe.wait_ge(t_free, TPC * s + (j + 1))
                    for k in range(KC):
                        tr = nc.tensor.transpose(ps_t[j % 2][:, k * P:(k + 1) * P], zf[:, j, k * P:(k + 1) * P], ident[:])
                    tr.then_inc(t_done, 1)

            def by_tokens(dst, key, c, j, cols, start=True, stop=True):
                t = slice(j * P, (j + 1) * P)
                for m, (a, w) in enumerate(((z_hi, hi[key]), (z_hi, lo[key]), (z_lo, hi[key]))):
                    for k in range(KC):
                        mm = nc.tensor.matmul(dst, a[:, c, k, t], w[:, k, cols], start=(m == 0 and k == 0),
                                              stop=(m == 2 and k == KC - 1))
                return mm

            def by_columns(dst, key, c, cols):
                for m, (w, a) in enumerate(((hi[key], z_hi), (hi[key], z_lo), (lo[key], z_hi))):
                    for k in range(KC):
                        mm = nc.tensor.matmul(dst, w[:, k, cols], a[:, c, k, :], start=(m == 0 and k == 0),
                                              stop=(m == 2 and k == KC - 1))
                return mm

            def main(s, layer, n, c):
                pe.wait_ge(t_free, 2 + TPC * (s + 1))
                if layer in (O_, F0):
                    for j in range(TPC):
                        pe.wait_ge(y_free, TPC * s + (j + 1))
                        by_tokens(ps_y[j % 2][:], "o" if layer == O_ else "0", c, j, slice(0, H)).then_inc(y_done, 1)
                if layer == L1:
                    q = s - CHUNKS * L1
                    pe.wait_ge(y_free, TPC * s + 2)
                    by_columns(ps_y[0][:], "gu", c, slice(0, S))
                    by_columns(ps_y[1][:], "gu", c, slice(S, 2 * S)).then_inc(gu_done, 1)
                    for f in range(FB):
                        rows = P if f < FB - 1 else F_LAST
                        cols = slice(f * P, f * P + rows)
                        pe.wait_ge(h_set, q * FB + (f + 1))
                        by_columns(ps_p[2 * (f % 2)][0:rows, :], "g", c, cols).then_inc(p_done, 1)
                        by_columns(ps_p[2 * (f % 2) + 1][0:rows, :], "u", c, cols).then_inc(p_done, 1)
                    pe.wait_ge(dl, (TERMS + 4) * (q + 1))
                    for j in range(TPC):
                        t = slice(j * P, (j + 1) * P)
                        pe.wait_ge(y_free, TPC * s + (j + 1))
                        for m in range(TERMS):
                            nc.tensor.matmul(ps_y[j % 2][:], terms[:, m, t], wt[:, m, :], start=(m == 0), stop=False)
                        if j == 0:
                            pe.wait_ge(h_set, 2 + FB * (q + 1))
                        for f in range(FB):
                            rows = P if f < FB - 1 else F_LAST
                            mm = nc.tensor.matmul(ps_y[j % 2][:], hidden[0:rows, f, t], wd[0:rows, f, :], start=False,
                                                  stop=(f == FB - 1))
                        mm.then_inc(y_done, 1)
                if layer == L3:
                    for j in range(TPC):
                        mm = by_tokens(ps_p[0][:, j * RA:(j + 1) * RA], "ra", c, j, slice(0, RA))
                    mm.then_inc(r_done, 1)
                    for j in range(TPC):
                        pe.wait_ge(gm_set, (1 + TPC) * n + j + 2)
                        if TPC * n + j >= 2:
                            pe.wait_ge(gt_set, TPC * n + j - 1)
                        nc.tensor.transpose(ps_p[1 + j % 2][:, 0:P], gm[:, j, :], ident[:]).then_inc(gt_done, 1)
                    for j in range(TPC):
                        pe.wait_ge(gt_set, TPC * n + j + 1)
                        pe.wait_ge(y_free, TPC * s + (j + 1))
                        nc.tensor.matmul(ps_y[j % 2][:], gmt[:, j, :], wb[:], start=True, stop=True).then_inc(y_done, 1)

            def stage(s, layer, n, c):
                if not (layer == L3 and n == CHUNKS - 1):
                    transposes(s + 1)
                main(s, layer, n, c)

            transposes(0)
            pe.wait_ge(wlo, len(order))
            pe.wait_ge(wt_in, 32)
            pe.wait_ge(wt_set, G)
            pe.wait_ge(wd_in, 32)
            layer_loops(pe, stage)


def sandwich_kernel(nc, t, out):
    context = nc.dram_tensor("context", [TOKENS, H], F32, kind="Internal").ap()
    attention_block(nc, t["x"], t["w_qkv"], t["b_qk"], t["b_v"], t["ident"], context)
    layers_block(nc, t["x"], context, t["w_o"], t["b_o"], t["w_0"], t["b_0"], t["w_gu"], t["point"], t["w_terms"],
                 t["discount"], t["w_g"], t["w_u"], t["w_d"], t["w_ra"], t["w_b"], t["ident"], out)


_OUTS = [((BATCH, SEQ, H), "float32")]


def kernel(**inputs):
    import numpy as _np
    import concourse.bacc as _bacc
    from concourse import mybir as _mybir
    from concourse.bass_utils import run_bass_kernel_spmd as _run

    nc = _bacc.Bacc("TRN2", target_bir_lowering=False, num_devices=1)
    nc.disable_value_cache = True
    a = {k: _np.asarray(v) for k, v in inputs.items()}
    two_h = 2 * H
    bias = a["L0_attn_attn_qkvb"]
    laid = {
        "x": a["L0_attn_x"].reshape(TOKENS, H),
        "w_qkv": a["L0_attn_attn_qkvw"],
        "b_qk": bias[:two_h].reshape(2 * KC, P).T,
        "b_v": bias[two_h:].reshape(1, H),
        "ident": _np.eye(P, dtype=_np.float32),
        "w_o": a["L0_attn_attn_ow"],
        "b_o": a["L0_attn_attn_ob"].reshape(1, H),
        "w_0": a["L0_ffn_weight"].T,
        "b_0": a["L0_ffn_bias"].reshape(1, H),
        "w_gu": _np.concatenate([a["L1_attn_gate_w"], a["L1_attn_up_w"]], 0).T,
        "point": a["L1_attn_local_point"].reshape(-1, 1),
        "w_terms": _np.concatenate([a["L1_attn_local_approx_output"][:, :, None], a["L1_attn_fuse_weight"]], 2).transpose(1, 2, 0),
        "discount": a["L1_attn_discount_factor"].reshape(1, -1),
        "w_g": a["L1_attn_ffn_gate_w"].T,
        "w_u": a["L1_attn_ffn_up_w"].T,
        "w_d": a["L1_attn_ffn_down_w"].T,
        "w_ra": _np.concatenate([a["L1_ffn_router_w"], a["L1_ffn_A"].reshape(-1, H)], 0).T,
        "w_b": a["L1_ffn_B"].transpose(0, 2, 1).reshape(-1, H),
    }
    arrays, t = {}, {}
    for name, value in laid.items():
        value = _np.ascontiguousarray(value)
        arrays[f"in_{name}_dram"] = value
        t[name] = nc.dram_tensor(f"in_{name}_dram", value.shape, _mybir.dt.from_np(value.dtype), kind="ExternalInput").ap()
    out = nc.dram_tensor("out_0_dram", (TOKENS, H), F32, kind="ExternalOutput").ap()
    sandwich_kernel(nc, t, out)
    r = _run(nc, [arrays], core_ids=[0])
    return r.results[0]["out_0_dram"].reshape(BATCH, SEQ, H)
```

```python
from contextlib import ExitStack

import concourse.bass as bass
from concourse import mybir

F32 = mybir.dt.float32
F16 = mybir.dt.float16
BF16 = mybir.dt.bfloat16
I32 = mybir.dt.int32
ACT = mybir.ActivationFunctionType
ALU = mybir.AluOpType
AX_X = mybir.AxisListType.X
RMAX = bass.bass_isa.ReduceOp.max

P = 128
BATCH, SEQ, H = 2, 1024, 512
TOKENS = BATCH * SEQ
KC = H // P
HEADS = 32
HD = H // HEADS
SOFTMAX_SCALE = float(HD) ** -0.5
EPS = 1e-5
CHUNK = 512
TPC = CHUNK // P
CHUNKS = TOKENS // CHUNK

Z_BITS = 10
Z_SCALE = float(2 ** Z_BITS)
W_BITS = 14
EXP_MASK = 0x7F800000
SCALE_FROM_EXP = float((254 + W_BITS) << 23)
INV_FROM_EXP = -float((W_BITS + Z_BITS) << 23)
TINY = 1e-30

GH = 4
GROUPS_B = HEADS // GH
GROUPS = BATCH * GROUPS_B
KT = SEQ // P
HALF = SEQ // 2
Q_ROWS = (0, 1, 2, 0, 1, 0)
K_ROWS = (0, 0, 0, 1, 1, 2)
STACK = 6 * HD
MAX_ROW = STACK
ROWS = STACK + 2
SLOTS = 3
MAX_MM = GH * KT * 2
MAX_BY = 26
EXPS = 2 * KT * 2
PAIRS = EXPS // 2
PROBS = 8
PAIR_LAG = 5
SHARED_ROWS = ()
STORE_RING = 4
RING = 3
FOLDS = 9


def pair_at(u):
    for p in range(-2, PAIRS):
        first_of_half = p % KT == 0
        if 2 * p + PAIR_LAG + first_of_half == u:
            return (p < 0, p % PAIRS)
    return None


def ring_plan(prologue=False, first=False, last=False):
    plan, n = [], 0

    def use(u, what, which):
        nonlocal n
        plan.append((u, what, which, n % RING, n // RING))
        n += 1

    if prologue:
        for w in range(MAX_MM):
            use(0, "scores", w)
        use(1, "max", 0)
        return plan
    for u in range(EXPS):
        if not last:
            for w in range(MAX_MM * min(u, MAX_BY) // MAX_BY, MAX_MM * min(u + 1, MAX_BY) // MAX_BY):
                use(u, "scores", w)
            if u == MAX_BY + 2:
                use(u, "max", 0)
        if u == PAIR_LAG + 2 and not first:
            use(u, "ctx", 1)
        if u == PAIR_LAG + 2 + 2 * KT:
            use(u, "ctx", 0)
    return plan


def uses(plan, bank):
    return sum(b == bank for _, _, _, b, _ in plan)


def find(plan, what, which):
    return next((b, k) for _, a, w, b, k in plan if (a, w) == (what, which))


def attention_block(nc, x, w_qkv, b_qk, b_v, ident_dram, ctx_dram):
    qk_dram = nc.dram_tensor("qk_parts", [2, 3, TOKENS // SEQ * H, SEQ], BF16, kind="Internal").ap()
    qk_groups = qk_dram.rearrange("w s (g r) t -> w s g r t", r=GH * HD)

    with ExitStack() as ctx:
        def sb(name, shape, dt):
            return ctx.enter_context(nc.sbuf_tensor(name, shape, dt))

        def psum(name, shape, dt=F32):
            return ctx.enter_context(nc.psum_tensor(name, shape, dt))

        def sem(name):
            return ctx.enter_context(nc.semaphore(name))

        arena = sb("arena", [P, PROBS * 2 * HALF], F32)
        xin = arena[:, 0:2 * TPC * H].rearrange("p (c j f) -> p c j f", c=2, j=TPC)
        z_both = arena[:, 2 * TPC * H:4 * TPC * H].bitcast(F16).rearrange("p (w c k t) -> p w c k t", w=2, c=2, k=KC)
        z_hi, z_lo = z_both[:, 0], z_both[:, 1]
        probs = arena[:].rearrange("p (r t) -> p r t", r=PROBS)
        w_hi = sb("w_hi", [P, KC, 3 * H], F16)
        w_lo = sb("w_lo", [P, KC, 3 * H], F16)
        bqk = sb("bqk", [P, 2 * KC], F32)
        bv = sb("bv", [P, H], F32)
        ident = sb("ident", [P, P], F32)
        amax = sb("amax", [P, 4], F32)
        wscale = sb("wscale", [P, 2], F32)
        stats = sb("stats", [P, 2, TPC, 6], F32)
        mv = sb("mv", [P, 2, TPC, 2], F32)
        rstd = sb("rstd", [P, 2, TPC], F32)
        neg_half = sb("neg_half", [P, TPC], F32)
        y = sb("y", [P, STORE_RING, CHUNK], F32)
        parts = sb("parts", [P, STORE_RING, 3, CHUNK], BF16)
        v_all = sb("v_all", [P, TOKENS // P, H], F32)
        stack = sb("stack", [P, SLOTS, 2, GH * SEQ], BF16)
        w_stage = stack[:].rearrange("p s w t -> p (s w t)")[:, 0:2 * KC * 3 * H].bitcast(F32)
        v_stage = sb("v_stage", [P, SLOTS, KT, GH, 32], F32)
        shared = sb("shared", [P, 2, SEQ], F32)
        max_part = sb("max_part", [P, MAX_MM], F32)
        maxes = sb("maxes", [P, GH * KT], F32)
        max_rows = sb("max_rows", [GH * KT, 2, P], BF16)
        ctx_t = sb("ctx_t", [P, HALF], F32)
        rsum = sb("rsum", [P, 2, 4 * GH], F32)
        ctx_n = sb("ctx_n", [P, 2, 4, GH * HD], F32)

        ps_s = [psum(f"ps_s{i}", [P, 2 * HALF]) for i in range(2)]
        ps_c = psum("ps_c", [P, HALF])
        ps_r = [psum(f"ps_r{i}", [P, 512]) for i in range(RING)]
        ps_tr = ps_r[0:2]
        ps_vp = [ps_c, ps_r[2]]
        ps_qk = [ps_s[i][:, 512 * e:512 * (e + 1)] for i in range(2) for e in range(2)]

        consts_in = sem("consts_in")
        w_in = sem("w_in")
        x_in = [sem(f"x_in{c}") for c in range(2)]
        neg_half_set = sem("neg_half_set")
        amax_set = sem("amax_set")
        amax_all = sem("amax_all")
        exp_set = sem("exp_set")
        wscale_set = sem("wscale_set")
        w_hi_set = sem("w_hi_set")
        w_lo_set = sem("w_lo_set")
        stats_set = sem("stats_set")
        mv_set = sem("mv_set")
        var_eps = sem("var_eps")
        rstd_set = sem("rstd_set")
        z_set = sem("z_set")
        tr_done = sem("tr_done")
        z_hi_set = sem("z_hi_set")
        tr_free = sem("tr_free")
        v_done = sem("v_done")
        v_free = sem("v_free")
        qk_done = sem("qk_done")
        qk_free = sem("qk_free")
        part_step = sem("part_step")
        parts_set = sem("parts_set")
        stored = [sem(f"stored{s}") for s in range(STORE_RING)]
        stage_const = sem("stage_const")
        loaded = [sem(f"loaded{i}") for i in range(SLOTS)]
        v_staged = sem("v_staged")
        ring_done = [sem(f"ring_done{b}") for b in range(RING)]
        ring_free = [sem(f"ring_free{b}") for b in range(RING)]
        folded = sem("folded")
        shared_free = sem("shared_free")
        mx_set = sem("mx_set")
        mx_step = sem("mx_step")
        mx_in = sem("mx_in")
        st_done = sem("st_done")
        exp_done = sem("exp_done")
        pv_done = sem("pv_done")
        pv_free = sem("pv_free")
        rsum_set = sem("rsum_set")
        ctx_out = [sem(f"ctx_out{h}") for h in range(2)]
        block = ctx.enter_context(nc.Block())

        prologue, plan0 = ring_plan(prologue=True), ring_plan(first=True)
        plan_n, plan_z = ring_plan(), ring_plan(last=True)

        def plan_of(g):
            return plan_n if not isinstance(g, int) else plan0 if g == 0 else plan_z if g == GROUPS - 1 else plan_n

        def used(g, bank):
            if isinstance(g, int) and g == 0:
                return uses(prologue, bank)
            return uses(prologue, bank) + uses(plan0, bank) + uses(plan_n, bank) * (g - 1)

        def after(g, what, which):
            bank, k = find(plan_of(g), what, which)
            return bank, used(g, bank) + k + 1

        def steps(engine, step):
            step(0, 0, first=True)
            with engine.Fori(0, (GROUPS - 4) // SLOTS) as i:
                step(3 * i + 1, 1)
                step(3 * i + 2, 2)
                step(3 * i + 3, 0)
            step(GROUPS - 3, 1)
            step(GROUPS - 2, 2)
            step(GROUPS - 1, 0, last=True)

        @block.sync
        def _(sp):
            for n in range(2):
                sp.dma_start(xin[:, n], x[n * CHUNK:(n + 1) * CHUNK, :].rearrange("(j p) f -> p j f", p=P)).then_inc(x_in[n], 16)
            sp.dma_start(ident[:], ident_dram).then_inc(consts_in, 16)
            sp.dma_start(bqk[:], b_qk).then_inc(consts_in, 16)
            sp.dma_start(bv[:], b_v.to_broadcast([P, H])).then_inc(consts_in, 16)

            def store_parts(n, c):
                for f in range(8):
                    sp.wait_ge(parts_set, 8 * n + f + 1)
                    row = (n - c) * (H // 2) + (f % 4) * P
                    dst = qk_dram[f // 4, :, bass.ds(row, P), c * CHUNK:(c + 1) * CHUNK]
                    sp.dma_start(dst.rearrange("s r t -> r s t"), parts[:, f % STORE_RING]).then_inc(stored[f % STORE_RING], 16)

            def load_x(n):
                sp.wait_ge(tr_done, TPC * (n - 1))
                sp.dma_start(xin[:, n % 2], x[n * CHUNK:(n + 1) * CHUNK, :].rearrange("(j p) f -> p j f", p=P)
                             ).then_inc(x_in[n % 2], 16)

            load_x(2)
            store_parts(0, 0)
            load_x(3)
            for n in range(1, CHUNKS):
                store_parts(n, n % 2)
            for s in range(STORE_RING):
                sp.wait_ge(stored[s], 16 + 16 * 8 * CHUNKS // STORE_RING)

            def load(g, slot):
                for which, rows in ((0, Q_ROWS), (1, K_ROWS)):
                    for r, part in enumerate(rows):
                        sp.dma_start(stack[r * HD:(r + 1) * HD, slot, which, :].rearrange("d (j t) -> d j t", j=GH),
                                     qk_groups[which, part, g, :, :].rearrange("(j d) t -> d j t", j=GH)
                                     ).then_inc(loaded[slot], 16)

            def max_rows_in(bank, count, slot):
                sp.wait_ge(ring_free[bank], count + 1)
                for s in range(2):
                    sp.dma_start(stack[MAX_ROW + s:MAX_ROW + s + 1, slot, 0, :], max_rows[:, s, :]).then_inc(mx_in, 16)

            def ctx_store(g, half, bank, count):
                sp.wait_ge(ring_free[bank], count + 1)
                row = (g // GROUPS_B) * SEQ + half * HALF
                dst = ctx_dram[bass.ds(row, HALF), bass.ds((g % GROUPS_B) * GH * HD, GH * HD)]
                sp.dma_start(dst.rearrange("(t p) f -> p t f", p=P), ctx_n[:, half]).then_inc(ctx_out[half], 16)

            def step(g, slot, first=False, last=False):
                if not isinstance(g, int) or g + 2 < GROUPS:
                    if not first:
                        sp.wait_ge(st_done, EXPS * g)
                    load(g + 2, (slot + 2) % SLOTS)
                if not first:
                    ctx_store(g - 1, 1, *after(g, "ctx", 1))
                ctx_store(g, 0, *after(g, "ctx", 0))
                if not last:
                    max_rows_in(*after(g, "max", 0), (slot + 1) % SLOTS)

            sp.wait_ge(w_lo_set, KC)
            sp.wait_ge(stage_const, 2)
            load(0, 0)
            load(1, 1)
            bank, k = find(prologue, "max", 0)
            max_rows_in(bank, k + 1, 0)
            steps(sp, step)
            bank = 0
            ctx_store(GROUPS - 1, 1, bank, used(GROUPS - 1, bank) + uses(plan_z, bank) + 1)
            for half in range(2):
                sp.wait_ge(ctx_out[half], 16 + 16 * GROUPS)

        @block.gpsimd
        def _(pool):
            nc.gpsimd.memset(neg_half[:], -0.5).then_inc(neg_half_set, 1)
            nc.gpsimd.memset(v_stage[:], 0.0).then_inc(stage_const, 1)
            def rstds(n, c):
                pool.wait_ge(mv_set, TPC * (n + 1))
                nc.gpsimd.tensor_scalar(rstd[:, c, :], mv[:, c, :, 1], EPS, None, ALU.add).then_inc(var_eps, 1)
                pool.wait_ge(var_eps, n + 1)
                pool.wait_ge(neg_half_set, 1)
                nc.gpsimd.tensor_tensor(rstd[:, c, :], rstd[:, c, :], neg_half[:], ALU.pow).then_inc(rstd_set, 1)

            rstds(0, 0)
            rstds(1, 1)
            pool.wait_ge(amax_set, 1)
            nc.gpsimd.partition_all_reduce(amax[:, 1:2], amax[:, 0:1], P, RMAX).then_inc(amax_all, 1)
            rstds(2, 0)
            rstds(3, 1)

            v_view = v_all[:].rearrange("p (b t) (g j d) -> p b t g j d", b=BATCH, g=GROUPS_B, j=GH)

            def stage_v(g, par):
                nc.gpsimd.tensor_copy(v_stage[:, par, :, :, 0:HD],
                                      v_view[:, g // GROUPS_B, :, g % GROUPS_B, :, :]).then_inc(v_staged, 1)

            def fold(bank, count, gg, t, r):
                pool.wait_ge(ring_free[bank], count + 1)
                width, buf = SEQ // 2, shared[:, t % 2]
                for m in range(FOLDS):
                    done = (gg * len(SHARED_ROWS) + t) * FOLDS + m
                    if m:
                        pool.wait_ge(folded, done)
                    to = buf[:, 0:width] if m < FOLDS - 1 else max_part[:, 2 * r:2 * r + 2]
                    ins = nc.gpsimd.tensor_tensor(to, buf[:, 0:width], buf[:, width:2 * width], ALU.max)
                    ins.then_inc(folded, 1)
                    width //= 2
                pool.wait_ge(folded, done + 1)
                pool.sem_inc(shared_free, 1)

            def folds(plan, before, gg):
                for t, r in enumerate(SHARED_ROWS):
                    bank, k = find(plan, "scores", 2 * r + 1)
                    fold(bank, before(bank) + k + 1, gg, t, r)

            def step(g, slot, first=False, last=False):
                if last:
                    return
                if not first:
                    pool.wait_ge(pv_done, 4 + PAIRS * (g - 1))
                stage_v(g + 1, (slot + 1) % SLOTS)
                folds(plan_of(g), lambda bank: used(g, bank), g + 1)

            pool.wait_ge(v_free, 2 + TOKENS // P)
            pool.wait_ge(stage_const, 2)
            stage_v(0, 0)
            folds(prologue, lambda bank: 0, 0)
            steps(pool, step)

        @block.scalar
        def _(act):
            nc.scalar.dma_start(w_stage.rearrange("p (k n) -> p k n", k=KC), w_qkv.rearrange("(k p) n -> p k n", p=P)).then_inc(w_in, 16)
            act.wait_ge(w_in, 16)
            act.wait_ge(wscale_set, 2)
            for k in range(KC):
                nc.scalar.activation(w_hi[:, k, :], w_stage[:, k * 3 * H:(k + 1) * 3 * H], ACT.Copy,
                                     scale=wscale[:, 0:1]).then_inc(w_hi_set, 1)
            act.wait_ge(consts_in, 48)

            def project(n, c):
                for j in range(TPC):
                    act.wait_ge(tr_done, TPC * n + j + 1)
                    nc.scalar.activation(z_hi[:, c, :, j * P:(j + 1) * P],
                                         ps_tr[j % 2][:].rearrange("p (k t) -> p k t", k=KC), ACT.Copy,
                                         scale=Z_SCALE).then_inc(z_hi_set, 1)
                for f in range(8):
                    act.wait_ge(qk_done, 8 * n + f + 1)
                    act.wait_ge(stored[f % STORE_RING], 16 * (2 * n + f // STORE_RING + 1))
                    nc.scalar.activation(y[:, f % STORE_RING], ps_qk[f % 4], ACT.Identity,
                                         bias=bqk[:, f:f + 1], scale=wscale[:, 1:2])
                    nc.scalar.activation(parts[:, f % STORE_RING, 0], ps_qk[f % 4], ACT.Identity,
                                         bias=bqk[:, f:f + 1], scale=wscale[:, 1:2]).then_inc(qk_free, 1)

            with act.Fori(0, BATCH) as i:
                for c in range(2):
                    project(2 * i + c, c)

            def share(w, bank, count, gg):
                t = SHARED_ROWS.index(w // 2)
                act.wait_ge(ring_done[bank], count)
                if w % 2 == 0:
                    act.wait_ge(shared_free, gg * len(SHARED_ROWS) + t + 1)
                at = (w % 2) * (SEQ // 2)
                nc.scalar.copy(shared[:, t % 2, at:at + SEQ // 2], ps_r[bank][:]).then_inc(ring_free[bank], 1)

            def shares(plan, before, gg, u):
                for at, what, w, bank, k in plan:
                    if at == u and what == "scores" and w // 2 in SHARED_ROWS:
                        share(w, bank, before(bank) + k + 1, gg)

            def take_ctx(g, half):
                act.wait_ge(pv_done, 4 + PAIRS * g + KT * (half + 1))
                if half or not isinstance(g, int) or g:
                    act.wait_ge(rsum_set, 2 * g + half)
                nc.scalar.copy(ctx_t[:], ps_c[:]).then_inc(pv_free, 1)

            def step(g, slot, first=False, last=False):
                for u in range(EXPS):
                    act.wait_ge(st_done, EXPS * g + (u + 1))
                    if u % 2 == 0:
                        act.wait_ge(pv_done, PAIRS * g + (u // 2 + 1))
                    nc.scalar.activation(probs[:, u % PROBS], ps_s[u % 2][:], ACT.Exp,
                                         scale=SOFTMAX_SCALE).then_inc(exp_done, 1)
                    if u == PAIR_LAG - 1 and not first:
                        take_ctx(g - 1, 1)
                    if u == PAIR_LAG - 1 + 2 * KT:
                        take_ctx(g, 0)
                    shares(plan_of(g), lambda bank: used(g, bank), g + 1, u)

            shares(prologue, lambda bank: 0, 0, 0)
            steps(act, step)
            take_ctx(GROUPS - 1, 1)

        @block.vector
        def _(dve):
            for credits, count in ((tr_free, 2), (v_free, 2), (qk_free, 4), (exp_done, 2), (pv_done, 4),
                                   (pv_free, 1), (shared_free, 2), *((s, 1) for s in ring_free), *((s, 16) for s in stored), *((s, 16) for s in ctx_out)):
                dve.sem_inc(credits, count)

            def norm_in(n, c):
                dve.wait_ge(x_in[c], 16 * (n // 2 + 1))
                for j in range(TPC):
                    nc.vector.bn_stats(stats[:, c, j, :], xin[:, c, j, :]).then_inc(stats_set, 1)
                dve.wait_ge(stats_set, TPC * (n + 1))
                for j in range(TPC):
                    nc.vector.bn_aggr(mv[:, c, j, :], stats[:, c, j, :]).then_inc(mv_set, 1)
                dve.wait_ge(rstd_set, n + 1)
                for j in range(TPC):
                    nc.vector.tensor_scalar(xin[:, c, j, :], xin[:, c, j, :], mv[:, c, j, 0:1], rstd[:, c, j:j + 1],
                                            ALU.subtract, ALU.mult).then_inc(z_set, 1)

            def split_weights():
                dve.wait_ge(w_in, 16)
                nc.vector.tensor_reduce(amax[:, 0:1], w_stage, AX_X, ALU.max,
                                        apply_absolute_value=True).then_inc(amax_set, 1)
                dve.wait_ge(amax_all, 1)
                nc.vector.tensor_scalar(amax[:, 1:2], amax[:, 1:2], TINY, None, ALU.max).then_inc(exp_set, 1)
                dve.wait_ge(exp_set, 1)
                nc.vector.tensor_single_scalar(amax[:, 2:3].bitcast(I32), amax[:, 1:2].bitcast(I32), EXP_MASK,
                                               ALU.bitwise_and).then_inc(exp_set, 1)
                dve.wait_ge(exp_set, 2)
                nc.vector.tensor_scalar(wscale[:, 0:1].bitcast(I32), amax[:, 2:3].bitcast(I32), -1.0,
                                        SCALE_FROM_EXP, ALU.mult, ALU.add).then_inc(wscale_set, 1)
                nc.vector.tensor_scalar(wscale[:, 1:2].bitcast(I32), amax[:, 2:3].bitcast(I32), INV_FROM_EXP,
                                        None, ALU.add).then_inc(wscale_set, 1)
                dve.wait_ge(wscale_set, 2)
                for k in range(KC):
                    dve.wait_ge(w_hi_set, k + 1)
                    nc.vector.scalar_tensor_tensor(out=w_lo[:, k, :], in0=w_stage[:, k * 3 * H:(k + 1) * 3 * H],
                                                   scalar=wscale[:, 0:1], in1=w_hi[:, k, :], op0=ALU.mult,
                                                   op1=ALU.subtract).then_inc(w_lo_set, 1)

            def project(n, c):
                for j in range(TPC):
                    dve.wait_ge(z_hi_set, TPC * n + j + 1)
                    nc.vector.scalar_tensor_tensor(
                        out=z_lo[:, c, :, j * P:(j + 1) * P], in0=ps_tr[j % 2][:].rearrange("p (k t) -> p k t", k=KC),
                        scalar=Z_SCALE, in1=z_hi[:, c, :, j * P:(j + 1) * P], op0=ALU.mult,
                        op1=ALU.subtract).then_inc(tr_free, 1)
                for j in range(TPC):
                    dve.wait_ge(v_done, TPC * n + j + 1)
                    nc.vector.scalar_tensor_tensor(out=v_all[:, TPC * n + j, :], in0=ps_vp[j % 2][:],
                                                   scalar=wscale[:, 1:2], in1=bv[:], op0=ALU.mult,
                                                   op1=ALU.add).then_inc(v_free, 1)
                for f in range(8):
                    s = f % STORE_RING
                    dve.wait_ge(qk_free, 4 + 8 * n + f + 1)
                    nc.vector.tensor_tensor(y[:, s], y[:, s], parts[:, s, 0], ALU.subtract).then_inc(part_step, 1)
                    dve.wait_ge(part_step, 2 * (8 * n + f) + 1)
                    nc.vector.tensor_copy(parts[:, s, 1], y[:, s]).then_inc(part_step, 1)
                    dve.wait_ge(part_step, 2 * (8 * n + f) + 2)
                    nc.vector.tensor_tensor(parts[:, s, 2], y[:, s], parts[:, s, 1], ALU.subtract).then_inc(parts_set, 1)

            norm_in(0, 0)
            norm_in(1, 1)
            split_weights()
            dve.wait_ge(consts_in, 48)
            project(0, 0)
            norm_in(2, 0)
            project(1, 1)
            norm_in(3, 1)
            project(2, 0)
            project(3, 1)
            for s in range(SLOTS):
                nc.vector.memset(stack[MAX_ROW:ROWS, s, 1, :], 1.0)
            dve.wait_ge(stage_const, 1)
            nc.vector.memset(v_stage[:, :, :, :, HD:HD + 1], 1.0).then_inc(stage_const, 1)

            def reduce_max(w, bank, count):
                dve.wait_ge(ring_done[bank], count)
                nc.vector.tensor_reduce(max_part[:, w:w + 1], ps_r[bank][:], AX_X, ALU.max).then_inc(ring_free[bank], 1)

            def join_max(gg, bank, count):
                dve.wait_ge(shared_free, 2 + len(SHARED_ROWS) * (gg + 1))
                dve.wait_ge(ring_free[bank], count + 1)
                nc.vector.tensor_reduce(maxes[:], max_part[:].rearrange("p (t h) -> p t h", h=2), AX_X,
                                        ALU.max).then_inc(mx_set, 1)

            def split_max(gg, bank, count):
                dve.wait_ge(ring_done[bank], count)
                if not (isinstance(gg, int) and gg == 0):
                    dve.wait_ge(mx_in, 32 * gg)
                turned = ps_r[bank][0:GH * KT, 0:P]
                nc.vector.tensor_scalar(max_rows[:, 0, :], turned, -1.0, None, ALU.mult).then_inc(mx_step, 1)
                dve.wait_ge(mx_step, gg + 1)
                nc.vector.scalar_tensor_tensor(out=max_rows[:, 1, :], in0=turned, scalar=-1.0, in1=max_rows[:, 0, :],
                                               op0=ALU.mult, op1=ALU.subtract).then_inc(ring_free[bank], 1)

            def normalise(g, half, bank, count):
                view = ps_r[bank][:].rearrange("p (t j c) -> p (t j) c", t=4, j=GH)
                dve.wait_ge(ring_done[bank], count)
                nc.vector.reciprocal(rsum[:, half], view[:, :, HD]).then_inc(rsum_set, 1)
                dve.wait_ge(rsum_set, 2 * g + half + 1)
                dve.wait_ge(ctx_out[half], 16 * (g + 1))
                nc.vector.tensor_tensor(ctx_n[:, half].rearrange("p t (j d) -> p (t j) d", j=GH), view[:, :, 0:HD],
                                        rsum[:, half].unsqueeze(2).to_broadcast([P, 4 * GH, HD]),
                                        ALU.mult).then_inc(ring_free[bank], 1)

            last_w = max(w for w in range(MAX_MM) if w // 2 not in SHARED_ROWS)

            def step(g, slot, first=False, last=False):
                due = [(u + (what != "scores"), what, which, bank, k) for u, what, which, bank, k in plan_of(g)]
                for u in range(EXPS + 1):
                    for _, what, which, bank, k in sorted((d for d in due if d[0] == u), key=lambda d: d[1] == "scores"):
                        count = used(g, bank) + (k + 1)
                        if what == "scores" and which // 2 not in SHARED_ROWS:
                            reduce_max(which, bank, count)
                        if what == "max":
                            split_max(g + 1, bank, count)
                        if what == "ctx":
                            normalise(g - which, which, bank, count)
                    if u == MAX_BY - 1 and not last:
                        bank, k = find(plan_of(g), "scores", last_w)
                        join_max(g + 1, bank, used(g, bank) + (k + 1))

            for _, what, w, bank, k in prologue:
                if what == "scores" and w // 2 not in SHARED_ROWS:
                    reduce_max(w, bank, k + 1)
            bank, k = find(prologue, "scores", last_w)
            join_max(0, bank, k + 1)
            bank, k = find(prologue, "max", 0)
            split_max(0, bank, k + 1)
            steps(dve, step)
            normalise(GROUPS - 1, 1, 0, used(GROUPS - 1, 0) + uses(plan_z, 0) + 1)

        @block.tensor
        def _(pe):
            pe.wait_ge(consts_in, 48)

            def transposes(n, c):
                for j in range(TPC):
                    pe.wait_ge(z_set, TPC * n + j + 1)
                    pe.wait_ge(tr_free, TPC * n + j + 1)
                    for k in range(KC):
                        tr = nc.tensor.transpose(ps_tr[j % 2][:, k * P:(k + 1) * P], xin[:, c, j, k * P:(k + 1) * P], ident[:])
                    tr.then_inc(tr_done, 1)

            def project(n, c):
                transposes(n, c)
                pe.wait_ge(tr_free, 2 + TPC * (n + 1))
                pe.wait_ge(w_lo_set, KC)
                for j in range(TPC):
                    pe.wait_ge(v_free, TPC * n + j + 1)
                    t = slice(j * P, (j + 1) * P)
                    passes = [(z_hi, w_hi), (z_hi, w_lo), (z_lo, w_hi)]
                    for m, (a, w) in enumerate(passes):
                        for k in range(KC):
                            mm = nc.tensor.matmul(ps_vp[j % 2][:], a[:, c, k, t], w[:, k, 2 * H:3 * H],
                                                  start=(m == 0 and k == 0), stop=(m == 2 and k == KC - 1))
                    mm.then_inc(v_done, 1)
                for f in range(8):
                    pe.wait_ge(qk_free, 8 * n + f + 1)
                    passes = [(w_hi, z_hi), (w_hi, z_lo), (w_lo, z_hi)]
                    for m, (w, a) in enumerate(passes):
                        for k in range(KC):
                            mm = nc.tensor.matmul(ps_qk[f % 4], w[:, k, f * P:(f + 1) * P], a[:, c, k, :],
                                                  start=(m == 0 and k == 0), stop=(m == 2 and k == KC - 1))
                    mm.then_inc(qk_done, 1)

            with pe.Fori(0, BATCH) as i:
                for c in range(2):
                    project(2 * i + c, c)

            def max_tile(slot, w, bank, count):
                j, qt, kh = w // (2 * KT), w // 2 % KT, w % 2
                pe.wait_ge(ring_free[bank], count)
                nc.tensor.matmul(ps_r[bank][:], stack[0:STACK, slot, 0, j * SEQ + qt * P:j * SEQ + (qt + 1) * P],
                                 stack[0:STACK, slot, 1, j * SEQ + kh * HALF:j * SEQ + (kh + 1) * HALF],
                                 start=True, stop=True).then_inc(ring_done[bank], 1)

            def turn_max(gg, bank, count):
                pe.wait_ge(mx_set, gg + 1)
                pe.wait_ge(ring_free[bank], count)
                nc.tensor.transpose(ps_r[bank][0:GH * KT, 0:P], maxes[:], ident[:]).then_inc(ring_done[bank], 1)

            def turn_ctx(g, half, bank, count):
                pe.wait_ge(pv_free, 1 + 2 * g + half + 1)
                pe.wait_ge(ring_free[bank], count)
                for t in range(4):
                    tr = nc.tensor.transpose(ps_r[bank][:, t * P:(t + 1) * P], ctx_t[:, t * P:(t + 1) * P], ident[:])
                tr.then_inc(ring_done[bank], 1)

            def scores(g, slot, u):
                half, kt, hp = u // (2 * KT), u // 2 % KT, u % 2
                pe.wait_ge(exp_done, EXPS * g + (u + 1))
                for e in range(2):
                    j = 2 * hp + e
                    mm = nc.tensor.matmul(ps_s[u % 2][:, e * HALF:(e + 1) * HALF],
                                          stack[0:ROWS, slot, 1, j * SEQ + kt * P:j * SEQ + (kt + 1) * P],
                                          stack[0:ROWS, slot, 0, j * SEQ + half * HALF:j * SEQ + (half + 1) * HALF],
                                          start=True, stop=True)
                mm.then_inc(st_done, 1)

            def times_v(g, slot, pair):
                half, kt = pair // KT, pair % KT
                pe.wait_ge(exp_done, EXPS * g + (2 * pair + 4))
                if pair == 0:
                    pe.wait_ge(v_staged, g + 1)
                if kt == 0:
                    pe.wait_ge(pv_free, 2 * g + half + 1)
                for j in range(GH):
                    mm = nc.tensor.matmul(ps_c[32 * j:32 * j + 32, :], v_stage[:, slot, kt, j, :],
                                          probs[:, (2 * pair + j // 2) % PROBS, (j % 2) * HALF:(j % 2 + 1) * HALF],
                                          start=(kt == 0), stop=(kt == KT - 1), skip_group_check=True)
                mm.then_inc(pv_done, 1)

            def step(g, slot, first=False, last=False):
                pe.wait_ge(mx_in, 32 * (g + 1))
                if not last:
                    nxt = (slot + 1) % SLOTS
                    pe.wait_ge(loaded[nxt], 192 * loads_by(g + 1, nxt))
                for u in range(EXPS):
                    scores(g, slot, u)
                    for at, what, which, bank, k in plan_of(g):
                        count = used(g, bank) + (k + 1)
                        if at == u and what == "scores":
                            max_tile(nxt, which, bank, count)
                        if at == u and what == "max":
                            turn_max(g + 1, bank, count)
                    if (found := pair_at(u)) is not None:
                        before, pair = found
                        if not before:
                            times_v(g, slot, pair)
                        elif not first:
                            times_v(g - 1, (slot - 1) % SLOTS, pair)
                    for at, what, half, bank, k in plan_of(g):
                        if at == u and what == "ctx":
                            turn_ctx(g - half, half, bank, used(g, bank) + (k + 1))

            def loads_by(g, slot):
                return (g - slot) // SLOTS + 1

            pe.wait_ge(tr_free, 2 + TOKENS // P)
            pe.wait_ge(v_free, 2 + TOKENS // P)
            pe.wait_ge(qk_free, 4 + 8 * CHUNKS)
            pe.wait_ge(loaded[0], 192)
            pe.wait_ge(stage_const, 2)
            for _, what, w, bank, k in prologue:
                if what == "scores":
                    max_tile(0, w, bank, k + 1)
                else:
                    turn_max(0, bank, k + 1)
            steps(pe, step)
            for pair in (PAIRS - 2, PAIRS - 1):
                times_v(GROUPS - 1, 0, pair)
            turn_ctx(GROUPS - 1, 1, 0, used(GROUPS - 1, 0) + uses(plan_z, 0) + 1)


def layers_block(nc, x, ctx_dram, w_o, b_o, w_0, b_0, w_gu, point, w_terms, discount, w_g, w_u, w_d, w_ra, w_b,
                 ident_dram, out):
    F = w_g.shape[1]
    FB = -(-F // P)
    F_LAST = F - (FB - 1) * P
    S = w_gu.shape[1] // 2
    G = w_terms.shape[1] - 1
    TERMS = G + 1
    GRAD_ORDER_MIN, THD = 4, 2.5
    RA = w_ra.shape[1]
    E = 4
    R = (RA - E) // E
    LORA_SCALE = 4.0
    CTX_BITS = 4
    O_, F0, L1, L3 = range(4)
    ROUTE_EXP, ROUTE_STEPS = 9, 20
    T_COLS, H_COLS = TERMS * CHUNK, FB * CHUNK
    assert S == P

    with ExitStack() as ctx:
        def sb(name, shape, dt):
            return ctx.enter_context(nc.sbuf_tensor(name, shape, dt))

        def psum(name, shape, dt=F32):
            return ctx.enter_context(nc.psum_tensor(name, shape, dt))

        def sem(name):
            return ctx.enter_context(nc.semaphore(name))

        xs = sb("xs", [P, TOKENS // P, H], F32)
        zf = sb("zf", [P, TPC, H], F32)
        z_hi = sb("zz_hi", [P, 2, KC, CHUNK], F16)
        z_lo = sb("zz_lo", [P, 2, KC, CHUNK], F16)
        y = sb("yy", [P, TPC, H], F32)
        work = sb("work", [P, T_COLS + H_COLS], F32)
        terms = work[:, 0:T_COLS].rearrange("p (m t) -> p m t", m=TERMS)
        hidden = work[:, T_COLS:T_COLS + H_COLS].rearrange("p (f t) -> p f t", f=FB)
        wd = sb("wd", [P, FB, H], F32)
        wt = sb("wt", [P, TERMS, H], F32)
        wb = sb("wb", [P, H], F32)
        wdims = {"o": H, "0": H, "gu": 2 * S, "g": F, "ra": RA, "u": F}
        names = list(wdims)
        hi = {k: sb(f"hi_{k}", [P, KC, n], F16) for k, n in wdims.items()}
        lo = {k: sb(f"lo_{k}", [P, KC, n], F16) for k, n in wdims.items()}
        w_amax = sb("w_amax", [P, len(names), 3], F32)
        w_scale = sb("w_scale", [P, len(names), 2], F32)
        bo = sb("bo", [P, H], F32)
        b0 = sb("b0", [P, H], F32)
        lp = sb("lp", [P, 1], F32)
        disc = sb("disc", [P, G], F32)
        ident = sb("ident2", [P, P], F32)
        ones = sb("ones", [P, P], F32)
        half = sb("half", [P, TPC], F32)
        eps = sb("eps", [P, TPC], F32)
        turn = sb("turn", [P, 1], F32)
        st_x = sb("st_x", [P, TPC, 6], F32)
        mv_x = sb("mv_x", [P, TPC, 2], F32)
        rs_x = sb("rs_x", [P, TPC], F32)
        st_y = sb("st_y", [P, TPC, 6], F32)
        mv_y = sb("mv_y", [P, TPC, 2], F32)
        rs_y = sb("rs_y", [P, TPC], F32)
        c_amax = sb("c_amax", [P, TPC], F32)
        c_exp = sb("c_exp", [P, TPC], F32)
        c_scale = sb("c_scale", [P, TPC], F32)
        c_inv = sb("c_inv", [P, 2, TPC], F32)
        delta, kept = hidden[:, FB - 1, :], hidden[:, FB - 2, :]
        sg = sb("sg", [P, 2, CHUNK], F32)
        lm = work[:, 0:TPC * RA].rearrange("p (j r) -> p j r", j=TPC)
        gt = sb("gt", [P, 6, TPC], F32)
        rank = sb("rank", [P, TPC, E], F32)
        top = sb("top", [P, TPC], F32)
        gates = sb("gates", [P, TPC, E], F32)
        gm = sb("gm", [P, TPC, P], F32)
        gmt = work[:, T_COLS:T_COLS + TPC * P].rearrange("p (j t) -> p j t", j=TPC)

        ps_t = [psum(f"ps_t{i}", [P, 512]) for i in range(2)]
        ps_y = [psum(f"ps_y{i}", [P, 512]) for i in range(2)]
        ps_p = [psum(f"ps_p{i}", [P, 512]) for i in range(4)]

        w_in = {k: sem(f"w_in_{k}") for k in names}
        c_in = sem("c_in")
        wt_in, wd_in = sem("wt_in"), sem("wd_in")
        xs_in = sem("xs_in")
        cx_in = [sem(f"cx_in{c}") for c in range(2)]
        mem = sem("mem")
        absd = sem("absd")
        colsum = sem("colsum")
        signed = sem("signed")
        tern = sem("tern")
        quant = sem("quant")
        wa = sem("wa")
        wr = sem("wr")
        we = sem("we")
        ws = sem("ws")
        whi = {k: sem(f"whi_{k}") for k in names}
        w_split = {k: sem(f"w_split_{k}") for k in names}
        wsc = sem("wsc")
        disc_e = sem("disc_e")
        wt_set = sem("wt_set")
        sx, ax, vx, rx = sem("sx"), sem("ax"), sem("vx"), sem("rx")
        z_set = sem("zf_set")
        t_done = sem("t_done")
        zh_set = sem("zh_set")
        t_free = sem("t_free")
        y_done = sem("y_done")
        y_free = sem("y_free")
        sy, ay, vy, ry = sem("sy"), sem("ay"), sem("vy"), sem("ry")
        yn = sem("yn")
        x_set = sem("x_set")
        cs = sem("cs")
        gu_done = sem("gu_done")
        dl = sem("dl")
        p_done = sem("p_done")
        sg_set = sem("sg_set")
        h_set = sem("h_set")
        r_done = sem("r_done")
        rt = sem("rt")
        ex = sem("ex")
        gm_set = sem("gm_set")
        gt_done = sem("gt_done")
        gt_set = sem("gt_set")
        stored = sem("out_stored")
        block = ctx.enter_context(nc.Block())

        narrow, wide = ["o", "0", "gu", "ra"], ["g", "u"]
        stage_at, at = {}, 0
        for k in ("gu", "ra", "o", "0"):
            stage_at[k] = at
            at += KC * wdims[k]
        stage_at["u"] = stage_at["o"]
        context_at = T_COLS + H_COLS - TPC * H
        assert max(at, stage_at["u"] + KC * F) <= context_at
        chunk_in = [zf, work[:, context_at:].rearrange("p (j f) -> p j f", j=TPC)]
        wd_flat = wd[:].rearrange("p f n -> p (f n)")

        def staged(k):
            if k == "g":
                return wd_flat[:, 0:KC * F]
            return work[:, stage_at[k]:stage_at[k] + KC * wdims[k]]

        def kpn(w):
            return w.rearrange("(k p) n -> p k n", p=P)

        split_after = {0: ["0", "gu"], 1: ["g", "ra"], 2: ["u"], 3: []}
        t_a, t_b = wd_flat[:, 0:KC * H], wd_flat[:, KC * H:2 * KC * H]
        inv = {k: w_scale[:, names.index(k), 1:2] for k in names}

        assert KC == CHUNKS == 4

        def wide_blocks(layer, n):
            if layer == O_ and n >= 2:
                return [("g", 2 * n - 4), ("g", 2 * n - 3)]
            return [("u", n)] if layer == F0 else []

        def block_of(k, n):
            one = lambda ap: ap[:, n, :] if isinstance(n, int) else ap[:, bass.ds(n, 1), :].rearrange("p a f -> p (a f)")
            return one(staged(k).rearrange("p (k n) -> p k n", k=KC)), one(hi[k]), one(lo[k])

        def x_tile(n, j):
            if isinstance(n, int):
                return xs[:, TPC * n + j, :]
            return xs[:, bass.ds(TPC * n + j, 1), :].rearrange("p a f -> p (a f)")

        def has_stage(ahead, layer, n):
            return layer != L3 or n + ahead < CHUNKS

        def layer_loops(engine, stage, scale_weight=lambda k: None, before=lambda layer: None):
            before(O_)
            for n in range(CHUNKS):
                stage(n, O_, n, n % 2)
                for k in split_after[n]:
                    scale_weight(k)
            for layer in (F0, L1):
                before(layer)
                with engine.Fori(0, CHUNKS // 2) as i:
                    for c in range(2):
                        stage(CHUNKS * layer + c + 2 * i, layer, 2 * i + c, c)
            before(L3)
            for n in range(CHUNKS):
                stage(CHUNKS * L3 + n, L3, n, n % 2)

        @block.sync
        def _(sp):
            def load_context(n):
                if n >= 2:
                    sp.wait_ge(t_done, TPC * (n - 1))
                sp.dma_start(chunk_in[n % 2][:], ctx_dram[n * CHUNK:(n + 1) * CHUNK, :].rearrange("(j p) f -> p j f", p=P)
                             ).then_inc(cx_in[n % 2], 16)

            load_context(0)
            for dst, src in ((ident[:], ident_dram), (bo[:], b_o.to_broadcast([P, H])), (b0[:], b_0.to_broadcast([P, H])),
                             (lp[:], point), (disc[:], discount.to_broadcast([P, G]))):
                sp.dma_start(dst, src).then_inc(c_in, 16)
            sp.dma_start(xs[:], x.rearrange("(j p) f -> p j f", p=P)).then_inc(xs_in, 16)

            load_context(1)
            sp.wait_ge(quant, 3)
            sp.dma_start(staged("g").rearrange("p (k n) -> p k n", k=KC), kpn(w_g)).then_inc(w_in["g"], 16)
            load_context(2)
            for k in ("o", "0"):
                sp.wait_ge(w_split[k], 1)
            sp.dma_start(staged("u").rearrange("p (k n) -> p k n", k=KC), kpn(w_u)).then_inc(w_in["u"], 16)
            load_context(3)
            sp.wait_ge(w_split["g"], KC)
            sp.dma_start(wd[:, 0:FB - 1, :], w_d[0:(FB - 1) * P, :].rearrange("(f p) n -> p f n", p=P)
                         ).then_inc(wd_in, 16)
            sp.dma_start(wd[0:F_LAST, FB - 1, :], w_d[(FB - 1) * P:F, :]).then_inc(wd_in, 16)
            sp.wait_ge(mem, 5)
            for n in range(CHUNKS):
                sp.wait_ge(x_set, TPC * (CHUNKS * L3 + n + 1))
                sp.dma_start(out[n * CHUNK:(n + 1) * CHUNK, :].rearrange("(j p) f -> p j f", p=P),
                             xs[:, n * TPC:(n + 1) * TPC, :]).then_inc(stored, 16)
            sp.wait_ge(stored, 16 * CHUNKS)

        @block.gpsimd
        def _(pool):
            nc.gpsimd.memset(half[:], -0.5).then_inc(mem, 1)
            nc.gpsimd.memset(eps[:], EPS).then_inc(mem, 1)
            nc.gpsimd.memset(ones[:], 1.0).then_inc(mem, 1)
            nc.gpsimd.memset(gm[:], 0.0).then_inc(mem, 1)
            nc.gpsimd.memset(wb[:], 0.0).then_inc(mem, 1)
            for k, w in (("gu", w_gu), ("ra", w_ra)):
                nc.gpsimd.dma_start(staged(k).rearrange("p (k n) -> p k n", k=KC), kpn(w)).then_inc(w_in[k], 16)
            nc.gpsimd.dma_start(wt[:], w_terms).then_inc(wt_in, 16)
            pool.wait_ge(mem, 5)
            nc.gpsimd.dma_start(wb[0:E * R, :], w_b).then_inc(wt_in, 16)

            def scale_weight(k):
                a = w_amax[:, names.index(k)]
                pool.wait_ge(wa, names.index(k) + 1)
                nc.gpsimd.partition_all_reduce(a[:, 1:2], a[:, 0:1], P, RMAX).then_inc(wr, 1)

            scale_weight("o")
            pool.wait_ge(signed, 1)
            pool.wait_ge(tern, 2)
            nc.gpsimd.tensor_tensor(t_a, t_a, t_b, ALU.mult).then_inc(quant, 1)
            pool.wait_ge(quant, 1)
            nc.gpsimd.tensor_tensor(t_a, t_a, staged("0"), ALU.subtract).then_inc(quant, 1)
            pool.wait_ge(quant, 2)
            nc.gpsimd.tensor_tensor(staged("0"), staged("0"), t_a, ALU.add).then_inc(quant, 1)

            def split_block(k, block):
                scaled, high, low = block_of(k, block)
                pool.wait_ge(wsc, block + 1 + (KC if k == "u" else 0))
                nc.gpsimd.tensor_tensor(low, scaled, high, ALU.subtract).then_inc(w_split[k], 1)

            def inv_std(seen, mv, rs, steps, done, means):
                pool.wait_ge(means, TPC * (seen + 1))
                nc.gpsimd.tensor_tensor(rs[:], mv[:, :, 1], eps[:], ALU.add).then_inc(steps, 1)
                pool.wait_ge(steps, seen + 1)
                nc.gpsimd.tensor_tensor(rs[:], rs[:], half[:], ALU.pow).then_inc(done, 1)

            def stage(s, layer, n, c):
                blocks = wide_blocks(layer, n)
                for k, block in blocks[0:1]:
                    split_block(k, block)
                inv_std(s, mv_y, rs_y, vy, ry, ay)
                if has_stage(3, layer, n) and not (layer == O_ and n == 0):
                    inv_std(s + 3 - CHUNKS, mv_x, rs_x, vx, rx, ax)
                for j in range(TPC):
                    pool.wait_ge(yn, TPC * s + (j + 1))
                    nc.gpsimd.tensor_tensor(x_tile(n, j), x_tile(n, j), y[:, j, :], ALU.add).then_inc(x_set, 1)
                for k, block in blocks[1:]:
                    split_block(k, block)

            pool.wait_ge(xs_in, 16)
            layer_loops(pool, stage, scale_weight)

        @block.scalar
        def _(act):
            for k, w in (("o", w_o), ("0", w_0)):
                nc.scalar.dma_start(staged(k).rearrange("p (k n) -> p k n", k=KC), kpn(w)).then_inc(w_in[k], 16)

            def scale_weight(k):
                if k in narrow:
                    act.wait_ge(ws, 2 * (names.index(k) + 1))
                    nc.scalar.activation(hi[k][:].rearrange("p k n -> p (k n)"), staged(k), ACT.Copy,
                                         scale=w_scale[:, names.index(k), 0:1]).then_inc(whi[k], 1)

            scale_weight("o")
            act.wait_ge(w_in["0"], 16)
            nc.scalar.activation(t_a, staged("0"), ACT.Abs).then_inc(absd, 1)
            nc.scalar.activation(t_b, staged("0"), ACT.Sign).then_inc(signed, 1)
            def high_part(s, c, j):
                act.wait_ge(t_done, TPC * s + (j + 1))
                nc.scalar.activation(z_hi[:, c, :, j * P:(j + 1) * P],
                                     ps_t[j % 2][:].rearrange("p (k t) -> p k t", k=KC), ACT.Copy,
                                     scale=Z_SCALE).then_inc(zh_set, 1)

            def copy_out(s, j):
                act.wait_ge(y_done, TPC * s + (j + 1))
                act.wait_ge(x_set, TPC * s - 3 + j)
                nc.scalar.copy(y[:, j, :], ps_y[j % 2][:]).then_inc(y_free, 1)

            def stage(s, layer, n, c):
                if layer == L1:
                    for f in range(FB):
                        rows = P if f < FB - 1 else F_LAST
                        k = (s - CHUNKS * L1) * FB + f
                        act.wait_ge(p_done, 2 * k + 1)
                        act.wait_ge(h_set, k + 1)
                        nc.scalar.activation(sg[0:rows, f % 2, :], ps_p[2 * (f % 2)][0:rows, :], ACT.Silu,
                                             scale=inv["g"][0:rows, :]).then_inc(sg_set, 1)
                if layer == L3:
                    act.wait_ge(rt, ROUTE_STEPS * n + ROUTE_EXP)
                    nc.scalar.activation(gates[:], gates[:], ACT.Exp).then_inc(ex, 1)
                    for j in range(TPC):
                        act.wait_ge(gt_done, TPC * n + j + 1)
                        nc.scalar.copy(gmt[:, j, :], ps_p[1 + j % 2][:, 0:P]).then_inc(gt_set, 1)
                for pair in ((0, 1), (2, 3)):
                    for j in pair:
                        if has_stage(1, layer, n):
                            high_part(s + 1, 1 - c, j)
                        if layer == L1:
                            copy_out(s, j)
                    for j in pair if layer == L3 else ():
                        copy_out(s, j)
                    for k, block in wide_blocks(layer, n)[pair[0] // 2:pair[0] // 2 + 1]:
                        scaled, high, _ = block_of(k, block)
                        scale = w_scale[:, names.index(k), 0:1]
                        act.wait_ge(ws, 2 * (names.index(k) + 1))
                        nc.scalar.activation(high, scaled, ACT.Copy, scale=scale).then_inc(whi[k], 1)
                        nc.scalar.activation(scaled, scaled, ACT.Copy, scale=scale).then_inc(wsc, 1)

            def before(layer):
                if layer == L1:
                    act.wait_ge(c_in, 80)
                    nc.scalar.activation(disc[:], disc[:], ACT.Exp, scale=-1.0).then_inc(disc_e, 1)
                    act.wait_ge(disc_e, 1)
                    act.wait_ge(wt_in, 32)
                    for m in range(G):
                        nc.scalar.activation(wt[:, m + 1, :], wt[:, m + 1, :], ACT.Copy, scale=disc[:, m:m + 1]).then_inc(wt_set, 1)

            for j in range(TPC):
                high_part(0, 0, j)
            layer_loops(act, stage, scale_weight, before)

        @block.vector
        def _(dve):
            for credits, count in ((t_free, 2), (y_free, 2), (h_set, 2)):
                dve.sem_inc(credits, count)

            def split(k):
                m = names.index(k)
                a, sc = w_amax[:, names.index(k)], w_scale[:, names.index(k)]
                if k == "0":
                    dve.wait_ge(quant, 3)
                dve.wait_ge(w_in[k], 16)
                nc.vector.tensor_reduce(a[:, 0:1], staged(k), AX_X, ALU.max, apply_absolute_value=True).then_inc(wa, 1)
                dve.wait_ge(wr, m + 1)
                nc.vector.tensor_scalar(a[:, 1:2], a[:, 1:2], TINY, None, ALU.max).then_inc(we, 1)
                dve.wait_ge(we, 2 * m + 1)
                nc.vector.tensor_single_scalar(a[:, 2:3].bitcast(I32), a[:, 1:2].bitcast(I32), EXP_MASK,
                                               ALU.bitwise_and).then_inc(we, 1)
                dve.wait_ge(we, 2 * m + 2)
                nc.vector.tensor_scalar(sc[:, 0:1].bitcast(I32), a[:, 2:3].bitcast(I32), -1.0, SCALE_FROM_EXP,
                                        ALU.mult, ALU.add).then_inc(ws, 1)
                nc.vector.tensor_scalar(sc[:, 1:2].bitcast(I32), a[:, 2:3].bitcast(I32), INV_FROM_EXP, None,
                                        ALU.add).then_inc(ws, 1)
                dve.wait_ge(ws, 2 * m + 2)
                if k in narrow:
                    dve.wait_ge(whi[k], 1)
                    nc.vector.scalar_tensor_tensor(out=lo[k][:].rearrange("p k n -> p (k n)"), in0=staged(k),
                                                   scalar=sc[:, 0:1], in1=hi[k][:].rearrange("p k n -> p (k n)"),
                                                   op0=ALU.mult, op1=ALU.subtract).then_inc(w_split[k], 1)

            def ternary():
                k3 = t_a.rearrange("p (k n) -> p k n", k=KC)
                dve.wait_ge(colsum, 1)
                nc.vector.tensor_scalar(sg[:, 0, :], ps_y[0][:], 1.0 / H, 0.7, ALU.mult, ALU.mult).then_inc(tern, 1)
                dve.wait_ge(tern, 1)
                nc.vector.tensor_tensor(k3, k3, sg[:, 0:1, :].to_broadcast([P, KC, H]), ALU.is_gt).then_inc(tern, 1)

            def scale_context(n, c):
                dve.wait_ge(cx_in[c], 16 * (n // 2 + 1))
                nc.vector.tensor_reduce(c_amax[:], chunk_in[c][:], AX_X, ALU.max, apply_absolute_value=True).then_inc(cs, 1)
                dve.wait_ge(cs, 6 * n + 1)
                nc.vector.tensor_scalar(c_amax[:], c_amax[:], TINY, None, ALU.max).then_inc(cs, 1)
                dve.wait_ge(cs, 6 * n + 2)
                nc.vector.tensor_single_scalar(c_exp[:].bitcast(I32), c_amax[:].bitcast(I32), EXP_MASK,
                                               ALU.bitwise_and).then_inc(cs, 1)
                dve.wait_ge(cs, 6 * n + 3)
                nc.vector.tensor_scalar(c_scale[:].bitcast(I32), c_exp[:].bitcast(I32), -1.0,
                                        float((254 + CTX_BITS) << 23), ALU.mult, ALU.add).then_inc(cs, 1)
                nc.vector.tensor_scalar(c_inv[:, c, :].bitcast(I32), c_exp[:].bitcast(I32), -float(CTX_BITS << 23), None,
                                        ALU.add).then_inc(cs, 1)
                dve.wait_ge(cs, 6 * n + 5)
                nc.vector.tensor_scalar(c_inv[:, c, :], c_inv[:, c, :], inv["o"], None, ALU.mult).then_inc(cs, 1)
                for j in range(TPC):
                    nc.vector.tensor_scalar(chunk_in[c][:, j, :], chunk_in[c][:, j, :], c_scale[:, j:j + 1], None,
                                            ALU.mult).then_inc(z_set, 1)

            def x_stats(s, n):
                seen = s - CHUNKS
                dve.wait_ge(x_set, TPC * (seen + 1))
                for j in range(TPC):
                    nc.vector.bn_stats(st_x[:, j, :], x_tile(n, j)).then_inc(sx, 1)
                dve.wait_ge(sx, TPC * (seen + 1))
                nc.vector.memset(turn[:], 0.0)
                for j in range(TPC):
                    nc.vector.bn_aggr(mv_x[:, j, :], st_x[:, j, :]).then_inc(ax, 1)

            def normalise(s, n, j):
                dve.wait_ge(rx, s - CHUNKS + 1)
                dve.wait_ge(t_done, TPC * (s - 1) + (j + 1))
                nc.vector.tensor_scalar(zf[:, j, :], x_tile(n, j), mv_x[:, j, 0:1], rs_x[:, j:j + 1], ALU.subtract,
                                        ALU.mult).then_inc(z_set, 1)

            def low_part(s, c, j):
                dve.wait_ge(zh_set, TPC * s + (j + 1))
                nc.vector.scalar_tensor_tensor(
                    out=z_lo[:, c, :, j * P:(j + 1) * P], in0=ps_t[j % 2][:].rearrange("p (k t) -> p k t", k=KC),
                    scalar=Z_SCALE, in1=z_hi[:, c, :, j * P:(j + 1) * P], op0=ALU.mult,
                    op1=ALU.subtract).then_inc(t_free, 1)

            def make_terms(q):
                DL = TERMS + 4
                dve.wait_ge(gu_done, q + 1)
                nc.vector.tensor_scalar(delta, ps_y[0][:], inv["gu"], lp[:, 0:1], ALU.mult,
                                        ALU.subtract).then_inc(dl, 1)
                nc.vector.tensor_scalar(terms[:, 0, :], ps_y[1][:], inv["gu"], None, ALU.mult).then_inc(dl, 1)
                dve.wait_ge(dl, DL * q + 2)
                nc.vector.tensor_single_scalar(kept, delta, THD, ALU.is_le).then_inc(dl, 1)
                dve.wait_ge(dl, DL * q + 3)
                nc.vector.scalar_tensor_tensor(out=kept, in0=delta, scalar=-THD, in1=kept, op0=ALU.is_ge,
                                               op1=ALU.mult).then_inc(dl, 1)
                dve.wait_ge(dl, DL * q + 4)
                nc.vector.tensor_tensor(kept, kept, delta, ALU.mult).then_inc(dl, 1)
                for m in range(1, TERMS):
                    dve.wait_ge(dl, DL * q + (4 + m))
                    by = kept if m == GRAD_ORDER_MIN + 1 else delta
                    nc.vector.tensor_tensor(terms[:, m, :], terms[:, m - 1, :], by, ALU.mult).then_inc(dl, 1)

            def make_hidden(q, blocks):
                for f in blocks:
                    rows = P if f < FB - 1 else F_LAST
                    k = q * FB + f
                    dve.wait_ge(sg_set, k + 1)
                    dve.wait_ge(p_done, 2 * k + 2)
                    nc.vector.scalar_tensor_tensor(out=hidden[0:rows, f, :], in0=ps_p[2 * (f % 2) + 1][0:rows, :],
                                                   scalar=inv["u"][0:rows, :], in1=sg[0:rows, f % 2, :], op0=ALU.mult,
                                                   op1=ALU.mult).then_inc(h_set, 1)

            def route(n):
                base = ROUTE_STEPS * n
                count = [0]

                def done(ins, wait=True):
                    count[0] += 1
                    ins.then_inc(rt, 1)
                    if wait:
                        dve.wait_ge(rt, base + count[0])

                dve.wait_ge(r_done, n + 1)
                done(nc.vector.tensor_scalar(lm, ps_p[0][:, 0:TPC * RA].rearrange("p (j r) -> p j r", j=TPC),
                                             inv["ra"], None, ALU.mult))
                lg = lm[:, :, 0:E]
                pairs = [(a, b) for a in range(E) for b in range(a + 1, E)]
                done(nc.vector.tensor_reduce(top[:], lg, AX_X, ALU.max), wait=False)
                for i, (a, b) in enumerate(pairs):
                    done(nc.vector.tensor_tensor(gt[:, i, :], lg[:, :, b], lg[:, :, a], ALU.is_gt), wait=(i == 5))
                done(nc.vector.tensor_tensor(gates[:], lg, top[:].unsqueeze(2).to_broadcast([P, TPC, E]), ALU.subtract))
                assert count[0] == ROUTE_EXP
                g = lambda a, b: gt[:, pairs.index((a, b)), :]
                chains = [(0, [(g(0, 1), 1), (g(0, 2), 1), (g(0, 3), 1)]), (1, [(g(0, 1), -1), (g(1, 2), 1), (g(1, 3), 1)]),
                          (2, [(g(0, 2), -1), (g(1, 2), -1), (g(2, 3), 1)]), (3, [(g(0, 3), -1), (g(1, 3), -1), (g(2, 3), -1)])]
                for step in (1, 2):
                    for e, terms_ in chains:
                        r = rank[:, :, e]
                        if step == 1:
                            (a, sa), (b, sb_) = terms_[0], terms_[1]
                            done(nc.vector.scalar_tensor_tensor(out=r, in0=a, scalar=float(sa), in1=b, op0=ALU.mult,
                                                                op1=ALU.add if sb_ > 0 else ALU.subtract), wait=(e == 3))
                        else:
                            c_, sc_ = terms_[2]
                            done(nc.vector.scalar_tensor_tensor(out=r, in0=r, scalar=float(sum(s < 0 for _, s in terms_)), in1=c_,
                                                                op0=ALU.add, op1=ALU.add if sc_ > 0 else ALU.subtract),
                                 wait=(e == 3))
                dve.wait_ge(ex, n + 1)
                done(nc.vector.scalar_tensor_tensor(out=gates[:], in0=rank[:], scalar=2.0, in1=gates[:], op0=ALU.is_lt,
                                                    op1=ALU.mult))
                done(nc.vector.tensor_reduce(top[:], gates[:], AX_X, ALU.add))
                done(nc.vector.reciprocal(top[:], top[:]))
                assert count[0] == ROUTE_STEPS, count
                nc.vector.scalar_tensor_tensor(out=gates[:], in0=gates[:], scalar=LORA_SCALE,
                                               in1=top[:].unsqueeze(2).to_broadcast([P, TPC, E]), op0=ALU.mult,
                                               op1=ALU.mult).then_inc(gm_set, 1)
                dve.wait_ge(gm_set, (1 + TPC) * n + 1)
                dve.wait_ge(mem, 5)
                for j in range(TPC):
                    nc.vector.tensor_tensor(gm[:, j, 0:E * R].rearrange("p (e r) -> p e r", e=E),
                                            lm[:, j, E:RA].rearrange("p (e r) -> p e r", e=E),
                                            gates[:, j, :].unsqueeze(2).to_broadcast([P, E, R]),
                                            ALU.mult).then_inc(gm_set, 1)

            def y_stats(s, layer, c, j):
                if layer in (O_, F0):
                    dve.wait_ge(y_done, TPC * s + (j + 1))
                    if not (layer == O_ and s == 0):
                        dve.wait_ge(x_set, TPC * s - 3 + j)
                    nc.vector.scalar_tensor_tensor(out=y[:, j, :], in0=ps_y[j % 2][:],
                                                   scalar=c_inv[:, c, j:j + 1] if layer == O_ else inv["0"],
                                                   in1=(bo if layer == O_ else b0)[:], op0=ALU.mult,
                                                   op1=ALU.add).then_inc(y_free, 1)
                dve.wait_ge(y_free, 2 + TPC * s + (j + 1))
                nc.vector.bn_stats(st_y[:, j, :], y[:, j, :]).then_inc(sy, 1)

            def stage(s, layer, n, c):
                if layer == L1:
                    q = s - CHUNKS * L1
                    make_hidden(q, [0])
                    make_terms(q)
                    make_hidden(q, range(1, FB))
                if layer == L3:
                    route(n)
                for pair in ((0, 1), (2, 3)):
                    for j in pair:
                        if has_stage(1, layer, n):
                            low_part(s + 1, 1 - c, j)
                        if has_stage(2, layer, n) and not (layer == O_ and n < 2):
                            normalise(s + 2, (n + 2) % CHUNKS, j)
                        if layer != L3:
                            y_stats(s, layer, c, j)
                    for j in pair if layer == L3 else ():
                        y_stats(s, layer, c, j)
                dve.wait_ge(sy, TPC * (s + 1))
                nc.vector.memset(turn[:], 0.0)
                for j in range(TPC):
                    nc.vector.bn_aggr(mv_y[:, j, :], st_y[:, j, :]).then_inc(ay, 1)
                if layer == O_ and n < 2:
                    scale_context(n + 2, c)
                if has_stage(3, layer, n) and not (layer == O_ and n == 0):
                    x_stats(s + 3, (n + 3) % CHUNKS)
                dve.wait_ge(ry, s + 1)
                for j in range(TPC):
                    nc.vector.tensor_scalar(y[:, j, :], y[:, j, :], mv_y[:, j, 0:1], rs_y[:, j:j + 1], ALU.subtract,
                                            ALU.mult).then_inc(yn, 1)

            def before(layer):
                if layer == L1:
                    dve.wait_ge(w_split["u"], KC)

            split("o")
            dve.wait_ge(c_in, 80)
            scale_context(0, 0)
            for j in range(TPC):
                low_part(0, 0, j)
            ternary()
            scale_context(1, 1)
            layer_loops(dve, stage, split, before)

        @block.tensor
        def _(pe):
            def transposes(s, j, src=zf):
                pe.wait_ge(z_set, TPC * s + (j + 1))
                pe.wait_ge(t_free, TPC * s + (j + 1))
                for k in range(KC):
                    tr = nc.tensor.transpose(ps_t[j % 2][:, k * P:(k + 1) * P], src[:, j, k * P:(k + 1) * P], ident[:])
                tr.then_inc(t_done, 1)

            def by_tokens(dst, key, c, j, cols, start=True, stop=True):
                t = slice(j * P, (j + 1) * P)
                for m, (a, w) in enumerate(((z_hi, hi[key]), (z_hi, lo[key]), (z_lo, hi[key]))):
                    for k in range(KC):
                        mm = nc.tensor.matmul(dst, a[:, c, k, t], w[:, k, cols], start=(m == 0 and k == 0),
                                              stop=(m == 2 and k == KC - 1))
                return mm

            def by_columns(dst, key, c, cols):
                for m, (w, a) in enumerate(((hi[key], z_hi), (hi[key], z_lo), (lo[key], z_hi))):
                    for k in range(KC):
                        mm = nc.tensor.matmul(dst, w[:, k, cols], a[:, c, k, :], start=(m == 0 and k == 0),
                                              stop=(m == 2 and k == KC - 1))
                return mm

            def project(q, c, f):
                rows = P if f < FB - 1 else F_LAST
                cols = slice(f * P, f * P + rows)
                pe.wait_ge(h_set, q * FB + (f + 1))
                by_columns(ps_p[2 * (f % 2)][0:rows, :], "g", c, cols).then_inc(p_done, 1)
                by_columns(ps_p[2 * (f % 2) + 1][0:rows, :], "u", c, cols).then_inc(p_done, 1)

            def stage(s, layer, n, c):
                q = s - CHUNKS * L1
                if layer != L3:
                    pe.wait_ge(t_free, 2 + TPC * (s + 1))
                if layer == L1:
                    project(q, c, 0)
                    pe.wait_ge(y_free, TPC * s + 2)
                    by_columns(ps_y[0][:], "gu", c, slice(0, S))
                    by_columns(ps_y[1][:], "gu", c, slice(S, 2 * S)).then_inc(gu_done, 1)
                    for f in range(1, FB):
                        project(q, c, f)
                    pe.wait_ge(dl, (TERMS + 4) * (q + 1))
                if layer == L3:
                    for j in range(TPC):
                        pe.wait_ge(gm_set, (1 + TPC) * n + j + 2)
                        if TPC * n + j >= 2:
                            pe.wait_ge(gt_set, TPC * n + j - 1)
                        nc.tensor.transpose(ps_p[1 + j % 2][:, 0:P], gm[:, j, :], ident[:]).then_inc(gt_done, 1)
                    for pair in ((0, 1), (2, 3)):
                        for j in pair:
                            if has_stage(1, layer, n):
                                transposes(s + 1, j)
                        for j in pair:
                            pe.wait_ge(gt_set, TPC * n + j + 1)
                            pe.wait_ge(y_free, TPC * s + (j + 1))
                            nc.tensor.matmul(ps_y[j % 2][:], gmt[:, j, :], wb[:], start=True, stop=True).then_inc(y_done, 1)
                    if has_stage(1, layer, n):
                        logits(s + 1, 1 - c)
                for j in range(TPC) if layer != L3 else ():
                    transposes(s + 1, j, chunk_in[1 - c] if layer == O_ and n < CHUNKS - 1 else zf)
                    pe.wait_ge(y_free, TPC * s + (j + 1))
                    if layer in (O_, F0):
                        mm = by_tokens(ps_y[j % 2][:], "o" if layer == O_ else "0", c, j, slice(0, H))
                    if layer == L1:
                        t = slice(j * P, (j + 1) * P)
                        for m in range(TERMS):
                            nc.tensor.matmul(ps_y[j % 2][:], terms[:, m, t], wt[:, m, :], start=(m == 0), stop=False)
                        if j == 0:
                            pe.wait_ge(h_set, 2 + FB * (q + 1))
                            pe.wait_ge(wd_in, 32)
                        for f in range(FB):
                            rows = P if f < FB - 1 else F_LAST
                            mm = nc.tensor.matmul(ps_y[j % 2][:], hidden[0:rows, f, t], wd[0:rows, f, :], start=False,
                                                  stop=(f == FB - 1))
                    mm.then_inc(y_done, 1)

            def logits(s, c):
                pe.wait_ge(t_free, 2 + TPC * (s + 1))
                for j in range(TPC):
                    mm = by_tokens(ps_p[0][:, j * RA:(j + 1) * RA], "ra", c, j, slice(0, RA))
                mm.then_inc(r_done, 1)

            pe.wait_ge(c_in, 80)
            for j in range(TPC):
                transposes(0, j)
            pe.wait_ge(absd, 1)
            pe.wait_ge(mem, 5)
            for k in range(KC):
                mm = nc.tensor.matmul(ps_y[0][:], ones[:], t_a[:, k * H:(k + 1) * H], start=(k == 0), stop=(k == KC - 1))
            mm.then_inc(colsum, 1)

            def before(layer):
                if layer == O_:
                    pe.wait_ge(tern, 1)
                    pe.wait_ge(w_split["o"], 1)
                if layer == F0:
                    pe.wait_ge(w_split["0"], 1)
                if layer == L1:
                    for k in ("gu", "ra"):
                        pe.wait_ge(w_split[k], 1)
                    for k in wide:
                        pe.wait_ge(w_split[k], KC)
                    pe.wait_ge(wt_in, 32)
                    pe.wait_ge(wt_set, G)
                if layer == L3:
                    logits(CHUNKS * L3, 0)

            layer_loops(pe, stage, before=before)




def sandwich_kernel(nc, t, out):
    context = nc.dram_tensor("context", [TOKENS, H], F32, kind="Internal").ap()
    attention_block(nc, t["x"], t["w_qkv"], t["b_qk"], t["b_v"], t["ident"], context)
    layers_block(nc, t["x"], context, t["w_o"], t["b_o"], t["w_0"], t["b_0"], t["w_gu"], t["point"], t["w_terms"],
                 t["discount"], t["w_g"], t["w_u"], t["w_d"], t["w_ra"], t["w_b"], t["ident"], out)


_OUTS = [((BATCH, SEQ, H), "float32")]


def kernel(**inputs):
    import numpy as _np
    import concourse.bacc as _bacc
    from concourse import mybir as _mybir
    from concourse.bass_utils import run_bass_kernel_spmd as _run

    nc = _bacc.Bacc("TRN2", target_bir_lowering=False, num_devices=1)
    nc.disable_value_cache = True
    a = {k: _np.asarray(v) for k, v in inputs.items()}
    two_h = 2 * H
    bias = a["L0_attn_attn_qkvb"]
    laid = {
        "x": a["L0_attn_x"].reshape(TOKENS, H),
        "w_qkv": a["L0_attn_attn_qkvw"],
        "b_qk": bias[:two_h].reshape(2 * KC, P).T,
        "b_v": bias[two_h:].reshape(1, H),
        "ident": _np.eye(P, dtype=_np.float32),
        "w_o": a["L0_attn_attn_ow"],
        "b_o": a["L0_attn_attn_ob"].reshape(1, H),
        "w_0": a["L0_ffn_weight"].T,
        "b_0": a["L0_ffn_bias"].reshape(1, H),
        "w_gu": _np.concatenate([a["L1_attn_gate_w"], a["L1_attn_up_w"]], 0).T,
        "point": a["L1_attn_local_point"].reshape(-1, 1),
        "w_terms": _np.concatenate([a["L1_attn_local_approx_output"][:, :, None], a["L1_attn_fuse_weight"]], 2).transpose(1, 2, 0),
        "discount": a["L1_attn_discount_factor"].reshape(1, -1),
        "w_g": a["L1_attn_ffn_gate_w"].T,
        "w_u": a["L1_attn_ffn_up_w"].T,
        "w_d": a["L1_attn_ffn_down_w"].T,
        "w_ra": _np.concatenate([a["L1_ffn_router_w"], a["L1_ffn_A"].reshape(-1, H)], 0).T,
        "w_b": a["L1_ffn_B"].transpose(0, 2, 1).reshape(-1, H),
    }
    arrays, t = {}, {}
    for name, value in laid.items():
        value = _np.ascontiguousarray(value)
        arrays[f"in_{name}_dram"] = value
        t[name] = nc.dram_tensor(f"in_{name}_dram", value.shape, _mybir.dt.from_np(value.dtype), kind="ExternalInput").ap()
    out = nc.dram_tensor("out_0_dram", (TOKENS, H), F32, kind="ExternalOutput").ap()
    sandwich_kernel(nc, t, out)
    r = _run(nc, [arrays], core_ids=[0])
    return r.results[0]["out_0_dram"].reshape(BATCH, SEQ, H)
```

```python
from contextlib import ExitStack

import concourse.bass as bass
from concourse import mybir

F32 = mybir.dt.float32
F16 = mybir.dt.float16
BF16 = mybir.dt.bfloat16
I32 = mybir.dt.int32
ACT = mybir.ActivationFunctionType
ALU = mybir.AluOpType
AX_X = mybir.AxisListType.X
RMAX = bass.bass_isa.ReduceOp.max

P = 128
BATCH, SEQ, H = 2, 1024, 512
TOKENS = BATCH * SEQ
KC = H // P
HEADS = 32
HD = H // HEADS
SOFTMAX_SCALE = float(HD) ** -0.5
EPS = 1e-5
CHUNK = 512
TPC = CHUNK // P
CHUNKS = TOKENS // CHUNK

Z_BITS = 10
Z_SCALE = float(2 ** Z_BITS)
W_BITS = 14
EXP_MASK = 0x7F800000
SCALE_FROM_EXP = float((254 + W_BITS) << 23)
INV_FROM_EXP = -float((W_BITS + Z_BITS) << 23)
TINY = 1e-30

GH = 4
GROUPS_B = HEADS // GH
GROUPS = BATCH * GROUPS_B
KT = SEQ // P
HALF = SEQ // 2
Q_ROWS = (0, 1, 2, 0, 1, 0)
K_ROWS = (0, 0, 0, 1, 1, 2)
STACK = 6 * HD
MAX_ROW = STACK
ROWS = STACK + 2
SLOTS = 3
MAX_MM = GH * KT * 2
EXPS = 2 * KT * 2
MAX_BY = 26
EARLY = MAX_MM * (EXPS - MAX_BY) // EXPS
PAIRS = EXPS // 2
BEFORE_V = 1
QK_TILES = 2 * KC
PER_QK = MAX_MM // (2 * QK_TILES)
TURN_LAG = 2
PROBS = 8
PAIR_LAG = 5
STORE_RING = 4
RING = 3


def pair_at(u):
    for p in range(-2, PAIRS):
        first_of_half = p % KT == 0
        if 2 * p + PAIR_LAG + first_of_half == u:
            return (p < 0, p % PAIRS)
    return None


def ring_plan(prologue=False, first=False, nexts=2):
    plan, n = [], 0

    def use(u, what, which):
        nonlocal n
        plan.append((u, what, which, n % RING, n // RING))
        n += 1

    if prologue:
        for w in range(MAX_MM):
            use(w // PER_QK, "scores", w)
        use(2 * QK_TILES, "max", 0)
        for w in range(EARLY):
            use(2 * QK_TILES, "early", w)
        return plan
    for u in range(EXPS):
        if u < MAX_BY and nexts >= 1:
            for w in range((MAX_MM - EARLY) * u // MAX_BY, (MAX_MM - EARLY) * (u + 1) // MAX_BY):
                use(u, "scores", EARLY + w)
        if u >= MAX_BY and nexts >= 2:
            for w in range(EARLY * (u - MAX_BY) // (EXPS - MAX_BY), EARLY * (u - MAX_BY + 1) // (EXPS - MAX_BY)):
                use(u, "early", w)
        if u == MAX_BY + TURN_LAG and nexts >= 1:
            use(u, "max", 0)
        if u == PAIR_LAG + 2 and not first:
            use(u, "ctx", 1)
        if u == PAIR_LAG + 2 + 2 * KT:
            use(u, "ctx", 0)
    return plan


def uses(plan, bank):
    return sum(b == bank for _, _, _, b, _ in plan)


def find(plan, what, which):
    return next((b, k) for _, a, w, b, k in plan if (a, w) == (what, which))


def attention_block(nc, x, w_qkv, b_qk, b_v, ident_dram, ident, ctx_dram, w_o, wo_hi, wo_lo, wo_scale,
                    first_chunk):
    qk_dram = nc.dram_tensor("qk_parts", [2, 3, TOKENS // SEQ * H, SEQ], BF16, kind="Internal").ap()
    qk_groups = qk_dram.rearrange("w s (g r) t -> w s g r t", r=GH * HD)

    with ExitStack() as ctx:
        def sb(name, shape, dt):
            return ctx.enter_context(nc.sbuf_tensor(name, shape, dt))

        def psum(name, shape, dt=F32):
            return ctx.enter_context(nc.psum_tensor(name, shape, dt))

        def sem(name):
            return ctx.enter_context(nc.semaphore(name))

        arena = sb("arena", [P, PROBS * 2 * HALF], F32)
        xin = arena[:, 0:2 * TPC * H].rearrange("p (c j f) -> p c j f", c=2, j=TPC)
        z_both = arena[:, 2 * TPC * H:4 * TPC * H].bitcast(F16).rearrange("p (w c k t) -> p w c k t", w=2, c=2, k=KC)
        z_hi, z_lo = z_both[:, 0], z_both[:, 1]
        probs = arena[:].rearrange("p (r t) -> p r t", r=PROBS)
        w_hi = sb("w_hi", [P, KC, 3 * H], F16)
        w_lo = sb("w_lo", [P, KC, 3 * H], F16)
        bqk = sb("bqk", [P, 2 * KC], F32)
        bv = sb("bv", [P, H], F32)
        assert KC == TPC
        wo_stage = first_chunk
        wo_amax = sb("wo_amax", [P, 3], F32)
        amax_k = sb("amax_k", [P, KC], F32)
        amax = sb("amax", [P, 3], F32)
        wscale = sb("wscale", [P, 2], F32)
        stats = sb("stats", [P, 2, TPC, 6], F32)
        mv = sb("mv", [P, 2, TPC, 2], F32)
        rstd = sb("rstd", [P, 2, TPC], F32)
        neg_half = sb("neg_half", [P, TPC], F32)
        y = sb("y", [P, STORE_RING, CHUNK], F32)
        parts = sb("parts", [P, STORE_RING, 3, CHUNK], BF16)
        v_all = sb("v_all", [P, TOKENS // P, H], F32)
        stack = sb("stack", [P, SLOTS, 2, GH * SEQ], BF16)
        w_stage = stack[:].rearrange("p s w t -> p (s w t)")[:, 0:2 * KC * 3 * H].bitcast(F32)
        v_stage = sb("v_stage", [P, SLOTS, KT, GH, 32], F32)
        max_part = sb("max_part", [P, MAX_MM], F32)
        maxes = sb("maxes", [P, GH * KT], F32)
        max_rows = sb("max_rows", [GH * KT, 2, P], BF16)
        ctx_t = sb("ctx_t", [P, HALF], F32)
        rsum = sb("rsum", [P, 2, 4 * GH], F32)
        ctx_n = sb("ctx_n", [P, 2, 4, GH * HD], F32)

        ps_s = [psum(f"ps_s{i}", [P, 2 * HALF]) for i in range(2)]
        ps_c = psum("ps_c", [P, HALF])
        ps_r = [psum(f"ps_r{i}", [P, 512]) for i in range(RING)]
        ps_tr = ps_r[0:2]
        ps_vp = [ps_c, ps_r[2]]
        ps_qk = [ps_s[i][:, 512 * e:512 * (e + 1)] for i in range(2) for e in range(2)]

        consts_in = sem("consts_in")
        w_in = [sem(f"w_in{k}") for k in range(KC)]
        x_in = [sem(f"x_in{c}") for c in range(2)]
        wo_in = sem("wo_in")
        first_in = sem("first_in")
        wo_own = sem("wo_own")
        wo_all = sem("wo_all")
        wo_exp, wo_scaled = sem("wo_exp"), sem("wo_scaled")
        wo_hi_set, wo_lo_set = sem("wo_hi_set"), sem("wo_lo_set")
        neg_half_set = sem("neg_half_set")
        amax_set = sem("amax_set")
        amax_all = sem("amax_all")
        exp_set = sem("exp_set")
        wscale_set = sem("wscale_set")
        w_hi_set = sem("w_hi_set")
        w_lo_set = sem("w_lo_set")
        stats_set = sem("stats_set")
        mv_set = sem("mv_set")
        var_eps = sem("var_eps")
        rstd_set = sem("rstd_set")
        z_set = sem("z_set")
        tr_done = sem("tr_done")
        z_hi_set = sem("z_hi_set")
        tr_free = sem("tr_free")
        v_done = sem("v_done")
        v_free = sem("v_free")
        qk_done = sem("qk_done")
        qk_free = sem("qk_free")
        rest_set = sem("rest_set")
        second_set = sem("second_set")
        parts_set = sem("parts_set")
        stored = [sem(f"stored{s}") for s in range(STORE_RING)]
        stage_const = sem("stage_const")
        loaded = [sem(f"loaded{i}") for i in range(SLOTS)]
        v_staged = sem("v_staged")
        ring_done = [sem(f"ring_done{b}") for b in range(RING)]
        ring_free = [sem(f"ring_free{b}") for b in range(RING)]
        mx_set = sem("mx_set")
        mx_step = sem("mx_step")
        mx_in = sem("mx_in")
        st_done = sem("st_done")
        exp_done = sem("exp_done")
        pv_done = sem("pv_done")
        pv_free = sem("pv_free")
        rsum_set = sem("rsum_set")
        ctx_out = [sem(f"ctx_out{h}") for h in range(2)]
        block = ctx.enter_context(nc.Block())

        prologue, plan_n = ring_plan(prologue=True), ring_plan()
        plans = {0: ring_plan(first=True), GROUPS - 2: ring_plan(nexts=1), GROUPS - 1: ring_plan(nexts=0)}

        def plan_of(g):
            return plans.get(g, plan_n) if isinstance(g, int) else plan_n

        def used(g, bank):
            if isinstance(g, int):
                return uses(prologue, bank) + sum(uses(plan_of(before), bank) for before in range(g))
            return uses(prologue, bank) + uses(plan_of(0), bank) + uses(plan_n, bank) * (g - 1)

        def after(g, what, which):
            bank, k = find(plan_of(g), what, which)
            return bank, used(g, bank) + k + 1

        def turned_beside_v(n):
            return 0 < n < CHUNKS - 1

        def beside_qk(n, f):
            return [use for use in prologue if use[1] == "scores" and use[0] == (n - (CHUNKS - 2)) * QK_TILES + f]

        def steps(engine, step):
            step(0, 0, first=True)
            with engine.Fori(0, (GROUPS - 4) // SLOTS) as i:
                step(3 * i + 1, 1)
                step(3 * i + 2, 2)
                step(3 * i + 3, 0)
            step(GROUPS - 3, 1)
            step(GROUPS - 2, 2)
            step(GROUPS - 1, 0, last=True)

        @block.sync
        def _(sp):
            sp.dma_start(xin[:, 0], x[0:CHUNK, :].rearrange("(j p) f -> p j f", p=P)).then_inc(x_in[0], 16)
            sp.dma_start(ident[:], ident_dram).then_inc(consts_in, 16)
            sp.dma_start(bqk[:], b_qk).then_inc(consts_in, 16)
            sp.dma_start(bv[:], b_v.to_broadcast([P, H])).then_inc(consts_in, 16)

            def store_parts(n, c):
                for f in range(QK_TILES):
                    sp.wait_ge(parts_set, QK_TILES * n + f + 1)
                    row = (n // 2) * H + (f % KC) * P
                    dst = qk_dram[f // 4, :, bass.ds(row, P), c * CHUNK:(c + 1) * CHUNK]
                    sp.dma_start(dst.rearrange("s r t -> r s t"), parts[:, f % STORE_RING]).then_inc(stored[f % STORE_RING], 16)

            def load_x(n):
                sp.wait_ge(tr_done, TPC * (n - 1))
                sp.dma_start(xin[:, n % 2], x[n * CHUNK:(n + 1) * CHUNK, :].rearrange("(j p) f -> p j f", p=P)
                             ).then_inc(x_in[n % 2], 16)

            def batch_stored(b):
                for s in range(STORE_RING):
                    sp.wait_ge(stored[s], 16 + 16 * QK_TILES * 2 * (b + 1) // STORE_RING)

            def load(g, slot):
                for which, rows in ((0, Q_ROWS), (1, K_ROWS)):
                    for r, part in enumerate(rows):
                        sp.dma_start(stack[r * HD:(r + 1) * HD, slot, which, :].rearrange("d (j t) -> d j t", j=GH),
                                     qk_groups[which, part, g, :, :].rearrange("(j d) t -> d j t", j=GH)
                                     ).then_inc(loaded[slot], 16)

            def max_rows_in(bank, count, slot):
                sp.wait_ge(ring_free[bank], count + 1)
                for s in range(2):
                    sp.dma_start(stack[MAX_ROW + s:MAX_ROW + s + 1, slot, 0, :], max_rows[:, s, :]).then_inc(mx_in, 16)

            def ctx_store(g, half, bank, count):
                sp.wait_ge(ring_free[bank], count + 1)
                row = (g // GROUPS_B) * SEQ + half * HALF
                dst = ctx_dram[bass.ds(row, HALF), bass.ds((g % GROUPS_B) * GH * HD, GH * HD)]
                sp.dma_start(dst.rearrange("(t p) f -> p t f", p=P), ctx_n[:, half]).then_inc(ctx_out[half], 16)

            def step(g, slot, first=False, last=False):
                if not isinstance(g, int) or g + 2 < GROUPS:
                    if not first:
                        sp.wait_ge(st_done, EXPS * g)
                    load(g + 2, (slot + 2) % SLOTS)
                if isinstance(g, int) and g == GROUPS - SLOTS:
                    sp.wait_ge(wo_lo_set, 1)
                    sp.wait_ge(ctx_out[0], 16 + 16 * g)
                    sp.dma_start(first_chunk[:], ctx_dram[0:CHUNK, :].rearrange("(j p) f -> p j f", p=P)).then_inc(first_in, 16)
                if not first:
                    ctx_store(g - 1, 1, *after(g, "ctx", 1))
                ctx_store(g, 0, *after(g, "ctx", 0))
                if not last:
                    max_rows_in(*after(g, "max", 0), (slot + 1) % SLOTS)

            load_x(2)
            sp.dma_start(wo_stage[:], w_o.rearrange("(k p) n -> p k n", p=P)).then_inc(wo_in, 16)
            store_parts(0, 0)
            load_x(3)
            store_parts(1, 1)
            batch_stored(0)
            sp.wait_ge(w_lo_set, KC)
            load(0, 0)
            load(1, 1)
            store_parts(2, 0)
            store_parts(3, 1)
            batch_stored(1)
            bank, k = find(prologue, "max", 0)
            max_rows_in(bank, k + 1, 0)
            steps(sp, step)
            bank = 0
            ctx_store(GROUPS - 1, 1, bank, used(GROUPS, bank) + 1)
            sp.wait_ge(first_in, 16)
            for half in range(2):
                sp.wait_ge(ctx_out[half], 16 + 16 * GROUPS)

        @block.gpsimd
        def _(pool):
            nc.gpsimd.memset(neg_half[:], -0.5).then_inc(neg_half_set, 1)
            nc.gpsimd.memset(v_stage[:], 0.0).then_inc(stage_const, 1)
            pool.wait_ge(stage_const, 1)
            nc.gpsimd.memset(v_stage[:, :, :, :, HD:HD + 1], 1.0).then_inc(stage_const, 1)

            def rstds(n, c):
                pool.wait_ge(mv_set, TPC * (n + 1))
                nc.gpsimd.tensor_scalar(rstd[:, c, :], mv[:, c, :, 1], EPS, None, ALU.add).then_inc(var_eps, 1)
                pool.wait_ge(var_eps, n + 1)
                pool.wait_ge(neg_half_set, 1)
                nc.gpsimd.tensor_tensor(rstd[:, c, :], rstd[:, c, :], neg_half[:], ALU.pow).then_inc(rstd_set, 1)

            rstds(0, 0)
            pool.wait_ge(amax_set, KC + 1)
            nc.gpsimd.partition_all_reduce(amax[:, 1:2], amax[:, 0:1], P, RMAX).then_inc(amax_all, 1)
            rstds(1, 1)
            pool.wait_ge(w_lo_set, KC)
            pool.wait_ge(rstd_set, 2)
            for s in range(SLOTS):
                nc.gpsimd.memset(stack[MAX_ROW:ROWS, s, 1, :], 1.0).then_inc(stage_const, 1)
                pool.wait_ge(stage_const, 3 + s)
            for n in range(CHUNKS):
                for f in range(QK_TILES):
                    if f == TPC and n + 2 < CHUNKS:
                        rstds(n + 2, n % 2)
                    if (n, f) == (1, QK_TILES - 2):
                        pool.wait_ge(wo_own, 1)
                        nc.gpsimd.partition_all_reduce(wo_amax[:, 1:2], wo_amax[:, 0:1], P, RMAX).then_inc(wo_all, 1)
                    s = f % STORE_RING
                    pool.wait_ge(second_set, QK_TILES * n + f + 1)
                    nc.gpsimd.tensor_tensor(parts[:, s, 2], y[:, s], parts[:, s, 1], ALU.subtract).then_inc(parts_set, 1)

            v_view = v_all[:].rearrange("p (b t) (g j d) -> p b t g j d", b=BATCH, g=GROUPS_B, j=GH)

            def stage_v(g, par):
                nc.gpsimd.tensor_copy(v_stage[:, par, :, :, 0:HD],
                                      v_view[:, g // GROUPS_B, :, g % GROUPS_B, :, :]).then_inc(v_staged, 1)

            def step(g, slot, first=False, last=False):
                if last:
                    return
                if not first:
                    pool.wait_ge(pv_done, 4 + PAIRS * (g - 1))
                stage_v(g + 1, (slot + 1) % SLOTS)

            pool.wait_ge(v_free, 2 + TOKENS // P)
            stage_v(0, 0)
            steps(pool, step)

        @block.scalar
        def _(act):
            act.wait_ge(x_in[0], 16)
            for k in range(KC):
                nc.scalar.dma_start(w_stage[:, k * 3 * H:(k + 1) * 3 * H], w_qkv[k * P:(k + 1) * P, :]).then_inc(w_in[k], 16)
            nc.scalar.dma_start(xin[:, 1], x[CHUNK:2 * CHUNK, :].rearrange("(j p) f -> p j f", p=P)).then_inc(x_in[1], 16)

            def high_part(n, j):
                act.wait_ge(tr_done, TPC * n + j + 1)
                nc.scalar.activation(z_hi[:, n % 2, :, j * P:(j + 1) * P],
                                     ps_tr[j % 2][:].rearrange("p (k t) -> p k t", k=KC), ACT.Copy,
                                     scale=Z_SCALE).then_inc(z_hi_set, 1)

            def second_part(n, f):
                act.wait_ge(rest_set, QK_TILES * n + f + 1)
                nc.scalar.copy(parts[:, f % STORE_RING, 1], y[:, f % STORE_RING]).then_inc(second_set, 1)

            def project(n):
                for j in range(TPC):
                    if turned_beside_v(n):
                        high_part(n + 1, j)
                for f in range(QK_TILES):
                    act.wait_ge(qk_done, QK_TILES * n + f + 1)
                    act.wait_ge(stored[f % STORE_RING], 16 * (2 * n + f // STORE_RING + 1))
                    nc.scalar.activation(y[:, f % STORE_RING], ps_qk[f % 4], ACT.Identity,
                                         bias=bqk[:, f:f + 1], scale=wscale[:, 1:2])
                    nc.scalar.activation(parts[:, f % STORE_RING, 0], ps_qk[f % 4], ACT.Identity,
                                         bias=bqk[:, f:f + 1], scale=wscale[:, 1:2]).then_inc(qk_free, 1)
                    if f:
                        second_part(n, f - 1)
                    if n == 0 and f < TPC:
                        high_part(1, f)
                second_part(n, QK_TILES - 1)
                if n == 1:
                    act.wait_ge(wo_scaled, 2)
                    nc.scalar.activation(wo_hi[:], wo_stage[:], ACT.Copy, scale=wo_scale[:, 0:1]).then_inc(wo_hi_set, 1)

            for j in range(TPC):
                high_part(0, j)
            act.wait_ge(wscale_set, 2)
            for k in range(KC):
                nc.scalar.activation(w_hi[:, k, :], w_stage[:, k * 3 * H:(k + 1) * 3 * H], ACT.Copy,
                                     scale=wscale[:, 0:1]).then_inc(w_hi_set, 1)
            act.wait_ge(consts_in, 48)
            for n in range(CHUNKS):
                project(n)

            def take_ctx(g, half):
                act.wait_ge(pv_done, 4 + PAIRS * g + KT * (half + 1))
                if half or not isinstance(g, int) or g:
                    act.wait_ge(rsum_set, 2 * g + half)
                nc.scalar.copy(ctx_t[:], ps_c[:]).then_inc(pv_free, 1)

            def step(g, slot, first=False, last=False):
                for u in range(EXPS):
                    act.wait_ge(st_done, EXPS * g + (u + 1))
                    if u % 2 == 0:
                        act.wait_ge(pv_done, PAIRS * g + (u // 2 + 1))
                    nc.scalar.activation(probs[:, u % PROBS], ps_s[u % 2][:], ACT.Exp,
                                         scale=SOFTMAX_SCALE).then_inc(exp_done, 1)
                    if u == PAIR_LAG - 1 and not first:
                        take_ctx(g - 1, 1)
                    if u == PAIR_LAG - 1 + 2 * KT:
                        take_ctx(g, 0)

            steps(act, step)
            take_ctx(GROUPS - 1, 1)

        @block.vector
        def _(dve):
            for credits, count in ((tr_free, 2), (v_free, 2), (qk_free, 4), (exp_done, 2), (pv_done, 4),
                                   (pv_free, 1), *((s, 1) for s in ring_free), *((s, 16) for s in stored), *((s, 16) for s in ctx_out)):
                dve.sem_inc(credits, count)

            def norm_in(n, c):
                dve.wait_ge(x_in[c], 16 * (n // 2 + 1))
                for j in range(TPC):
                    nc.vector.bn_stats(stats[:, c, j, :], xin[:, c, j, :]).then_inc(stats_set, 1)
                dve.wait_ge(stats_set, TPC * (n + 1))
                for j in range(TPC):
                    nc.vector.bn_aggr(mv[:, c, j, :], stats[:, c, j, :]).then_inc(mv_set, 1)
                dve.wait_ge(rstd_set, n + 1)
                for j in range(TPC):
                    nc.vector.tensor_scalar(xin[:, c, j, :], xin[:, c, j, :], mv[:, c, j, 0:1], rstd[:, c, j:j + 1],
                                            ALU.subtract, ALU.mult).then_inc(z_set, 1)

            def weight_maxima():
                for k in range(KC):
                    dve.wait_ge(w_in[k], 16)
                    nc.vector.tensor_reduce(amax_k[:, k:k + 1], w_stage[:, k * 3 * H:(k + 1) * 3 * H], AX_X, ALU.max,
                                            apply_absolute_value=True).then_inc(amax_set, 1)
                dve.wait_ge(amax_set, KC)
                nc.vector.tensor_reduce(amax[:, 0:1], amax_k[:], AX_X, ALU.max).then_inc(amax_set, 1)

            def scale_from(a, scale, steps, done):
                nc.vector.tensor_scalar(a[:, 1:2], a[:, 1:2], TINY, None, ALU.max).then_inc(steps, 1)
                dve.wait_ge(steps, 1)
                nc.vector.tensor_single_scalar(a[:, 2:3].bitcast(I32), a[:, 1:2].bitcast(I32), EXP_MASK,
                                               ALU.bitwise_and).then_inc(steps, 1)
                dve.wait_ge(steps, 2)
                nc.vector.tensor_scalar(scale[:, 0:1].bitcast(I32), a[:, 2:3].bitcast(I32), -1.0, SCALE_FROM_EXP,
                                        ALU.mult, ALU.add).then_inc(done, 1)
                nc.vector.tensor_scalar(scale[:, 1:2].bitcast(I32), a[:, 2:3].bitcast(I32), INV_FROM_EXP, None,
                                        ALU.add).then_inc(done, 1)

            def split_weights():
                dve.wait_ge(amax_all, 1)
                scale_from(amax, wscale, exp_set, wscale_set)
                dve.wait_ge(wscale_set, 2)
                for k in range(KC):
                    dve.wait_ge(w_hi_set, k + 1)
                    nc.vector.scalar_tensor_tensor(out=w_lo[:, k, :], in0=w_stage[:, k * 3 * H:(k + 1) * 3 * H],
                                                   scalar=wscale[:, 0:1], in1=w_hi[:, k, :], op0=ALU.mult,
                                                   op1=ALU.subtract).then_inc(w_lo_set, 1)

            def low_part(n, j):
                dve.wait_ge(z_hi_set, TPC * n + j + 1)
                nc.vector.scalar_tensor_tensor(
                    out=z_lo[:, n % 2, :, j * P:(j + 1) * P], in0=ps_tr[j % 2][:].rearrange("p (k t) -> p k t", k=KC),
                    scalar=Z_SCALE, in1=z_hi[:, n % 2, :, j * P:(j + 1) * P], op0=ALU.mult,
                    op1=ALU.subtract).then_inc(tr_free, 1)

            def take_rest(n, f):
                dve.wait_ge(qk_free, 4 + QK_TILES * n + f + 1)
                s = f % STORE_RING
                nc.vector.tensor_tensor(y[:, s], y[:, s], parts[:, s, 0], ALU.subtract).then_inc(rest_set, 1)

            def project(n):
                for j in range(TPC):
                    dve.wait_ge(v_done, TPC * n + j + 1)
                    nc.vector.scalar_tensor_tensor(out=v_all[:, TPC * n + j, :], in0=ps_vp[j % 2][:],
                                                   scalar=wscale[:, 1:2], in1=bv[:], op0=ALU.mult,
                                                   op1=ALU.add).then_inc(v_free, 1)
                    if turned_beside_v(n):
                        low_part(n + 1, j)
                if n == 0:
                    norm_in(1, 1)
                for f in range(QK_TILES):
                    beside = beside_qk(n, f)
                    for _, _, w, bank, k in beside[:PER_QK // 2]:
                        reduce_max(w, bank, k + 1)
                    if f:
                        take_rest(n, f - 1)
                    for _, _, w, bank, k in beside[PER_QK // 2:]:
                        reduce_max(w, bank, k + 1)
                    if n == 0 and f < TPC:
                        low_part(1, f)
                    if f == TPC and n + 2 < CHUNKS:
                        norm_in(n + 2, n % 2)
                    if (n, f) == (1, TPC):
                        dve.wait_ge(wo_in, 16)
                        nc.vector.tensor_reduce(wo_amax[:, 0:1], wo_stage[:].rearrange("p k n -> p (k n)"), AX_X, ALU.max,
                                                apply_absolute_value=True).then_inc(wo_own, 1)
                take_rest(n, QK_TILES - 1)
                if n == 1:
                    dve.wait_ge(wo_all, 1)
                    scale_from(wo_amax, wo_scale, wo_exp, wo_scaled)
                if n == 2:
                    dve.wait_ge(wo_hi_set, 1)
                    dve.wait_ge(wo_scaled, 2)
                    nc.vector.scalar_tensor_tensor(out=wo_lo[:], in0=wo_stage[:], scalar=wo_scale[:, 0:1], in1=wo_hi[:],
                                                   op0=ALU.mult, op1=ALU.subtract).then_inc(wo_lo_set, 1)

            def reduce_max(w, bank, count):
                dve.wait_ge(ring_done[bank], count)
                nc.vector.tensor_reduce(max_part[:, w:w + 1], ps_r[bank][:], AX_X, ALU.max).then_inc(ring_free[bank], 1)

            def join_max(gg, bank, count):
                dve.wait_ge(ring_free[bank], count + 1)
                nc.vector.tensor_reduce(maxes[:], max_part[:].rearrange("p (t h) -> p t h", h=2), AX_X,
                                        ALU.max).then_inc(mx_set, 1)

            def split_max(gg, bank, count):
                dve.wait_ge(ring_done[bank], count)
                if not (isinstance(gg, int) and gg == 0):
                    dve.wait_ge(mx_in, 32 * gg)
                turned = ps_r[bank][0:GH * KT, 0:P]
                nc.vector.tensor_scalar(max_rows[:, 0, :], turned, -1.0, None, ALU.mult).then_inc(mx_step, 1)
                dve.wait_ge(mx_step, gg + 1)
                nc.vector.scalar_tensor_tensor(out=max_rows[:, 1, :], in0=turned, scalar=-1.0, in1=max_rows[:, 0, :],
                                               op0=ALU.mult, op1=ALU.subtract).then_inc(ring_free[bank], 1)

            def normalise(g, half, bank, count):
                view = ps_r[bank][:].rearrange("p (t j c) -> p (t j) c", t=4, j=GH)
                dve.wait_ge(ring_done[bank], count)
                nc.vector.reciprocal(rsum[:, half], view[:, :, HD]).then_inc(rsum_set, 1)
                dve.wait_ge(rsum_set, 2 * g + half + 1)
                dve.wait_ge(ctx_out[half], 16 * (g + 1))
                nc.vector.tensor_tensor(ctx_n[:, half].rearrange("p t (j d) -> p (t j) d", j=GH), view[:, :, 0:HD],
                                        rsum[:, half].unsqueeze(2).to_broadcast([P, 4 * GH, HD]),
                                        ALU.mult).then_inc(ring_free[bank], 1)

            def step(g, slot, first=False, last=False):
                due = [(u + (what in ("max", "ctx")), what, which, bank, k) for u, what, which, bank, k in plan_of(g)]
                for u in range(EXPS + 1):
                    for _, what, which, bank, k in sorted((d for d in due if d[0] == u), key=lambda d: d[1] in ("scores", "early")):
                        count = used(g, bank) + (k + 1)
                        if what == "early" and which == 0:
                            dve.wait_ge(mx_set, g + 2)
                        if what in ("scores", "early"):
                            reduce_max(which, bank, count)
                        if what == "max":
                            split_max(g + 1, bank, count)
                        if what == "ctx":
                            normalise(g - which, which, bank, count)
                    if u == MAX_BY - 1 and not last:
                        bank, k = find(plan_of(g), "scores", MAX_MM - 1)
                        join_max(g + 1, bank, used(g, bank) + (k + 1))

            dve.wait_ge(consts_in, 48)
            norm_in(0, 0)
            weight_maxima()
            for j in range(TPC):
                low_part(0, j)
            split_weights()
            for n in range(CHUNKS):
                project(n)
            bank, k = find(prologue, "scores", MAX_MM - 1)
            join_max(0, bank, k + 1)
            bank, k = find(prologue, "max", 0)
            split_max(0, bank, k + 1)
            for _, what, w, bank, k in prologue:
                if what == "early":
                    if w == 0:
                        dve.wait_ge(mx_set, 1)
                    reduce_max(w, bank, k + 1)
            steps(dve, step)
            normalise(GROUPS - 1, 1, 0, used(GROUPS, 0) + 1)

        @block.tensor
        def _(pe):
            pe.wait_ge(consts_in, 48)

            def transposes(n, j):
                pe.wait_ge(z_set, TPC * n + j + 1)
                pe.wait_ge(tr_free, TPC * n + j + 1)
                for k in range(KC):
                    tr = nc.tensor.transpose(ps_tr[j % 2][:, k * P:(k + 1) * P], xin[:, n % 2, j, k * P:(k + 1) * P], ident[:])
                tr.then_inc(tr_done, 1)

            def project(n):
                c = n % 2
                pe.wait_ge(tr_free, 2 + TPC * (n + 1))
                if n == CHUNKS - 1:
                    for bank in range(RING):
                        done = sum(b == bank and at < QK_TILES for at, _, _, b, _ in prologue)
                        pe.wait_ge(ring_free[bank], 1 + done)
                for j in range(TPC):
                    pe.wait_ge(v_free, TPC * n + j + 1)
                    t = slice(j * P, (j + 1) * P)
                    for m, (a, w) in enumerate(((z_hi, w_hi), (z_lo, w_hi), (z_hi, w_lo))):
                        for k in range(KC):
                            if n == 0 and j == 0 and m != 1:
                                pe.wait_ge(w_lo_set if m else w_hi_set, k + 1)
                            mm = nc.tensor.matmul(ps_vp[j % 2][:], a[:, c, k, t], w[:, k, 2 * H:3 * H],
                                                  start=(m == 0 and k == 0), stop=(m == 2 and k == KC - 1))
                    mm.then_inc(v_done, 1)
                    if turned_beside_v(n):
                        transposes(n + 1, j)
                if n == CHUNKS - 2:
                    pe.wait_ge(loaded[0], 192)
                    pe.wait_ge(tr_free, 2 + TPC * CHUNKS)
                if n >= CHUNKS - 2:
                    pe.wait_ge(v_free, 2 + TPC * (n + 1))
                for f in range(QK_TILES):
                    beside = beside_qk(n, f)
                    pe.wait_ge(qk_free, QK_TILES * n + f + 1)
                    for m, (w, a) in enumerate(((w_hi, z_hi), (w_hi, z_lo), (w_lo, z_hi))):
                        for k in range(KC):
                            mm = nc.tensor.matmul(ps_qk[f % 4], w[:, k, f * P:(f + 1) * P], a[:, c, k, :],
                                                  start=(m == 0 and k == 0), stop=(m == 2 and k == KC - 1))
                            if (m, k) == (2, KC - 1):
                                mm.then_inc(qk_done, 1)
                            if beside and (KC * m + k + 1) % (3 * KC // PER_QK) == 0:
                                _, _, tile, bank, use = beside.pop(0)
                                max_tile(0, tile, bank, use + 1)
                    if n == 0 and f < TPC:
                        transposes(1, f)

            def max_tile(slot, w, bank, count):
                j, qt, kh = w // (2 * KT), w // 2 % KT, w % 2
                pe.wait_ge(ring_free[bank], count)
                nc.tensor.matmul(ps_r[bank][:], stack[0:STACK, slot, 0, j * SEQ + qt * P:j * SEQ + (qt + 1) * P],
                                 stack[0:STACK, slot, 1, j * SEQ + kh * HALF:j * SEQ + (kh + 1) * HALF],
                                 start=True, stop=True).then_inc(ring_done[bank], 1)

            def turn_max(gg, bank, count):
                pe.wait_ge(mx_set, gg + 1)
                pe.wait_ge(ring_free[bank], count)
                nc.tensor.transpose(ps_r[bank][0:GH * KT, 0:P], maxes[:], ident[:]).then_inc(ring_done[bank], 1)

            def turn_ctx(g, half, bank, count):
                pe.wait_ge(pv_free, 1 + 2 * g + half + 1)
                pe.wait_ge(ring_free[bank], count)
                for t in range(4):
                    tr = nc.tensor.transpose(ps_r[bank][:, t * P:(t + 1) * P], ctx_t[:, t * P:(t + 1) * P], ident[:])
                tr.then_inc(ring_done[bank], 1)

            def scores(g, slot, u):
                half, kt, hp = u // (2 * KT), u // 2 % KT, u % 2
                pe.wait_ge(exp_done, EXPS * g + (u + 1))
                for e in range(2):
                    j = 2 * hp + e
                    mm = nc.tensor.matmul(ps_s[u % 2][:, e * HALF:(e + 1) * HALF],
                                          stack[0:ROWS, slot, 1, j * SEQ + kt * P:j * SEQ + (kt + 1) * P],
                                          stack[0:ROWS, slot, 0, j * SEQ + half * HALF:j * SEQ + (half + 1) * HALF],
                                          start=True, stop=True)
                mm.then_inc(st_done, 1)

            def times_v(g, slot, pair):
                half, kt = pair // KT, pair % KT
                pe.wait_ge(exp_done, EXPS * g + (2 * pair + 4))
                if pair == 0:
                    pe.wait_ge(v_staged, g + 1)
                if kt == 0:
                    pe.wait_ge(pv_free, 2 * g + half + 1)
                for j in range(GH):
                    mm = nc.tensor.matmul(ps_c[32 * j:32 * j + 32, :], v_stage[:, slot, kt, j, :],
                                          probs[:, (2 * pair + j // 2) % PROBS, (j % 2) * HALF:(j % 2 + 1) * HALF],
                                          start=(kt == 0), stop=(kt == KT - 1), skip_group_check=True)
                mm.then_inc(pv_done, 1)

            def step(g, slot, first=False, last=False):
                pe.wait_ge(mx_in, 32 * (g + 1))
                nxt, after_it = (slot + 1) % SLOTS, (slot + 2) % SLOTS
                def side_tile(what, which, bank, count):
                    if what == "scores":
                        max_tile(nxt, which, bank, count)
                    if what == "early":
                        if which == 0:
                            pe.wait_ge(loaded[after_it], 192 * loads_by(g + 2, after_it))
                        max_tile(after_it, which, bank, count)
                    if what == "max":
                        turn_max(g + 1, bank, count)
                    if what == "ctx":
                        turn_ctx(g - which, which, bank, count)

                for u in range(EXPS):
                    beside = [(what, which, bank, used(g, bank) + (k + 1)) for at, what, which, bank, k in plan_of(g) if at == u]
                    scores(g, slot, u)
                    for use in beside[:BEFORE_V]:
                        side_tile(*use)
                    if (found := pair_at(u)) is not None:
                        before, pair = found
                        if not before:
                            times_v(g, slot, pair)
                        elif not first:
                            times_v(g - 1, (slot - 1) % SLOTS, pair)
                    for use in beside[BEFORE_V:]:
                        side_tile(*use)

            def loads_by(g, slot):
                return (g - slot) // SLOTS + 1

            for j in range(TPC):
                transposes(0, j)
            for n in range(CHUNKS):
                project(n)
            pe.wait_ge(qk_free, 4 + QK_TILES * CHUNKS)
            pe.wait_ge(loaded[1], 192)
            pe.wait_ge(stage_const, 2 + SLOTS)
            for _, what, w, bank, k in prologue:
                if what == "early":
                    max_tile(1, w, bank, k + 1)
                if what == "max":
                    turn_max(0, bank, k + 1)
            steps(pe, step)
            for pair in (PAIRS - 2, PAIRS - 1):
                times_v(GROUPS - 1, 0, pair)
            turn_ctx(GROUPS - 1, 1, 0, used(GROUPS, 0) + 1)


def layers_block(nc, x, ctx_dram, wo_hi, wo_lo, wo_scale, first_chunk, b_o, w_0, b_0, w_gu, point, w_terms, discount, w_g, w_u, w_d, w_ra, w_b,
                 ident, out):
    F = w_g.shape[1]
    FB = -(-F // P)
    F_LAST = F - (FB - 1) * P
    S = w_gu.shape[1] // 2
    G = w_terms.shape[1] - 1
    TERMS = G + 1
    GRAD_ORDER_MIN, THD = 4, 2.5
    RA = w_ra.shape[1]
    E = 4
    R = (RA - E) // E
    LORA_SCALE = 4.0
    CTX_BITS = 4
    O_, F0, L1, L3 = range(4)
    ROUTE_EXP, ROUTE_STEPS = 9, 20
    T_COLS, H_COLS = TERMS * CHUNK, FB * CHUNK
    assert S == P

    with ExitStack() as ctx:
        def sb(name, shape, dt):
            return ctx.enter_context(nc.sbuf_tensor(name, shape, dt))

        def psum(name, shape, dt=F32):
            return ctx.enter_context(nc.psum_tensor(name, shape, dt))

        def sem(name):
            return ctx.enter_context(nc.semaphore(name))

        xs = sb("xs", [P, TOKENS // P, H], F32)
        zf = first_chunk
        z_hi = sb("zz_hi", [P, 2, KC, CHUNK], F16)
        z_lo = sb("zz_lo", [P, 2, KC, CHUNK], F16)
        y = sb("yy", [P, TPC, H], F32)
        work = sb("work", [P, T_COLS + H_COLS], F32)
        terms = work[:, 0:T_COLS].rearrange("p (m t) -> p m t", m=TERMS)
        hidden = work[:, T_COLS:T_COLS + H_COLS].rearrange("p (f t) -> p f t", f=FB)
        wd = sb("wd", [P, FB, H], F32)
        wt = sb("wt", [P, TERMS, H], F32)
        wb = sb("wb", [P, H], F32)
        wdims = {"0": H, "gu": 2 * S, "ra": RA, "g": F, "u": F}
        names = [*wdims, "d"]
        hi = {k: sb(f"hi_{k}", [P, KC, n], F16) for k, n in wdims.items()}
        lo = {k: sb(f"lo_{k}", [P, KC, n], F16) for k, n in wdims.items()}
        hi["o"], lo["o"] = wo_hi, wo_lo
        wd_f16 = wd[:].rearrange("p f n -> p (f n)").bitcast(F16).rearrange("p (w f n) -> p w f n", w=2, f=FB)
        hi["d"], lo["d"] = wd_f16[:, 0], wd_f16[:, 1]
        h_f16 = work[:, T_COLS:T_COLS + H_COLS].bitcast(F16).rearrange("p (w f t) -> p w f t", w=2, f=FB)
        h_hi, h_lo = h_f16[:, 0], h_f16[:, 1]
        wide_max = sb("wide_max", [P, 2, KC], F32)
        d_max = sb("d_max", [P, FB // 2 + 1], F32)
        h_scale = sb("h_scale", [P, 5], F32)
        w_amax = sb("w_amax", [P, len(names), 3], F32)
        w_scale = sb("w_scale", [P, len(names), 2], F32)
        bo = sb("bo", [P, H], F32)
        b0 = sb("b0", [P, H], F32)
        lp = sb("lp", [P, 1], F32)
        disc = sb("disc", [P, G], F32)
        ones = sb("ones", [P, P], F32)
        half = sb("half", [P, TPC], F32)
        eps = sb("eps", [P, TPC], F32)
        turn = sb("turn", [P, 1], F32)
        st_x = sb("st_x", [P, TPC, 6], F32)
        mv_x = sb("mv_x", [P, TPC, 2], F32)
        rs_x = sb("rs_x", [P, TPC], F32)
        nm_x = sb("nm_x", [P, TPC], F32)
        minus = sb("minus", [P, TPC], F32)
        st_y = sb("st_y", [P, TPC, 6], F32)
        mv_y = sb("mv_y", [P, TPC, 2], F32)
        rs_y = sb("rs_y", [P, TPC], F32)
        c_amax = sb("c_amax", [P, TPC], F32)
        c_exp = sb("c_exp", [P, TPC], F32)
        c_scale = sb("c_scale", [P, TPC], F32)
        c_inv = sb("c_inv", [P, 3, TPC], F32)
        delta, kept = hidden[:, FB - 1, :], hidden[:, FB - 2, :]
        sg = sb("sg", [P, 2, CHUNK], F32)
        lm = work[:, 0:TPC * RA].rearrange("p (j r) -> p j r", j=TPC)
        gt = sb("gt", [P, 6, TPC], F32)
        rank = sb("rank", [P, TPC, E], F32)
        top = sb("top", [P, TPC], F32)
        gates = sb("gates", [P, TPC, E], F32)
        gm = sb("gm", [P, TPC, P], F32)
        gmt = work[:, T_COLS:T_COLS + TPC * P].rearrange("p (j t) -> p j t", j=TPC)

        ps_t = [psum(f"ps_t{i}", [P, 512]) for i in range(2)]
        ps_y = [psum(f"ps_y{i}", [P, 512]) for i in range(2)]
        ps_p = [psum(f"ps_p{i}", [P, 512]) for i in range(4)]

        w_in = {k: sem(f"w_in_{k}") for k in wdims}
        c_in = sem("c_in")
        wt_in = sem("wt_in")
        wd_in = [sem(f"wd_in{i}") for i in range(FB // 2)]
        wide_set = sem("wide_set")
        wd_max = sem("wd_max")
        hs = sem("hs")
        h32 = sem("h32")
        hh = sem("hh")
        xs_in = [sem(f"xs_in{n}") for n in range(CHUNKS)]
        cx_in = [sem(f"cx_in{c}") for c in range(2)]
        mem = sem("mem")
        absd = sem("absd")
        colsum = sem("colsum")
        signed = sem("signed")
        tern = sem("tern")
        quant = sem("quant")
        wa = sem("wa")
        wr = sem("wr")
        we = sem("we")
        ws = sem("ws")
        whi = {k: sem(f"whi_{k}") for k in names}
        w_split = {k: sem(f"w_split_{k}") for k in names}
        wsc = sem("wsc")
        disc_e = sem("disc_e")
        wt_set = sem("wt_set")
        sx, ax, vx, rx = sem("sx"), sem("ax"), sem("vx"), sem("rx")
        mx = sem("mx")
        z_set = sem("zf_set")
        t_done = sem("t_done")
        zh_set = sem("zh_set")
        t_free = sem("t_free")
        y_done = sem("y_done")
        y_free = sem("y_free")
        sy, ay, vy, ry = sem("sy"), sem("ay"), sem("vy"), sem("ry")
        yn = sem("yn")
        x_set = sem("x_set")
        cs = sem("cs")
        gu_done = sem("gu_done")
        dl = sem("dl")
        p_done = sem("p_done")
        sg_set = sem("sg_set")
        h_set = sem("h_set")
        r_done = sem("r_done")
        rt = sem("rt")
        ex = sem("ex")
        gm_set = sem("gm_set")
        gt_done = sem("gt_done")
        gt_set = sem("gt_set")
        stored = sem("out_stored")
        block = ctx.enter_context(nc.Block())

        narrow, wide = ["0", "gu", "ra"], ["g", "u"]
        stage_at, at = {}, 0
        for k in ("gu", "ra", "0"):
            stage_at[k] = at
            at += KC * wdims[k]
        stage_at["u"] = stage_at["0"]
        context_at = T_COLS + H_COLS - TPC * H
        assert max(at, stage_at["u"] + KC * F) <= context_at
        chunk_in = [zf, work[:, context_at:].rearrange("p (j f) -> p j f", j=TPC)]
        wd_flat = wd[:].rearrange("p f n -> p (f n)")

        def staged(k):
            if k == "g":
                return wd_flat[:, 0:KC * F]
            return work[:, stage_at[k]:stage_at[k] + KC * wdims[k]]

        def kpn(w):
            return w.rearrange("(k p) n -> p k n", p=P)

        maxima_after = {0: ["0", "gu"], 1: ["ra"], 2: [], 3: []}
        wide_maxima = {2: "g", 3: "u"}
        t_a, t_b = wd_flat[:, 0:KC * H], wd_flat[:, KC * H:2 * KC * H]
        inv = {k: w_scale[:, names.index(k), 1:2] for k in names}
        inv["o"] = wo_scale[:, 1:2]
        assert FB == 10
        f32_blocks = lambda ap: ap.rearrange("p k n -> p (k n)").bitcast(F32).rearrange("p (f n) -> p f n", f=2)
        d_stage = [f32_blocks(w[:]) for w in (hi["o"], lo["o"], hi["0"], lo["0"])] + [sg[:]]
        d_pieces = [(d_stage[i][:], slice(2 * i, 2 * i + 2), P) for i in range(FB // 2 - 1)]
        d_pieces += [(sg[:, 0:1, :], slice(FB - 2, FB - 1), P), (sg[0:F_LAST, 1:2, :], slice(FB - 1, FB), F_LAST)]
        WIDE_FLOOR = 2.0 ** -20
        H_SCALE = 2.0 ** (16 - 2 * 9 - 2 * (W_BITS + 1) - 1)

        assert KC == CHUNKS

        def wide_blocks(layer, n):
            return [("g", n), ("u", n)] if layer == F0 else []

        def block_of(k, n):
            one = lambda ap: ap[:, n, :] if isinstance(n, int) else ap[:, bass.ds(n, 1), :].rearrange("p a f -> p (a f)")
            return one(staged(k).rearrange("p (k n) -> p k n", k=KC)), one(hi[k]), one(lo[k])

        def x_tile(n, j):
            if isinstance(n, int):
                return xs[:, TPC * n + j, :]
            return xs[:, bass.ds(TPC * n + j, 1), :].rearrange("p a f -> p (a f)")

        def has_stage(ahead, layer, n):
            return layer != L3 or n + ahead < CHUNKS

        def layer_loops(engine, stage, take_maximum=lambda k: None, scale_weight=lambda k: None,
                        before=lambda layer: None):
            before(O_)
            for n in range(CHUNKS):
                stage(n, O_, n, n % 2)
                for k in maxima_after.get(n - 1, ()):
                    scale_weight(k)
                if n in wide_maxima:
                    scale_weight(wide_maxima[n])
                for k in maxima_after[n]:
                    take_maximum(k)
            for layer in (F0, L1):
                before(layer)
                with engine.Fori(0, CHUNKS // 2) as i:
                    for c in range(2):
                        stage(CHUNKS * layer + c + 2 * i, layer, 2 * i + c, c)
            before(L3)
            for n in range(CHUNKS):
                stage(CHUNKS * L3 + n, L3, n, n % 2)

        @block.sync
        def _(sp):
            def load_context(n):
                if n >= 2:
                    sp.wait_ge(t_done, TPC * (n - 1))
                sp.dma_start(chunk_in[n % 2][:], ctx_dram[n * CHUNK:(n + 1) * CHUNK, :].rearrange("(j p) f -> p j f", p=P)
                             ).then_inc(cx_in[n % 2], 16)

            for dst, src in ((bo[:], b_o.to_broadcast([P, H])), (b0[:], b_0.to_broadcast([P, H])),
                             (lp[:], point), (disc[:], discount.to_broadcast([P, G]))):
                sp.dma_start(dst, src).then_inc(c_in, 16)

            load_context(1)
            load_context(2)
            for n in range(CHUNKS):
                sp.dma_start(xs[:, n * TPC:(n + 1) * TPC, :],
                             x[n * CHUNK:(n + 1) * CHUNK, :].rearrange("(j p) f -> p j f", p=P)).then_inc(xs_in[n], 16)
            sp.wait_ge(quant, 3)
            sp.dma_start(staged("g").rearrange("p (k n) -> p k n", k=KC), kpn(w_g)).then_inc(w_in["g"], 16)
            load_context(3)
            sp.wait_ge(w_split["0"], 1)
            sp.dma_start(staged("u").rearrange("p (k n) -> p k n", k=KC), kpn(w_u)).then_inc(w_in["u"], 16)
            for i in range(FB // 2):
                sp.wait_ge(y_done, TPC * CHUNKS if i < 2 else 2 * TPC * CHUNKS)
                if i < FB // 2 - 1:
                    sp.dma_start(d_stage[i], w_d[2 * i * P:2 * (i + 1) * P, :].rearrange("(f p) n -> p f n", p=P)
                                 ).then_inc(wd_in[i], 16)
                else:
                    sp.dma_start(sg[:, 0, :], w_d[(FB - 2) * P:(FB - 1) * P, :]).then_inc(wd_in[i], 16)
                    sp.dma_start(sg[0:F_LAST, 1, :], w_d[(FB - 1) * P:F, :]).then_inc(wd_in[i], 16)
            sp.wait_ge(mem, 7)
            for n in range(CHUNKS - 1):
                sp.wait_ge(x_set, TPC * (CHUNKS * L3 + n + 1))
                sp.dma_start(out[n * CHUNK:(n + 1) * CHUNK, :].rearrange("(j p) f -> p j f", p=P),
                             xs[:, n * TPC:(n + 1) * TPC, :]).then_inc(stored, 16)
            for t in range(TOKENS // P - TPC, TOKENS // P):
                sp.wait_ge(x_set, TPC * CHUNKS * L3 + t + 1)
                sp.dma_start(out[t * P:(t + 1) * P, :], xs[:, t, :]).then_inc(stored, 16)
            sp.wait_ge(stored, 16 * (CHUNKS - 1 + TPC))

        @block.gpsimd
        def _(pool):
            nc.gpsimd.memset(half[:], -0.5).then_inc(mem, 1)
            nc.gpsimd.memset(eps[:], EPS).then_inc(mem, 1)
            nc.gpsimd.memset(ones[:], 1.0).then_inc(mem, 1)
            nc.gpsimd.memset(gm[:], 0.0).then_inc(mem, 1)
            nc.gpsimd.memset(wb[:], 0.0).then_inc(mem, 1)
            nc.gpsimd.memset(minus[:], -1.0).then_inc(mem, 1)
            nc.gpsimd.memset(d_max[:], 0.0).then_inc(mem, 1)
            pool.wait_ge(w_in["0"], 16)
            for k, w in (("gu", w_gu), ("ra", w_ra)):
                nc.gpsimd.dma_start(staged(k).rearrange("p (k n) -> p k n", k=KC), kpn(w)).then_inc(w_in[k], 16)
            nc.gpsimd.dma_start(wt[:], w_terms).then_inc(wt_in, 16)
            pool.wait_ge(mem, 7)
            nc.gpsimd.dma_start(wb[0:E * R, :], w_b).then_inc(wt_in, 16)

            def take_maximum(k):
                a = w_amax[:, names.index(k)]
                pool.wait_ge(wa, names.index(k) + 1)
                nc.gpsimd.partition_all_reduce(a[:, 1:2], a[:, 0:1], P, RMAX).then_inc(wr, 1)

            pool.wait_ge(signed, 1)
            pool.wait_ge(tern, 2)
            nc.gpsimd.tensor_tensor(t_a, t_a, t_b, ALU.mult).then_inc(quant, 1)
            pool.wait_ge(quant, 1)
            nc.gpsimd.tensor_tensor(t_a, t_a, staged("0"), ALU.subtract).then_inc(quant, 1)
            pool.wait_ge(quant, 2)
            nc.gpsimd.tensor_tensor(staged("0"), staged("0"), t_a, ALU.add).then_inc(quant, 1)

            def split_block(k, block):
                scaled, high, low = block_of(k, block)
                pool.wait_ge(wsc, block + 1)
                nc.gpsimd.tensor_tensor(low, scaled, high, ALU.subtract).then_inc(w_split[k], 1)

            def inv_std(seen, mv, rs, steps, done, means):
                pool.wait_ge(means, TPC * (seen + 1))
                nc.gpsimd.tensor_tensor(rs[:], mv[:, :, 1], eps[:], ALU.add).then_inc(steps, 1)
                pool.wait_ge(steps, seen + 1)
                nc.gpsimd.tensor_tensor(rs[:], rs[:], half[:], ALU.pow).then_inc(done, 1)

            def minus_mean(seen):
                nc.gpsimd.tensor_tensor(nm_x[:], mv_x[:, :, 0], minus[:], ALU.mult).then_inc(mx, 1)
                pool.wait_ge(mx, 2 * seen + 1)
                pool.wait_ge(rx, seen + 1)
                nc.gpsimd.tensor_tensor(nm_x[:], nm_x[:], rs_x[:], ALU.mult).then_inc(mx, 1)

            def stage(s, layer, n, c):
                for k, block in wide_blocks(layer, n):
                    if k == "g":
                        split_block(k, block)
                if layer == O_ and n in wide_maxima:
                    take_maximum(wide_maxima[n])
                inv_std(s, mv_y, rs_y, vy, ry, ay)
                if has_stage(3, layer, n) and not (layer == O_ and n == 0):
                    inv_std(s + 3 - CHUNKS, mv_x, rs_x, vx, rx, ax)
                    minus_mean(s + 3 - CHUNKS)
                if layer == O_:
                    pool.wait_ge(xs_in[n], 16)
                for j in range(TPC):
                    pool.wait_ge(yn, TPC * s + (j + 1))
                    nc.gpsimd.tensor_tensor(x_tile(n, j), x_tile(n, j), y[:, j, :], ALU.add).then_inc(x_set, 1)

            def before(layer):
                if layer == L1:
                    take_maximum("d")

            layer_loops(pool, stage, take_maximum, before=before)

        @block.scalar
        def _(act):
            nc.scalar.dma_start(staged("0").rearrange("p (k n) -> p k n", k=KC), kpn(w_0)).then_inc(w_in["0"], 16)

            def scale_weight(k):
                if k in narrow:
                    act.wait_ge(ws, 2 * (names.index(k) + 1))
                    nc.scalar.activation(hi[k][:].rearrange("p k n -> p (k n)"), staged(k), ACT.Copy,
                                         scale=w_scale[:, names.index(k), 0:1]).then_inc(whi[k], 1)

            def high_part(s, c, j):
                act.wait_ge(t_done, TPC * s + (j + 1))
                nc.scalar.activation(z_hi[:, c, :, j * P:(j + 1) * P],
                                     ps_t[j % 2][:].rearrange("p (k t) -> p k t", k=KC), ACT.Copy,
                                     scale=Z_SCALE).then_inc(zh_set, 1)

            def normalise(s, n, j):
                act.wait_ge(mx, 2 * (s - CHUNKS + 1))
                act.wait_ge(t_done, TPC * (s - 1) + (j + 1))
                nc.scalar.activation(zf[:, j, :], x_tile(n, j), ACT.Identity, bias=nm_x[:, j:j + 1],
                                     scale=rs_x[:, j:j + 1]).then_inc(z_set, 1)

            def copy_out(s, j, scale=1.0):
                act.wait_ge(y_done, TPC * s + (j + 1))
                act.wait_ge(x_set, TPC * s - 3 + j)
                nc.scalar.activation(y[:, j, :], ps_y[j % 2][:], ACT.Copy, scale=scale).then_inc(y_free, 1)

            def stage(s, layer, n, c):
                if layer == L1:
                    for f in range(FB):
                        rows = P if f < FB - 1 else F_LAST
                        k = (s - CHUNKS * L1) * FB + f
                        act.wait_ge(p_done, 2 * k + 1)
                        act.wait_ge(h_set, k + 1)
                        nc.scalar.activation(sg[0:rows, f % 2, :], ps_p[2 * (f % 2)][0:rows, :], ACT.Silu,
                                             scale=inv["g"][0:rows, :]).then_inc(sg_set, 1)
                        act.wait_ge(h32, k + 1)
                        nc.scalar.copy(h_hi[0:rows, f, :], sg[0:rows, f % 2, :]).then_inc(hh, 1)
                if layer == L3:
                    for j in range(TPC):
                        act.wait_ge(gt_done, TPC * n + j + 1)
                        nc.scalar.copy(gmt[:, j, :], ps_p[1 + j % 2][:, 0:P]).then_inc(gt_set, 1)
                for pair in ((0, 1), (2, 3)):
                    for j in pair:
                        if has_stage(1, layer, n):
                            high_part(s + 1, 1 - c, j)
                        if layer == L1:
                            copy_out(s, j, h_scale[:, 4:5])
                    if has_stage(2, layer, n) and not (layer == O_ and n < 2):
                        for j in pair:
                            normalise(s + 2, (n + 2) % CHUNKS, j)
                    for j in pair if layer == L3 else ():
                        copy_out(s, j)
                    if layer == L3 and pair == (2, 3) and has_stage(1, layer, n):
                        exp_logits(n + 1)
                    for k, block in wide_blocks(layer, n)[pair[0] // 2:pair[0] // 2 + 1]:
                        scaled, high, _ = block_of(k, block)
                        scale = w_scale[:, names.index(k), 0:1]
                        act.wait_ge(ws, 2 * (names.index(k) + 1))
                        nc.scalar.activation(high, scaled, ACT.Copy, scale=scale).then_inc(whi[k], 1)
                        if k == "g":
                            nc.scalar.activation(scaled, scaled, ACT.Copy, scale=scale).then_inc(wsc, 1)

            def exp_logits(n):
                act.wait_ge(rt, ROUTE_STEPS * n + ROUTE_EXP)
                nc.scalar.activation(gates[:], gates[:], ACT.Exp).then_inc(ex, 1)

            def before(layer):
                if layer == L3:
                    exp_logits(0)
                if layer == L1:
                    act.wait_ge(c_in, 64)
                    nc.scalar.activation(disc[:], disc[:], ACT.Exp, scale=-1.0).then_inc(disc_e, 1)
                    act.wait_ge(ws, 2 * len(names))
                    for piece, blocks, rows in d_pieces:
                        nc.scalar.activation(hi["d"][0:rows, blocks, :], piece, ACT.Copy,
                                             scale=w_scale[0:rows, names.index("d"), 0:1]).then_inc(whi["d"], 1)
                    act.wait_ge(hs, 6)
                    act.wait_ge(wt_in, 32)
                    nc.scalar.activation(wt[:, 0, :], wt[:, 0, :], ACT.Copy, scale=h_scale[:, 2:3]).then_inc(wt_set, 1)
                    for m in range(G):
                        nc.scalar.activation(wt[:, m + 1, :], wt[:, m + 1, :], ACT.Copy, scale=disc[:, m:m + 1]).then_inc(wt_set, 1)
                    act.wait_ge(w_split["d"], len(d_pieces))

            for j in range(TPC):
                high_part(0, 0, j)
            act.wait_ge(w_in["0"], 16)
            nc.scalar.activation(t_a, staged("0"), ACT.Abs).then_inc(absd, 1)
            nc.scalar.activation(t_b, staged("0"), ACT.Sign).then_inc(signed, 1)
            layer_loops(act, stage, scale_weight=scale_weight, before=before)

        @block.vector
        def _(dve):
            for credits, count in ((t_free, 2), (y_free, 2), (h_set, 2)):
                dve.sem_inc(credits, count)

            def take_maximum(k):
                if k == "0":
                    dve.wait_ge(quant, 3)
                dve.wait_ge(w_in[k], 16)
                nc.vector.tensor_reduce(w_amax[:, names.index(k), 0:1], staged(k), AX_X, ALU.max,
                                        apply_absolute_value=True).then_inc(wa, 1)

            def scale_weight(k):
                m = names.index(k)
                a, sc = w_amax[:, m], w_scale[:, m]
                dve.wait_ge(wr, m + 1)
                floor = TINY if k in narrow else WIDE_FLOOR
                nc.vector.tensor_scalar(a[:, 1:2], a[:, 1:2], floor, None, ALU.max).then_inc(we, 1)
                dve.wait_ge(we, 2 * m + 1)
                nc.vector.tensor_single_scalar(a[:, 2:3].bitcast(I32), a[:, 1:2].bitcast(I32), EXP_MASK,
                                               ALU.bitwise_and).then_inc(we, 1)
                dve.wait_ge(we, 2 * m + 2)
                nc.vector.tensor_scalar(sc[:, 0:1].bitcast(I32), a[:, 2:3].bitcast(I32), -1.0, SCALE_FROM_EXP,
                                        ALU.mult, ALU.add).then_inc(ws, 1)
                nc.vector.tensor_scalar(sc[:, 1:2].bitcast(I32), a[:, 2:3].bitcast(I32), INV_FROM_EXP, None,
                                        ALU.add).then_inc(ws, 1)
                dve.wait_ge(ws, 2 * m + 2)
                if k in narrow:
                    dve.wait_ge(whi[k], 1)
                    nc.vector.scalar_tensor_tensor(out=lo[k][:].rearrange("p k n -> p (k n)"), in0=staged(k),
                                                   scalar=sc[:, 0:1], in1=hi[k][:].rearrange("p k n -> p (k n)"),
                                                   op0=ALU.mult, op1=ALU.subtract).then_inc(w_split[k], 1)

            def ternary():
                k3 = t_a.rearrange("p (k n) -> p k n", k=KC)
                dve.wait_ge(colsum, 1)
                nc.vector.tensor_scalar(sg[:, 0, :], ps_y[0][:], 1.0 / H, 0.7, ALU.mult, ALU.mult).then_inc(tern, 1)
                dve.wait_ge(tern, 1)
                nc.vector.tensor_tensor(k3, k3, sg[:, 0:1, :].to_broadcast([P, KC, H]), ALU.is_gt).then_inc(tern, 1)

            def scale_context(n, c):
                if n:
                    dve.wait_ge(cx_in[c], 16 * ((n + 1) // 2))
                nc.vector.tensor_reduce(c_amax[:], chunk_in[c][:], AX_X, ALU.max, apply_absolute_value=True).then_inc(cs, 1)
                dve.wait_ge(cs, 6 * n + 1)
                nc.vector.tensor_scalar(c_amax[:], c_amax[:], TINY, None, ALU.max).then_inc(cs, 1)
                dve.wait_ge(cs, 6 * n + 2)
                nc.vector.tensor_single_scalar(c_exp[:].bitcast(I32), c_amax[:].bitcast(I32), EXP_MASK,
                                               ALU.bitwise_and).then_inc(cs, 1)
                dve.wait_ge(cs, 6 * n + 3)
                nc.vector.tensor_scalar(c_scale[:].bitcast(I32), c_exp[:].bitcast(I32), -1.0,
                                        float((254 + CTX_BITS) << 23), ALU.mult, ALU.add).then_inc(cs, 1)
                nc.vector.tensor_scalar(c_inv[:, n % 3, :].bitcast(I32), c_exp[:].bitcast(I32), -float(CTX_BITS << 23), None,
                                        ALU.add).then_inc(cs, 1)
                dve.wait_ge(cs, 6 * n + 5)
                nc.vector.tensor_scalar(c_inv[:, n % 3, :], c_inv[:, n % 3, :], inv["o"], None, ALU.mult).then_inc(cs, 1)
                for j in range(TPC):
                    nc.vector.tensor_scalar(chunk_in[c][:, j, :], chunk_in[c][:, j, :], c_scale[:, j:j + 1], None,
                                            ALU.mult).then_inc(z_set, 1)

            def x_stats(s, n):
                seen = s - CHUNKS
                dve.wait_ge(x_set, TPC * (seen + 1))
                for j in range(TPC):
                    nc.vector.bn_stats(st_x[:, j, :], x_tile(n, j)).then_inc(sx, 1)
                dve.wait_ge(sx, TPC * (seen + 1))
                dve.wait_ge(z_set, TPC * s)
                nc.vector.memset(turn[:], 0.0)
                for j in range(TPC):
                    nc.vector.bn_aggr(mv_x[:, j, :], st_x[:, j, :]).then_inc(ax, 1)

            def low_part(s, c, j):
                dve.wait_ge(zh_set, TPC * s + (j + 1))
                nc.vector.scalar_tensor_tensor(
                    out=z_lo[:, c, :, j * P:(j + 1) * P], in0=ps_t[j % 2][:].rearrange("p (k t) -> p k t", k=KC),
                    scalar=Z_SCALE, in1=z_hi[:, c, :, j * P:(j + 1) * P], op0=ALU.mult,
                    op1=ALU.subtract).then_inc(t_free, 1)

            def make_terms(q):
                DL = TERMS + 4
                dve.wait_ge(gu_done, q + 1)
                nc.vector.tensor_scalar(delta, ps_y[0][:], inv["gu"], lp[:, 0:1], ALU.mult,
                                        ALU.subtract).then_inc(dl, 1)
                nc.vector.tensor_scalar(terms[:, 0, :], ps_y[1][:], inv["gu"], None, ALU.mult).then_inc(dl, 1)
                dve.wait_ge(dl, DL * q + 2)
                nc.vector.tensor_single_scalar(kept, delta, THD, ALU.is_le).then_inc(dl, 1)
                dve.wait_ge(dl, DL * q + 3)
                nc.vector.scalar_tensor_tensor(out=kept, in0=delta, scalar=-THD, in1=kept, op0=ALU.is_ge,
                                               op1=ALU.mult).then_inc(dl, 1)
                dve.wait_ge(dl, DL * q + 4)
                nc.vector.tensor_tensor(kept, kept, delta, ALU.mult).then_inc(dl, 1)
                for m in range(1, TERMS):
                    dve.wait_ge(dl, DL * q + (4 + m))
                    by = kept if m == GRAD_ORDER_MIN + 1 else delta
                    nc.vector.tensor_tensor(terms[:, m, :], terms[:, m - 1, :], by, ALU.mult).then_inc(dl, 1)

            def make_hidden(q, blocks):
                for f in blocks:
                    rows = P if f < FB - 1 else F_LAST
                    k = q * FB + f
                    dve.wait_ge(sg_set, k + 1)
                    dve.wait_ge(p_done, 2 * k + 2)
                    block = sg[0:rows, f % 2, :]
                    nc.vector.scalar_tensor_tensor(out=block, in0=ps_p[2 * (f % 2) + 1][0:rows, :],
                                                   scalar=h_scale[0:rows, 1:2], in1=block, op0=ALU.mult,
                                                   op1=ALU.mult).then_inc(h32, 1)
                    dve.wait_ge(hh, k + 1)
                    nc.vector.tensor_tensor(h_lo[0:rows, f, :], block, h_hi[0:rows, f, :], ALU.subtract).then_inc(h_set, 1)

            def route(n):
                base = ROUTE_STEPS * n
                count = [0]

                def done(ins, wait=True):
                    count[0] += 1
                    ins.then_inc(rt, 1)
                    if wait:
                        dve.wait_ge(rt, base + count[0])

                dve.wait_ge(r_done, n + 1)
                done(nc.vector.tensor_scalar(lm, ps_p[0][:, 0:TPC * RA].rearrange("p (j r) -> p j r", j=TPC),
                                             inv["ra"], None, ALU.mult))
                lg = lm[:, :, 0:E]
                pairs = [(a, b) for a in range(E) for b in range(a + 1, E)]
                done(nc.vector.tensor_reduce(top[:], lg, AX_X, ALU.max), wait=False)
                for i, (a, b) in enumerate(pairs):
                    done(nc.vector.tensor_tensor(gt[:, i, :], lg[:, :, b], lg[:, :, a], ALU.is_gt), wait=(i == 5))
                done(nc.vector.tensor_tensor(gates[:], lg, top[:].unsqueeze(2).to_broadcast([P, TPC, E]), ALU.subtract))
                assert count[0] == ROUTE_EXP
                g = lambda a, b: gt[:, pairs.index((a, b)), :]
                chains = [(0, [(g(0, 1), 1), (g(0, 2), 1), (g(0, 3), 1)]), (1, [(g(0, 1), -1), (g(1, 2), 1), (g(1, 3), 1)]),
                          (2, [(g(0, 2), -1), (g(1, 2), -1), (g(2, 3), 1)]), (3, [(g(0, 3), -1), (g(1, 3), -1), (g(2, 3), -1)])]
                for step in (1, 2):
                    for e, terms_ in chains:
                        r = rank[:, :, e]
                        if step == 1:
                            (a, sa), (b, sb_) = terms_[0], terms_[1]
                            done(nc.vector.scalar_tensor_tensor(out=r, in0=a, scalar=float(sa), in1=b, op0=ALU.mult,
                                                                op1=ALU.add if sb_ > 0 else ALU.subtract), wait=(e == 3))
                        else:
                            c_, sc_ = terms_[2]
                            done(nc.vector.scalar_tensor_tensor(out=r, in0=r, scalar=float(sum(s < 0 for _, s in terms_)), in1=c_,
                                                                op0=ALU.add, op1=ALU.add if sc_ > 0 else ALU.subtract),
                                 wait=(e == 3))
                dve.wait_ge(ex, n + 1)
                done(nc.vector.scalar_tensor_tensor(out=gates[:], in0=rank[:], scalar=2.0, in1=gates[:], op0=ALU.is_lt,
                                                    op1=ALU.mult))
                done(nc.vector.tensor_reduce(top[:], gates[:], AX_X, ALU.add))
                done(nc.vector.reciprocal(top[:], top[:]))
                assert count[0] == ROUTE_STEPS, count
                nc.vector.scalar_tensor_tensor(out=gates[:], in0=gates[:], scalar=LORA_SCALE,
                                               in1=top[:].unsqueeze(2).to_broadcast([P, TPC, E]), op0=ALU.mult,
                                               op1=ALU.mult).then_inc(gm_set, 1)
                dve.wait_ge(gm_set, (1 + TPC) * n + 1)
                dve.wait_ge(mem, 7)
                for j in range(TPC):
                    nc.vector.tensor_tensor(gm[:, j, 0:E * R].rearrange("p (e r) -> p e r", e=E),
                                            lm[:, j, E:RA].rearrange("p (e r) -> p e r", e=E),
                                            gates[:, j, :].unsqueeze(2).to_broadcast([P, E, R]),
                                            ALU.mult).then_inc(gm_set, 1)

            def y_stats(s, layer, c, j):
                if layer in (O_, F0):
                    dve.wait_ge(y_done, TPC * s + (j + 1))
                    if not (layer == O_ and s == 0):
                        dve.wait_ge(x_set, TPC * s - 3 + j)
                    nc.vector.scalar_tensor_tensor(out=y[:, j, :], in0=ps_y[j % 2][:],
                                                   scalar=c_inv[:, s % 3, j:j + 1] if layer == O_ else inv["0"],
                                                   in1=(bo if layer == O_ else b0)[:], op0=ALU.mult,
                                                   op1=ALU.add).then_inc(y_free, 1)
                dve.wait_ge(y_free, 2 + TPC * s + (j + 1))
                nc.vector.bn_stats(st_y[:, j, :], y[:, j, :]).then_inc(sy, 1)

            def stage(s, layer, n, c):
                if layer == L1:
                    q = s - CHUNKS * L1
                    make_hidden(q, [0])
                    make_terms(q)
                    make_hidden(q, range(1, FB))
                for pair in ((0, 1), (2, 3)):
                    for j in pair:
                        if has_stage(1, layer, n):
                            low_part(s + 1, 1 - c, j)
                        if layer != L3:
                            y_stats(s, layer, c, j)
                    for j in pair if layer == L3 else ():
                        y_stats(s, layer, c, j)
                    if layer == O_ and n in wide_maxima:
                        k = wide_maxima[n]
                        dve.wait_ge(w_in[k], 16)
                        for block in pair:
                            nc.vector.tensor_reduce(wide_max[:, n % 2, block:block + 1],
                                                    staged(k)[:, block * F:(block + 1) * F], AX_X, ALU.max,
                                                    apply_absolute_value=True).then_inc(wide_set, 1)
                    if layer == O_ and n < 2 and pair == (0, 1):
                        scale_context(n + 2, c)
                if layer == O_ and n in wide_maxima:
                    dve.wait_ge(wide_set, KC * (n - 1))
                    nc.vector.tensor_reduce(w_amax[:, names.index(wide_maxima[n]), 0:1], wide_max[:, n % 2, :], AX_X,
                                            ALU.max).then_inc(wa, 1)
                dve.wait_ge(sy, TPC * (s + 1))
                nc.vector.memset(turn[:], 0.0)
                for j in range(TPC):
                    nc.vector.bn_aggr(mv_y[:, j, :], st_y[:, j, :]).then_inc(ay, 1)
                if has_stage(3, layer, n) and not (layer == O_ and n == 0):
                    x_stats(s + 3, (n + 3) % CHUNKS)
                if layer == L3 and has_stage(1, layer, n):
                    route(n + 1)
                for k, block in wide_blocks(layer, n):
                    if k == "u":
                        staged_block, high, low = block_of(k, block)
                        dve.wait_ge(whi[k], block + 1)
                        nc.vector.scalar_tensor_tensor(out=low, in0=staged_block, scalar=w_scale[:, names.index(k), 0:1],
                                                       in1=high, op0=ALU.mult, op1=ALU.subtract).then_inc(w_split[k], 1)
                dve.wait_ge(ry, s + 1)
                for j in range(TPC):
                    nc.vector.tensor_scalar(y[:, j, :], y[:, j, :], mv_y[:, j, 0:1], rs_y[:, j:j + 1], ALU.subtract,
                                            ALU.mult).then_inc(yn, 1)

            def before(layer):
                if layer == L3:
                    route(0)
                if layer == L1:
                    dve.wait_ge(w_split["u"], KC)
                    dve.wait_ge(w_split["g"], KC)
                    for i, (piece, _, rows) in enumerate(d_pieces):
                        buffer = min(i, FB // 2 - 1)
                        dve.wait_ge(wd_in[buffer], 16 if buffer == i and buffer < FB // 2 - 1 else 32)
                        nc.vector.tensor_reduce(d_max[0:rows, i:i + 1], piece.rearrange("p f n -> p (f n)"), AX_X, ALU.max,
                                                apply_absolute_value=True).then_inc(wd_max, 1)
                    dve.wait_ge(wd_max, len(d_pieces))
                    nc.vector.tensor_reduce(w_amax[:, names.index("d"), 0:1], d_max[:], AX_X, ALU.max).then_inc(wa, 1)
                    scale_weight("d")
                    scale_of = lambda k: w_scale[:, names.index(k), 0:1]
                    nc.vector.scalar_tensor_tensor(out=h_scale[:, 0:1], in0=scale_of("g"), scalar=H_SCALE, in1=scale_of("u"),
                                                   op0=ALU.mult, op1=ALU.mult).then_inc(hs, 1)
                    nc.vector.scalar_tensor_tensor(out=h_scale[:, 3:4], in0=inv["g"],
                                                   scalar=4.0 ** (W_BITS + Z_BITS) / H_SCALE / 4.0 ** W_BITS,
                                                   in1=inv["u"], op0=ALU.mult, op1=ALU.mult).then_inc(hs, 1)
                    dve.wait_ge(hs, 2)
                    dve.wait_ge(ws, 2 * len(names))
                    nc.vector.tensor_tensor(h_scale[:, 1:2], h_scale[:, 0:1], inv["u"], ALU.mult).then_inc(hs, 1)
                    nc.vector.tensor_tensor(h_scale[:, 2:3], h_scale[:, 0:1], scale_of("d"), ALU.mult).then_inc(hs, 1)
                    nc.vector.scalar_tensor_tensor(out=h_scale[:, 4:5], in0=h_scale[:, 3:4], scalar=float(2 ** Z_BITS),
                                                   in1=inv["d"], op0=ALU.mult, op1=ALU.mult).then_inc(hs, 1)
                    dve.wait_ge(hs, 5)
                    dve.wait_ge(disc_e, 1)
                    nc.vector.tensor_scalar(disc[:], disc[:], h_scale[:, 2:3], None, ALU.mult).then_inc(hs, 1)
                    for i, (piece, blocks, rows) in enumerate(d_pieces):
                        dve.wait_ge(whi["d"], i + 1)
                        nc.vector.scalar_tensor_tensor(out=lo["d"][0:rows, blocks, :], in0=piece,
                                                       scalar=scale_of("d")[0:rows, :], in1=hi["d"][0:rows, blocks, :],
                                                       op0=ALU.mult, op1=ALU.subtract).then_inc(w_split["d"], 1)

            scale_context(0, 0)
            for j in range(TPC):
                low_part(0, 0, j)
            scale_context(1, 1)
            ternary()
            dve.wait_ge(c_in, 64)
            layer_loops(dve, stage, take_maximum, scale_weight, before)

        @block.tensor
        def _(pe):
            def transposes(s, j, src=zf):
                pe.wait_ge(z_set, TPC * s + (j + 1))
                pe.wait_ge(t_free, TPC * s + (j + 1))
                for k in range(KC):
                    tr = nc.tensor.transpose(ps_t[j % 2][:, k * P:(k + 1) * P], src[:, j, k * P:(k + 1) * P], ident[:])
                tr.then_inc(t_done, 1)

            def by_tokens(dst, key, c, j, cols, start=True, stop=True):
                t = slice(j * P, (j + 1) * P)
                for m, (a, w) in enumerate(((z_hi, hi[key]), (z_hi, lo[key]), (z_lo, hi[key]))):
                    for k in range(KC):
                        mm = nc.tensor.matmul(dst, a[:, c, k, t], w[:, k, cols], start=(m == 0 and k == 0),
                                              stop=(m == 2 and k == KC - 1))
                return mm

            def by_columns(dst, key, c, cols):
                for m, (w, a) in enumerate(((hi[key], z_hi), (hi[key], z_lo), (lo[key], z_hi))):
                    for k in range(KC):
                        mm = nc.tensor.matmul(dst, w[:, k, cols], a[:, c, k, :], start=(m == 0 and k == 0),
                                              stop=(m == 2 and k == KC - 1))
                return mm

            def project(q, c, f):
                rows = P if f < FB - 1 else F_LAST
                cols = slice(f * P, f * P + rows)
                pe.wait_ge(h_set, q * FB + (f + 1))
                by_columns(ps_p[2 * (f % 2)][0:rows, :], "g", c, cols).then_inc(p_done, 1)
                by_columns(ps_p[2 * (f % 2) + 1][0:rows, :], "u", c, cols).then_inc(p_done, 1)

            def stage(s, layer, n, c):
                q = s - CHUNKS * L1
                if layer != L3:
                    pe.wait_ge(t_free, 2 + TPC * (s + 1))
                if layer == L1:
                    project(q, c, 0)
                    pe.wait_ge(y_free, TPC * s + 2)
                    by_columns(ps_y[0][:], "gu", c, slice(0, S))
                    by_columns(ps_y[1][:], "gu", c, slice(S, 2 * S)).then_inc(gu_done, 1)
                    for f in range(1, FB):
                        project(q, c, f)
                    pe.wait_ge(dl, (TERMS + 4) * (q + 1))
                if layer == L3:
                    for j in range(TPC):
                        pe.wait_ge(gm_set, (1 + TPC) * n + j + 2)
                        if TPC * n + j >= 2:
                            pe.wait_ge(gt_set, TPC * n + j - 1)
                        nc.tensor.transpose(ps_p[1 + j % 2][:, 0:P], gm[:, j, :], ident[:]).then_inc(gt_done, 1)
                    for pair in ((0, 1), (2, 3)):
                        for j in pair:
                            if has_stage(1, layer, n):
                                transposes(s + 1, j)
                        for j in pair:
                            pe.wait_ge(gt_set, TPC * n + j + 1)
                            pe.wait_ge(y_free, TPC * s + (j + 1))
                            nc.tensor.matmul(ps_y[j % 2][:], gmt[:, j, :], wb[:], start=True, stop=True).then_inc(y_done, 1)
                    if has_stage(1, layer, n):
                        logits(s + 1, 1 - c)
                for j in range(TPC) if layer != L3 else ():
                    transposes(s + 1, j, chunk_in[1 - c] if layer == O_ and n < CHUNKS - 1 else zf)
                    pe.wait_ge(y_free, TPC * s + (j + 1))
                    if layer in (O_, F0):
                        mm = by_tokens(ps_y[j % 2][:], "o" if layer == O_ else "0", c, j, slice(0, H))
                    if layer == L1:
                        t = slice(j * P, (j + 1) * P)
                        if j == 0:
                            pe.wait_ge(wt_set, TERMS)
                        for m in range(TERMS):
                            nc.tensor.matmul(ps_y[j % 2][:], terms[:, m, t], wt[:, m, :], start=(m == 0), stop=False)
                        if j == 0:
                            pe.wait_ge(h_set, 2 + FB * (q + 1))
                            pe.wait_ge(w_split["d"], len(d_pieces))
                        for f in range(FB):
                            rows = P if f < FB - 1 else F_LAST
                            for m, (a, w) in enumerate(((h_hi, hi["d"]), (h_hi, lo["d"]), (h_lo, hi["d"]))):
                                mm = nc.tensor.matmul(ps_y[j % 2][:], a[0:rows, f, t], w[0:rows, f, :], start=False,
                                                      stop=(f == FB - 1 and m == 2))
                    mm.then_inc(y_done, 1)

            def logits(s, c):
                pe.wait_ge(t_free, 2 + TPC * (s + 1))
                for j in range(TPC):
                    mm = by_tokens(ps_p[0][:, j * RA:(j + 1) * RA], "ra", c, j, slice(0, RA))
                mm.then_inc(r_done, 1)

            for j in range(TPC):
                transposes(0, j)
            pe.wait_ge(absd, 1)
            pe.wait_ge(mem, 7)
            for k in range(KC):
                mm = nc.tensor.matmul(ps_y[0][:], ones[:], t_a[:, k * H:(k + 1) * H], start=(k == 0), stop=(k == KC - 1))
            mm.then_inc(colsum, 1)

            def before(layer):
                if layer == O_:
                    pe.wait_ge(tern, 1)
                if layer == F0:
                    pe.wait_ge(w_split["0"], 1)
                if layer == L1:
                    for k in ("gu", "ra"):
                        pe.wait_ge(w_split[k], 1)
                    for k in wide:
                        pe.wait_ge(w_split[k], KC)
                if layer == L3:
                    pe.wait_ge(wt_in, 32)
                    logits(CHUNKS * L3, 0)

            layer_loops(pe, stage, before=before)




def sandwich_kernel(nc, t, out):
    context = nc.dram_tensor("context", [TOKENS, H], F32, kind="Internal").ap()
    with ExitStack() as ctx:
        wo_hi = ctx.enter_context(nc.sbuf_tensor("wo_hi", [P, KC, H], F16))
        wo_lo = ctx.enter_context(nc.sbuf_tensor("wo_lo", [P, KC, H], F16))
        wo_scale = ctx.enter_context(nc.sbuf_tensor("wo_scale", [P, 2], F32))
        first = ctx.enter_context(nc.sbuf_tensor("first", [P, TPC, H], F32))
        ident = ctx.enter_context(nc.sbuf_tensor("ident", [P, P], F32))
        attention_block(nc, t["x"], t["w_qkv"], t["b_qk"], t["b_v"], t["ident"], ident, context, t["w_o"],
                        wo_hi, wo_lo, wo_scale, first)
        layers_block(nc, t["x"], context, wo_hi, wo_lo, wo_scale, first, t["b_o"], t["w_0"], t["b_0"], t["w_gu"],
                     t["point"], t["w_terms"], t["discount"], t["w_g"], t["w_u"], t["w_d"], t["w_ra"], t["w_b"], ident, out)


_OUTS = [((BATCH, SEQ, H), "float32")]


def kernel(**inputs):
    import numpy as _np
    import concourse.bacc as _bacc
    from concourse import mybir as _mybir
    from concourse.bass_utils import run_bass_kernel_spmd as _run

    nc = _bacc.Bacc("TRN2", target_bir_lowering=False, num_devices=1)
    nc.disable_value_cache = True
    a = {k: _np.asarray(v) for k, v in inputs.items()}
    two_h = 2 * H
    bias = a["L0_attn_attn_qkvb"]
    laid = {
        "x": a["L0_attn_x"].reshape(TOKENS, H),
        "w_qkv": a["L0_attn_attn_qkvw"],
        "b_qk": bias[:two_h].reshape(2 * KC, P).T,
        "b_v": bias[two_h:].reshape(1, H),
        "ident": _np.eye(P, dtype=_np.float32),
        "w_o": a["L0_attn_attn_ow"],
        "b_o": a["L0_attn_attn_ob"].reshape(1, H),
        "w_0": a["L0_ffn_weight"].T,
        "b_0": a["L0_ffn_bias"].reshape(1, H),
        "w_gu": _np.concatenate([a["L1_attn_gate_w"], a["L1_attn_up_w"]], 0).T,
        "point": a["L1_attn_local_point"].reshape(-1, 1),
        "w_terms": _np.concatenate([a["L1_attn_local_approx_output"][:, :, None], a["L1_attn_fuse_weight"]], 2).transpose(1, 2, 0),
        "discount": a["L1_attn_discount_factor"].reshape(1, -1),
        "w_g": a["L1_attn_ffn_gate_w"].T,
        "w_u": a["L1_attn_ffn_up_w"].T,
        "w_d": a["L1_attn_ffn_down_w"].T,
        "w_ra": _np.concatenate([a["L1_ffn_router_w"], a["L1_ffn_A"].reshape(-1, H)], 0).T,
        "w_b": a["L1_ffn_B"].transpose(0, 2, 1).reshape(-1, H),
    }
    arrays, t = {}, {}
    for name, value in laid.items():
        value = _np.ascontiguousarray(value)
        arrays[f"in_{name}_dram"] = value
        t[name] = nc.dram_tensor(f"in_{name}_dram", value.shape, _mybir.dt.from_np(value.dtype), kind="ExternalInput").ap()
    out = nc.dram_tensor("out_0_dram", (TOKENS, H), F32, kind="ExternalOutput").ap()
    sandwich_kernel(nc, t, out)
    r = _run(nc, [arrays], core_ids=[0])
    return r.results[0]["out_0_dram"].reshape(BATCH, SEQ, H)
```
